# Optimizing a Trainium2 kernel written in Bass

```python
import numpy as np
import jax
import jax.numpy as jnp

def _softmax(x, axis=-1):
    return jax.nn.softmax(x, axis=axis)

def _gelu(x):
    return jax.nn.gelu(x, approximate=True)

def _silu(x):
    return jax.nn.silu(x)

def _sigmoid(x):
    return jax.nn.sigmoid(x)

def _layernorm(x, axis=-1, eps=1e-05):
    m = jnp.mean(x, axis=axis, keepdims=True)
    v = jnp.var(x, axis=axis, keepdims=True)
    return (x - m) / jnp.sqrt(v + eps)

def _scatter_add(tgt, idx, src, axis=0):
    return tgt.at[idx].add(src)

def _segment_sum(src, seg, n):
    return jax.ops.segment_sum(src, seg, n)
kernel_name = 'mk_vit_tower_cls_d1_tok_img1024_r4_d1f42b'

def setup_inputs(seed: int=0):
    np.random.seed(seed)
    _w = jnp.asarray

    def _rec_inputs():
        import jax
        import jax.numpy as jnp
        _rk = jax.random.key(seed)
        x = -0.00016672 + 0.999947 * jax.random.normal(jax.random.fold_in(_rk, 1), (64, 3, 96, 96), jnp.float32)
        cls_tok = 0.02 * jax.random.normal(jax.random.fold_in(_rk, 5), (1, 1, 256), jnp.float32)
        return (x, cls_tok)
    x, cls_tok = _rec_inputs()

    def _L0_tok_setup():
        import jax, jax.numpy as jnp
        import numpy as np
        PATCH = 16
        EPS = 1e-05

        def _patchify(x, p):
            B, C, H, W = x.shape
            hp, wp = (H // p, W // p)
            x = x.reshape(B, C, hp, p, wp, p)
            x = x.transpose(0, 2, 4, 1, 3, 5)
            return x.reshape(B, hp * wp, C * p * p)
        key = jax.random.key(seed)
        ks = jax.random.split(key, 6)
        B, C, H = (64, 3, 96)
        E = 256
        P = PATCH
        N = (H // P) ** 2
        D = C * P * P
        x = jax.random.normal(ks[0], (B, C, H, H), dtype=jnp.float32)
        W = jax.random.normal(ks[1], (D, E), dtype=jnp.float32) * (1.0 / np.sqrt(D))
        b = jnp.zeros((E,), dtype=jnp.float32)
        cls_token = jax.random.normal(ks[2], (1, 1, E), dtype=jnp.float32) * 0.02
        pos_embedding = jax.random.normal(ks[3], (1, N + 1, E), dtype=jnp.float32) * 0.02
        gamma = jnp.ones((E,), dtype=jnp.float32)
        beta = jnp.zeros((E,), dtype=jnp.float32)
        return {'x': x, 'W': W, 'b': b, 'cls_token': cls_token, 'pos_embedding': pos_embedding, 'gamma': gamma, 'beta': beta}
    _L0_tok_all = _L0_tok_setup()
    _L0_tok_in = {k: v for k, v in _L0_tok_all.items() if k in ('W', 'b', 'cls_token', 'pos_embedding', 'gamma', 'beta')}
    del _L0_tok_all

    def _L0_attn_setup():
        import jax, jax.numpy as jnp
        import numpy as np
        import math
        from jax import lax
        EPS = 1e-06

        def _layernorm(x, scale, bias):
            mu = jnp.mean(x, axis=-1, keepdims=True)
            var = jnp.var(x, axis=-1, keepdims=True)
            return (x - mu) * lax.rsqrt(var + EPS) * scale + bias

        def _rmsnorm(x, scale):
            ms = jnp.mean(x * x, axis=-1, keepdims=True)
            return x * lax.rsqrt(ms + EPS) * scale

        def _apply_rope(x, phi):
            half = x.shape[-1] // 2
            x_r, x_i = (x[..., :half], x[..., half:])
            c, s = (jnp.cos(phi), jnp.sin(phi))
            return jnp.concatenate([x_r * c - x_i * s, x_r * s + x_i * c], axis=-1)

        def _ssd_trapezoidal_scan(x_heads, B_ssm, C_ssm, dt, A, lam):
            a = jnp.exp(A[None, None, :] * dt)
            Bb, L, H, P = x_heads.shape
            N = B_ssm.shape[-1]
            xs = (jnp.moveaxis(x_heads, 1, 0), jnp.moveaxis(B_ssm, 1, 0), jnp.moveaxis(C_ssm, 1, 0), jnp.moveaxis(a, 1, 0), jnp.moveaxis(dt, 1, 0), jnp.moveaxis(lam, 1, 0))
            h0 = jnp.zeros((Bb, H, P, N), x_heads.dtype)

            def step(carry, inp):
                h, prev_Bx = carry
                x_t, B_t, C_t, a_t, dt_t, lam_t = inp
                Bx = jnp.einsum('bhp,bn->bhpn', x_t, B_t)
                ae = a_t[:, :, None, None]
                dte = dt_t[:, :, None, None]
                le = lam_t[:, :, None, None]
                h = ae * h + dte * (le * Bx + (1.0 - le) * ae * prev_Bx)
                y = jnp.einsum('bhpn,bn->bhp', h, C_t)
                return ((h, Bx), y)
            _, ys = lax.scan(step, (h0, jnp.zeros_like(h0)), xs)
            return jnp.moveaxis(ys, 0, 1)
        D_MODEL, D_STATE, N_HEADS, EXPAND = (256, 64, 16, 2)
        D_INNER = D_MODEL * EXPAND
        HEAD_DIM = D_INNER // N_HEADS
        PROJ = D_INNER + D_INNER + D_STATE + D_STATE + N_HEADS + N_HEADS
        key = jax.random.key(seed)
        ks = jax.random.split(key, 6)
        u = jax.random.normal(ks[0], (4, 1024, D_MODEL), dtype=jnp.float32)
        in_proj_w = jax.random.normal(ks[1], (D_MODEL, PROJ), dtype=jnp.float32) * D_MODEL ** (-0.5)
        A_log = jnp.log(jnp.arange(1, N_HEADS + 1, dtype=jnp.float32))
        uu = jax.random.uniform(ks[2], (N_HEADS,), dtype=jnp.float32, minval=math.log(0.001), maxval=math.log(0.1))
        dt_vals = jnp.clip(jnp.exp(uu), 0.0001)
        dt_bias = dt_vals + jnp.log(-jnp.expm1(-dt_vals))
        theta_w = jax.random.normal(ks[3], (D_MODEL, D_STATE // 2), dtype=jnp.float32) * 0.01
        out_proj_w = jax.random.normal(ks[4], (D_INNER, D_MODEL), dtype=jnp.float32) * D_INNER ** (-0.5)
        return {'u': u, 'norm_scale': jnp.ones((D_MODEL,), jnp.float32), 'norm_bias': jnp.zeros((D_MODEL,), jnp.float32), 'in_proj_w': in_proj_w, 'A_log': A_log, 'dt_bias': dt_bias, 'bcB_scale': jnp.ones((D_STATE,), jnp.float32), 'bcC_scale': jnp.ones((D_STATE,), jnp.float32), 'B_bias': jnp.zeros((D_STATE,), jnp.float32), 'C_bias': jnp.zeros((D_STATE,), jnp.float32), 'theta_w': theta_w, 'D': jnp.ones((N_HEADS,), jnp.float32), 'out_proj_w': out_proj_w}
    _L0_attn_all = _L0_attn_setup()
    _L0_attn_in = {k: v for k, v in _L0_attn_all.items() if k in ('norm_scale', 'norm_bias', 'in_proj_w', 'A_log', 'dt_bias', 'bcB_scale', 'bcC_scale', 'B_bias', 'C_bias', 'theta_w', 'D', 'out_proj_w')}
    del _L0_attn_all

    def _L0_ffn_setup():
        import jax, jax.numpy as jnp
        import numpy as np
        TOP_K = 2
        key = jax.random.key(seed)
        k1, k2, k3, k4 = jax.random.split(key, 4)
        B, S, H, I, E = (2, 512, 256, 1024, 8)
        return {'hidden_states': jax.random.normal(k1, (B, S, H), jnp.float32), 'gate_w': jax.random.normal(k2, (E, H), jnp.float32) * 0.02, 'gate_up_proj': jax.random.normal(k3, (E, 2 * I, H), jnp.float32) * 0.02, 'down_proj': jax.random.normal(k4, (E, H, I), jnp.float32) * 0.02}
    _L0_ffn_all = _L0_ffn_setup()
    _L0_ffn_in = {k: v for k, v in _L0_ffn_all.items() if k in ('gate_w', 'gate_up_proj', 'down_proj')}
    del _L0_ffn_all
    return {'x': x, 'cls_tok': cls_tok, 'L0_tok_W': _L0_tok_in['W'], 'L0_tok_b': _L0_tok_in['b'], 'L0_tok_cls_token': _L0_tok_in['cls_token'], 'L0_tok_pos_embedding': _L0_tok_in['pos_embedding'], 'L0_tok_gamma': _L0_tok_in['gamma'], 'L0_tok_beta': _L0_tok_in['beta'], 'L0_attn_norm_scale': _L0_attn_in['norm_scale'], 'L0_attn_norm_bias': _L0_attn_in['norm_bias'], 'L0_attn_in_proj_w': _L0_attn_in['in_proj_w'], 'L0_attn_A_log': _L0_attn_in['A_log'], 'L0_attn_dt_bias': _L0_attn_in['dt_bias'], 'L0_attn_bcB_scale': _L0_attn_in['bcB_scale'], 'L0_attn_bcC_scale': _L0_attn_in['bcC_scale'], 'L0_attn_B_bias': _L0_attn_in['B_bias'], 'L0_attn_C_bias': _L0_attn_in['C_bias'], 'L0_attn_theta_w': _L0_attn_in['theta_w'], 'L0_attn_D': _L0_attn_in['D'], 'L0_attn_out_proj_w': _L0_attn_in['out_proj_w'], 'L0_ffn_gate_w': _L0_ffn_in['gate_w'], 'L0_ffn_gate_up_proj': _L0_ffn_in['gate_up_proj'], 'L0_ffn_down_proj': _L0_ffn_in['down_proj']}

def reference(x, cls_tok, L0_tok_W, L0_tok_b, L0_tok_cls_token, L0_tok_pos_embedding, L0_tok_gamma, L0_tok_beta, L0_attn_norm_scale, L0_attn_norm_bias, L0_attn_in_proj_w, L0_attn_A_log, L0_attn_dt_bias, L0_attn_bcB_scale, L0_attn_bcC_scale, L0_attn_B_bias, L0_attn_C_bias, L0_attn_theta_w, L0_attn_D, L0_attn_out_proj_w, L0_ffn_gate_w, L0_ffn_gate_up_proj, L0_ffn_down_proj):
    import jax
    import jax.numpy as jnp

    def _L0_tok_ref(x, W, b, cls_token, pos_embedding, gamma, beta):
        import jax, jax.numpy as jnp
        import numpy as np
        PATCH = 16
        EPS = 1e-05

        def _patchify(x, p):
            B, C, H, W = x.shape
            hp, wp = (H // p, W // p)
            x = x.reshape(B, C, hp, p, wp, p)
            x = x.transpose(0, 2, 4, 1, 3, 5)
            return x.reshape(B, hp * wp, C * p * p)
        B = x.shape[0]
        patches = _patchify(x, PATCH)
        tok = jnp.einsum('bnd,de->bne', patches, W) + b
        cls = jnp.broadcast_to(cls_token, (B, 1, tok.shape[-1]))
        h = jnp.concatenate([cls, tok], axis=1) + pos_embedding
        mu = jnp.mean(h, axis=-1, keepdims=True)
        var = jnp.mean(jnp.square(h - mu), axis=-1, keepdims=True)
        out = (h - mu) * jax.lax.rsqrt(var + EPS) * gamma + beta
        return out

    def _L0_attn_ref(u, norm_scale, norm_bias, in_proj_w, A_log, dt_bias, bcB_scale, bcC_scale, B_bias, C_bias, theta_w, D, out_proj_w):
        import jax, jax.numpy as jnp
        import numpy as np
        import math
        from jax import lax
        EPS = 1e-06

        def _layernorm(x, scale, bias):
            mu = jnp.mean(x, axis=-1, keepdims=True)
            var = jnp.var(x, axis=-1, keepdims=True)
            return (x - mu) * lax.rsqrt(var + EPS) * scale + bias

        def _rmsnorm(x, scale):
            ms = jnp.mean(x * x, axis=-1, keepdims=True)
            return x * lax.rsqrt(ms + EPS) * scale

        def _apply_rope(x, phi):
            half = x.shape[-1] // 2
            x_r, x_i = (x[..., :half], x[..., half:])
            c, s = (jnp.cos(phi), jnp.sin(phi))
            return jnp.concatenate([x_r * c - x_i * s, x_r * s + x_i * c], axis=-1)

        def _ssd_trapezoidal_scan(x_heads, B_ssm, C_ssm, dt, A, lam):
            a = jnp.exp(A[None, None, :] * dt)
            Bb, L, H, P = x_heads.shape
            N = B_ssm.shape[-1]
            xs = (jnp.moveaxis(x_heads, 1, 0), jnp.moveaxis(B_ssm, 1, 0), jnp.moveaxis(C_ssm, 1, 0), jnp.moveaxis(a, 1, 0), jnp.moveaxis(dt, 1, 0), jnp.moveaxis(lam, 1, 0))
            h0 = jnp.zeros((Bb, H, P, N), x_heads.dtype)

            def step(carry, inp):
                h, prev_Bx = carry
                x_t, B_t, C_t, a_t, dt_t, lam_t = inp
                Bx = jnp.einsum('bhp,bn->bhpn', x_t, B_t)
                ae = a_t[:, :, None, None]
                dte = dt_t[:, :, None, None]
                le = lam_t[:, :, None, None]
                h = ae * h + dte * (le * Bx + (1.0 - le) * ae * prev_Bx)
                y = jnp.einsum('bhpn,bn->bhp', h, C_t)
                return ((h, Bx), y)
            _, ys = lax.scan(step, (h0, jnp.zeros_like(h0)), xs)
            return jnp.moveaxis(ys, 0, 1)
        D_MODEL, D_STATE, N_HEADS, EXPAND = (256, 64, 16, 2)
        D_INNER = D_MODEL * EXPAND
        HEAD_DIM = D_INNER // N_HEADS
        PROJ = D_INNER + D_INNER + D_STATE + D_STATE + N_HEADS + N_HEADS
        residual = u
        x_in = _layernorm(u, norm_scale, norm_bias)
        proj = x_in @ in_proj_w
        i = 0
        x = proj[..., i:i + D_INNER]
        i += D_INNER
        z = proj[..., i:i + D_INNER]
        i += D_INNER
        B_raw = proj[..., i:i + D_STATE]
        i += D_STATE
        C_raw = proj[..., i:i + D_STATE]
        i += D_STATE
        dt_raw = proj[..., i:i + N_HEADS]
        i += N_HEADS
        lam_raw = proj[..., i:i + N_HEADS]
        A = -jnp.exp(A_log)
        dt = jax.nn.softplus(dt_raw + dt_bias)
        lam = jax.nn.sigmoid(lam_raw)
        B_ssm = _rmsnorm(B_raw, bcB_scale) + B_bias
        C_ssm = _rmsnorm(C_raw, bcC_scale) + C_bias
        theta = u @ theta_w
        dt_scalar = jnp.mean(dt, axis=-1, keepdims=True)
        phi = jnp.cumsum(dt_scalar.astype(jnp.float32) * theta.astype(jnp.float32), axis=1).astype(B_ssm.dtype)
        B_ssm = _apply_rope(B_ssm, phi)
        C_ssm = _apply_rope(C_ssm, phi)
        x = jax.nn.silu(x)
        x_heads = x.reshape(*x.shape[:-1], N_HEADS, HEAD_DIM)
        y_heads = _ssd_trapezoidal_scan(x_heads, B_ssm, C_ssm, dt, A, lam)
        y_heads = y_heads + x_heads * D[None, None, :, None]
        y = y_heads.reshape(*y_heads.shape[:-2], D_INNER) * jax.nn.silu(z)
        y = y @ out_proj_w
        return y + residual

    def _L0_ffn_ref(hidden_states, gate_w, gate_up_proj, down_proj):
        import jax, jax.numpy as jnp
        import numpy as np
        TOP_K = 2
        B, S, H = hidden_states.shape
        E = gate_w.shape[0]
        x = hidden_states.reshape(-1, H)
        T = x.shape[0]
        probs = jax.nn.softmax(x @ gate_w.T, axis=-1)
        w, idx = jax.lax.top_k(probs, TOP_K)
        w = w / jnp.sum(w, axis=-1, keepdims=True)
        combine = jnp.zeros((T, E), x.dtype).at[jnp.arange(T)[:, None], idx].add(w)

        def step(acc, inputs):
            gup, dn, ce = inputs
            g, u = jnp.split(x @ gup.T, 2, axis=-1)
            acc = acc + ce[:, None] * (jax.nn.silu(g) * u @ dn.T)
            return (acc, None)
        out, _ = jax.lax.scan(step, jnp.zeros_like(x), (gate_up_proj, down_proj, combine.T))
        return out.reshape(B, S, H)
    h = _L0_tok_ref(x, L0_tok_W, L0_tok_b, L0_tok_cls_token, L0_tok_pos_embedding, L0_tok_gamma, L0_tok_beta)
    h = jnp.concatenate([jnp.broadcast_to(cls_tok, (h.shape[0], 1, h.shape[2])), h], axis=1)
    h = h + _L0_attn_ref(_layernorm(h, axis=-1), L0_attn_norm_scale, L0_attn_norm_bias, L0_attn_in_proj_w, L0_attn_A_log, L0_attn_dt_bias, L0_attn_bcB_scale, L0_attn_bcC_scale, L0_attn_B_bias, L0_attn_C_bias, L0_attn_theta_w, L0_attn_D, L0_attn_out_proj_w)
    h = h + _L0_ffn_ref(_layernorm(h, axis=-1), L0_ffn_gate_w, L0_ffn_gate_up_proj, L0_ffn_down_proj)
    return h

_drawn_inputs = setup_inputs


def setup_inputs(seed=0):
    import zlib

    import numpy as np

    out = dict(_drawn_inputs(seed))
    spreads = {'L0_tok_b': (0.0, 0.1),
     'L0_tok_gamma': (1.0, 0.2),
     'L0_tok_beta': (0.0, 0.1),
     'L0_attn_norm_scale': (1.0, 0.2),
     'L0_attn_norm_bias': (0.0, 0.1),
     'L0_attn_bcB_scale': (1.0, 0.2),
     'L0_attn_bcC_scale': (1.0, 0.2),
     'L0_attn_B_bias': (0.0, 0.33),
     'L0_attn_C_bias': (0.0, 0.438),
     'L0_attn_D': (1.0, 0.2)}
    factors = {'L0_attn_theta_w': 8.0,
     'L0_ffn_gate_w': 5.792,
     'L0_ffn_gate_up_proj': 4.936,
     'L0_ffn_down_proj': 4.953}
    for name, (base, spread) in spreads.items():
        noise = np.random.default_rng([zlib.crc32(name.encode()), seed]).standard_normal(out[name].shape)
        drawn = base * np.exp(spread * noise) if base else spread * noise
        out[name] = jnp.asarray(drawn.astype(out[name].dtype))
    for name, factor in factors.items():
        out[name] = (out[name] * factor).astype(out[name].dtype)
    return out
```

```python
import concourse.bass as bass
from concourse import mybir
from concourse.alu_op_type import AluOpType as ALU
from contextlib import ExitStack
import numpy as np

BATCH, CH, IMG, PATCH = 64, 3, 96, 16
E = 256
HP = IMG // PATCH
NP = HP * HP
D = CH * PATCH * PATCH
L = NP + 2
G3 = 3
R = G3 * L
NT = -(-BATCH // G3)
LAST = (BATCH - G3 * (NT - 1)) * L
TOK = BATCH * L
INNER, STATE, HEADS = 512, 64, 16
HD = INNER // HEADS
HALF = STATE // 2
SMALL = 2 * STATE + 2 * HEADS + HALF
PROJ = 2 * INNER + 2 * STATE + 2 * HEADS
DC, KC, YC = D // 128, E // 128, INNER // 128
NE, FF = 8, 1024
FC = FF // 128
HFF = FF // 2
ST = TOK * 2 // 128 + NE - 1
RECW = 272
ID, CW = E, E + 1
ACC = TOK + 128
WEXP = KC * 2 * FF + FC * E
SLOTS = 4
OFF_GU, OFF_DN = 0, KC * 2 * FF

f32, i32 = mybir.dt.float32, mybir.dt.int32
ACT = mybir.ActivationFunctionType
AX = mybir.AxisListType
TWO_PI = 2.0 * np.pi
MAGIC = 1.5 * 2.0 ** 23
PI_HI = float(np.float32(6.28125))
PI_MD = float(np.float32(TWO_PI - 6.28125))
PI_LO = float(TWO_PI - 6.28125 - np.float32(TWO_PI - 6.28125))
PI_IN = 3.1415925

CONST = {}


def constants():
    k = np.arange(128)
    kk, ss = np.meshgrid(k, k, indexing="ij")
    same = (kk // L == ss // L) & (kk < R) & (ss < R)
    parts = [
        ("ident", np.eye(128)),
        ("causal", same & (kk < ss)),
        ("upto", same & (kk <= ss)),
        ("after", same & (kk > ss)),
        ("shift", same & (kk == ss + 1)),
        ("before", kk < ss),
        ("ones", np.ones((128, 128))),
        ("step", (k[:, None] % L) <= np.arange(L)[None, :]),
        ("lower", np.broadcast_to((np.arange(NE)[None, :] < np.arange(NE)[:, None]).reshape(1, -1), (128, NE * NE))),
        ("normed", (k % L != 0)[:, None]),
        ("raw", (k % L == 0)[:, None]),
        ("valid", (np.arange(NT)[None, :] * R + k[:, None] < TOK)),
        ("rowid", np.arange(NT)[None, :] * R + k[:, None]),
        ("spare", np.stack([ST * 128 + k, (ST + 1) * 128 + k], 1)),
        ("spareid", (TOK + k)[:, None]),
        ("carry", np.broadcast_to((np.arange(NT) != 0)[None, None, :], (128, NE, NT)).reshape(128, -1)),
        ("carry8", np.broadcast_to((np.arange(NE) != 0)[None, :], (128, NE))),
        ("by128", np.broadcast_to(np.arange(TOK // 128)[None, :] * 128.0, (128, TOK // 128))),
        ("tiles", np.broadcast_to(np.arange(ST)[None, :], (128, ST))),
        ("experts", np.broadcast_to(np.arange(NE)[None, :], (128, NE))),
        ("neghalf", np.full((128, 1), -0.5)),
        ("eps5", np.full((128, 1), 1e-5)),
        ("eps6", np.full((128, 2), 1e-6)),
        ("halfpi", np.full((128, 1), np.pi / 2)),
    ]
    at = 0
    for name, a in parts:
        CONST[name] = (at, at + a.shape[1])
        at += a.shape[1]
    return np.concatenate([np.asarray(a, np.float32) for _, a in parts], 1)


CONSTS = constants()


def program(nc, patches, base_a, base_b, gammas, betas, w_tok, w_in, w_theta, norm_cols, head_rows,
            bc_rows, w_out, w_gate, w_experts, consts, out):
    rec = nc.dram_tensor("records", ((ST + 2) * 128, RECW), f32, kind="Internal").ap()
    acc = nc.dram_tensor("accumulator", (ACC, E), f32, kind="Internal").ap()
    with ExitStack() as top:
        def sb(ctx, name, shape, dt=f32):
            return ctx.enter_context(nc.sbuf_tensor(name, shape, dt))

        def sems(names):
            return {n: top.enter_context(nc.semaphore(n)) for n in names.split()}

        ps = top.enter_context(nc.psum_tensor("ps", [128, 8, 512], f32))
        cst = sb(top, "cst", [128, CONSTS.shape[1]])
        recs = sb(top, "recs", [128, NT, RECW])
        posi = sb(top, "posi", [128, NT, 2], i32)
        tab = sb(top, "tab", [128, 2, ST], i32)
        upto_e = sb(top, "upto_e", [128, NE], i32)
        onehot = sb(top, "onehot", [128, ST, NE])

        def c(name, rows=R):
            a, b = CONST[name]
            return cst[0:rows, a:b]

        with ExitStack() as mid:
            keep = dict(
                xz=sb(mid, "xz", [128, NT, 2 * INNER]), hu=sb(mid, "hu", [128, NT, E]),
                rot=sb(mid, "rot", [128, NT, 2, STATE]), loga=sb(mid, "loga", [128, NT, HEADS]),
                coef=sb(mid, "coef", [128, NT, HEADS]), diag=sb(mid, "diag", [128, NT, HEADS]))
            small = recs[:, :, :].rearrange("p a b -> p (a b)")[:, 0:NT * SMALL].rearrange("p (t s) -> p t s", s=SMALL)
            with ExitStack() as ctx:
                embed_and_project(nc, ctx, sb, sems, ps, cst, c, keep, small, rec, acc, patches, base_a, base_b,
                                  gammas, betas, w_tok, w_in, w_theta, norm_cols, bc_rows, consts)
            with ExitStack() as ctx:
                scan_coefficients(nc, ctx, sb, sems, ps, c, keep, small, head_rows)
            with ExitStack() as ctx:
                logits = sb(ctx, "logits", [128, NT, NE])
                with ExitStack() as inner:
                    mix_tokens(nc, inner, sb, sems, ps, c, keep, recs, logits, acc, w_out, w_gate)
                route(nc, ctx, sb, sems, ps, c, recs, logits, posi, tab, upto_e, onehot, rec)
        with ExitStack() as ctx:
            experts(nc, ctx, sb, sems, ps, c, tab, upto_e, onehot, rec, acc, w_experts, out)


def lag(eng, sem, i, n):
    if not isinstance(i, int) or i >= n:
        eng.wait_ge(sem, i - n + 1)


def settle(eng, sem):
    eng.sem_inc(sem, 1)


def row(t, i, rows=R):
    return t[0:rows, bass.ds(i, 1), :].rearrange("p o n -> p (o n)")


def pairs(eng, step, first, last):
    assert (last - first) % 2 == 0 and first % 2 == 0
    with eng.Fori(first // 2, last // 2) as j:
        step(2 * j, 0)
        step(2 * j + 1, 1)


def embed_and_project(nc, ctx, sb, sems, ps, cst, c, keep, small, rec, acc, patches, base_a, base_b, gammas,
                      betas, w_tok, w_in, w_theta, norm_cols, bc_rows, consts):
    pin = sb(ctx, "pin", [128, 2, DC * R])
    wt = sb(ctx, "wt", [128, DC, E])
    wi = sb(ctx, "wi", [128, KC, PROJ])
    wth = sb(ctx, "wth", [128, KC, HALF])
    base = sb(ctx, "base", [128, E])
    gam = sb(ctx, "gam", [128, E])
    bet = sb(ctx, "bet", [128, E])
    ncol = sb(ctx, "ncol", [128, 2, KC])
    bcr = sb(ctx, "bcr", [128, 4, STATE])
    pre = sb(ctx, "pre", [128, E])
    hid = sb(ctx, "hid", [128, 2, E])
    ux = sb(ctx, "ux", [128, 2, 2, E])
    xt = sb(ctx, "xt", [128, 2, 4, R])
    bcw = sb(ctx, "bcw", [128, 2, STATE])
    junk = sb(ctx, "junk", [128, 2, STATE])
    st = sb(ctx, "st", [128, 6])
    mv1 = sb(ctx, "mv1", [128, 2, 2])
    mv2 = sb(ctx, "mv2", [128, 2, 2])
    rs1 = sb(ctx, "rs1", [128, 2])
    rs2 = sb(ctx, "rs2", [128, 2, 2])
    tmp = sb(ctx, "tmp", [128, 1])
    ms = sb(ctx, "ms", [128, 2])
    empty = sb(ctx, "empty", [128, RECW])
    s = sems("passed_a wload base_ok patch0 patch1 embedded pre_ok st1 mv1_ok p1 rs1_ok m1 n1 n2 hid_ok st2 mv2_ok "
             "p2 rs2_ok ux_ok xt_ps xt_ok proj_ok silu_ok small_ok bcw_ok ms_ok p3 rms_ok bn0 bn_ok hu_ok "
             "empty0 empty_ok empty_out")
    patch = [s["patch0"], s["patch1"]]
    tok = [ps[0:R, b, 0:E] for b in range(2)]
    tps = [ps[:, 2 + b, 0:4 * R].rearrange("p (a r) -> p a r", a=4) for b in range(2)]
    XP, ZP, SP_ = ps[0:R, 4, :], ps[0:R, 5, :], ps[0:R, 6, 0:SMALL]
    NCONST = 11

    with nc.Block() as block:
        @block.sync
        def _(sp):
            sp.dma_start(pin[:, 0, :], patches[0]).then_inc(patch[0], 16)
            sp.dma_start(wt[:], w_tok).then_inc(s["wload"], 16)
            for dst, src in ((base[0:R, :], base_a), (pre[0:R, :], base_b), (cst[:], consts), (gam[0:R, :], gammas),
                             (bet[0:R, :], betas), (ncol[:], norm_cols), (wi[:], w_in), (wth[:], w_theta),
                             (bcr[0:R], bc_rows)):
                sp.dma_start(dst, src).then_inc(s["wload"], 16)
            sp.dma_start(pin[:, 1, :], patches[1]).then_inc(patch[1], 16)

            def step(i, b):
                sp.wait_ge(s["embedded"], i - 1)
                sp.dma_start(pin[:, b, :], patches[bass.ds(i, 1)].rearrange("o p n -> p (o n)")).then_inc(patch[b], 16)
            pairs(sp, step, 2, NT)
            sp.wait_ge(s["empty_ok"], 1)
            sp.dma_start(rec.rearrange("(t p) w -> p t w", p=128),
                         empty[:, None, :].to_broadcast([128, ST + 2, RECW])).then_inc(s["empty_out"], 16)
            sp.dma_start(acc[TOK:ACC, :], empty[:, 0:E]).then_inc(s["empty_out"], 16)
            sp.wait_ge(s["empty_out"], 32)

        @block.tensor
        def _(pe):
            ident = c("ident", 128)[0:R, 0:R]

            def embed(i, b):
                pe.wait_ge(patch[b], 8 * (i + 2 - b))
                lag(pe, s["pre_ok"], i, 2)
                for k in range(DC):
                    last = nc.tensor.matmul(tok[b], pin[:, b, k * R:(k + 1) * R], wt[:, k, :],
                                            start=(k == 0), stop=(k == DC - 1))
                last.then_inc(s["embedded"], 1)

            def step(i, b, more=True):
                pe.wait_ge(s["ux_ok"], i + 1)
                lag(pe, s["xt_ok"], i, 2)
                for a in range(4):
                    last = nc.tensor.transpose(tps[b][:, a, :], ux[0:R, b, a // 2, (a % 2) * 128:(a % 2) * 128 + 128], ident)
                last.then_inc(s["xt_ps"], 1)
                if more:
                    embed(i + 1, 1 - b)
                pe.wait_ge(s["xt_ok"], i + 1)
                lag(pe, s["silu_ok"], i, 1)
                lag(pe, s["small_ok"], i, 1)
                for k in range(KC):
                    x = xt[:, b, 2 + k, :]
                    first, end = k == 0, k == KC - 1
                    nc.tensor.matmul(XP, x, wi[:, k, 0:INNER], start=first, stop=end)
                    nc.tensor.matmul(ZP, x, wi[:, k, INNER:2 * INNER], start=first, stop=end)
                    nc.tensor.matmul(SP_[:, 0:SMALL - HALF], x, wi[:, k, 2 * INNER:], start=first, stop=end)
                for k in range(KC):
                    last = nc.tensor.matmul(SP_[:, SMALL - HALF:], xt[:, b, k, :], wth[:, k, :], start=(k == 0),
                                            stop=(k == KC - 1))
                last.then_inc(s["proj_ok"], 1)

            pe.wait_ge(s["wload"], 16 * 10)
            embed(0, 0)
            step(0, 0)
            step(1, 1)
            pairs(pe, step, 2, NT - 2)
            step(NT - 2, 0)
            step(NT - 1, 1, more=False)

        @block.vector
        def _(dve):
            v = nc.vector
            v.memset(empty[:], 0.0).then_inc(s["empty0"], 1)
            dve.wait_ge(s["wload"], 16 * 10)
            dve.wait_ge(s["empty0"], 1)
            v.tensor_copy(empty[:, ID:ID + 1], c("spareid", 128)).then_inc(s["empty_ok"], 1)
            v.tensor_tensor(base[0:R, :], base[0:R, :], pre[0:R, :], ALU.add).then_inc(s["base_ok"], 1)
            dve.wait_ge(s["base_ok"], 1)

            def norms(i, b):
                h, u, xh = hid[0:R, b, :], ux[0:R, b, 0, :], ux[0:R, b, 1, :]
                m1, m2 = mv1[0:R, b, :], mv2[0:R, b, :]
                dve.wait_ge(s["embedded"], i + 1)
                v.tensor_tensor(pre[0:R, :], tok[b], base[0:R, :], ALU.add).then_inc(s["pre_ok"], 1)
                dve.wait_ge(s["pre_ok"], i + 1)
                v.bn_stats(st[0:R, :], pre[0:R, :]).then_inc(s["st1"], 1)
                dve.wait_ge(s["st1"], i + 1)
                settle(dve, s["passed_a"])
                v.bn_aggr(m1, st[0:R, :]).then_inc(s["mv1_ok"], 1)
                dve.wait_ge(s["mv1_ok"], i + 1)
                v.tensor_tensor(m1[:, 0:1], m1[:, 0:1], c("normed"), ALU.mult)
                dve.wait_ge(s["rs1_ok"], i + 1)
                v.tensor_scalar(rs1[0:R, b:b + 1], rs1[0:R, b:b + 1], c("normed"), c("raw"), ALU.mult, ALU.add).then_inc(s["m1"], 1)
                dve.wait_ge(s["m1"], i + 1)
                lag(dve, s["hu_ok"], i, 2)
                v.tensor_scalar(h, pre[0:R, :], m1[:, 0:1], rs1[0:R, b:b + 1], ALU.subtract, ALU.mult).then_inc(s["n1"], 1)
                dve.wait_ge(s["n1"], i + 1)
                v.tensor_tensor(h, h, gam[0:R, :], ALU.mult).then_inc(s["n2"], 1)
                dve.wait_ge(s["n2"], i + 1)
                v.tensor_tensor(h, h, bet[0:R, :], ALU.add).then_inc(s["hid_ok"], 1)
                dve.wait_ge(s["hid_ok"], i + 1)
                v.bn_stats(st[0:R, :], h).then_inc(s["st2"], 1)
                dve.wait_ge(s["st2"], i + 1)
                settle(dve, s["passed_a"])
                v.bn_aggr(m2, st[0:R, :]).then_inc(s["mv2_ok"], 1)
                dve.wait_ge(s["rs2_ok"], i + 1)
                lag(dve, s["xt_ps"], i, 2)
                v.tensor_scalar(u, h, m2[:, 0:1], rs2[0:R, b, 0:1], ALU.subtract, ALU.mult)
                v.tensor_scalar(xh, h, m2[:, 0:1], rs2[0:R, b, 1:2], ALU.subtract, ALU.mult).then_inc(s["ux_ok"], 1)

            def smalls(i, b):
                dve.wait_ge(s["proj_ok"], i + 1)
                lag(dve, s["bn_ok"], i, 1)
                v.tensor_copy(bcw[0:R].rearrange("p a n -> p (a n)"), SP_[:, 0:2 * STATE]).then_inc(s["bcw_ok"], 1)
                v.tensor_copy(row(small, i)[:, 2 * STATE:], SP_[:, 2 * STATE:]).then_inc(s["small_ok"], 1)
                dve.wait_ge(s["bcw_ok"], i + 1)
                for a in range(2):
                    last = v.tensor_tensor_reduce(out=junk[0:R, a, :], in0=bcw[0:R, a, :], in1=bcw[0:R, a, :], scale=1.0 / STATE,
                                                  scalar=0.0, op0=ALU.mult, op1=ALU.add, accum_out=ms[0:R, a:a + 1])
                last.then_inc(s["ms_ok"], 1)
                dve.wait_ge(s["rms_ok"], i + 1)
                for a in range(2):
                    last = v.scalar_tensor_tensor(out=bcw[0:R, a, :], in0=bcw[0:R, a, :], scalar=ms[0:R, a:a + 1],
                                                  in1=bcr[0:R, a, :], op0=ALU.mult, op1=ALU.mult)
                last.then_inc(s["bn0"], 1)
                dve.wait_ge(s["bn0"], i + 1)
                v.tensor_tensor(row(small, i)[:, 0:2 * STATE], bcw[0:R].rearrange("p a n -> p (a n)"),
                                bcr[0:R, 2:4, :].rearrange("p a n -> p (a n)"), ALU.add).then_inc(s["bn_ok"], 1)

            def step(i, b, more=True):
                if more:
                    norms(i + 1, 1 - b)
                smalls(i, b)

            norms(0, 0)
            step(0, 0)
            step(1, 1)
            pairs(dve, step, 2, NT - 2)
            step(NT - 2, 0)
            step(NT - 1, 1, more=False)

        @block.gpsimd
        def _(pool):
            g = nc.gpsimd
            half, e5, e6 = c("neghalf"), c("eps5"), c("eps6")
            pool.wait_ge(s["wload"], 16 * 10)

            def norms(i, b):
                r1, r2, r23 = rs1[0:R, b:b + 1], rs2[0:R, b, 0:1], rs2[0:R, b, 1:2]
                var1, var2, t = mv1[0:R, b, 1:2], mv2[0:R, b, 1:2], tmp[0:R, :]
                pool.wait_ge(s["mv1_ok"], i + 1)
                g.tensor_tensor(t, var1, e5, ALU.add).then_inc(s["p1"], 1)
                pool.wait_ge(s["p1"], i + 1)
                g.tensor_tensor(r1, t, half, ALU.pow).then_inc(s["rs1_ok"], 1)
                pool.wait_ge(s["mv2_ok"], i + 1)
                g.tensor_tensor(t, var2, e5, ALU.add).then_inc(s["p2"], 1)
                pool.wait_ge(s["p2"], 6 * i + 1)
                g.tensor_tensor(r2, t, half, ALU.pow).then_inc(s["p2"], 1)
                pool.wait_ge(s["p2"], 6 * i + 2)
                g.tensor_tensor(t, var2, r2, ALU.mult).then_inc(s["p2"], 1)
                pool.wait_ge(s["p2"], 6 * i + 3)
                g.tensor_tensor(t, t, r2, ALU.mult).then_inc(s["p2"], 1)
                pool.wait_ge(s["p2"], 6 * i + 4)
                g.tensor_tensor(t, t, e6[:, 0:1], ALU.add).then_inc(s["p2"], 1)
                pool.wait_ge(s["p2"], 6 * i + 5)
                g.tensor_tensor(t, t, half, ALU.pow).then_inc(s["p2"], 1)
                pool.wait_ge(s["p2"], 6 * i + 6)
                g.tensor_tensor(r23, t, r2, ALU.mult).then_inc(s["rs2_ok"], 1)
                pool.wait_ge(s["ux_ok"], i + 1)
                g.tensor_tensor(row(keep["hu"], i), hid[0:R, b, :], ux[0:R, b, 0, :], ALU.add).then_inc(s["hu_ok"], 1)

            def smalls(i, b):
                pool.wait_ge(s["ms_ok"], i + 1)
                g.tensor_tensor(ms[0:R, :], ms[0:R, :], e6, ALU.add).then_inc(s["p3"], 1)
                pool.wait_ge(s["p3"], i + 1)
                g.tensor_tensor(ms[0:R, :], ms[0:R, :], half.to_broadcast([R, 2]), ALU.pow).then_inc(s["rms_ok"], 1)

            def step(i, b, more=True):
                if more:
                    norms(i + 1, 1 - b)
                smalls(i, b)

            norms(0, 0)
            step(0, 0)
            step(1, 1)
            pairs(pool, step, 2, NT - 2)
            step(NT - 2, 0)
            step(NT - 1, 1, more=False)

        @block.scalar
        def _(act):
            a = nc.scalar

            def step(i, b):
                act.wait_ge(s["xt_ps"], i + 1)
                lag(act, s["proj_ok"], i, 2)
                a.activation(xt[:, b, 0:2, :], tps[b][:, 0:2, :], ACT.Copy)
                for k in range(KC):
                    last = a.activation(xt[:, b, 2 + k, :], tps[b][:, 2 + k, :], ACT.Identity, scale=ncol[:, 0, k:k + 1],
                                        bias=ncol[:, 1, k:k + 1])
                last.then_inc(s["xt_ok"], 1)
                act.wait_ge(s["proj_ok"], i + 1)
                a.activation(row(keep["xz"], i)[:, 0:INNER], XP, ACT.Silu)
                a.activation(row(keep["xz"], i)[:, INNER:], ZP, ACT.Silu).then_inc(s["silu_ok"], 1)

            act.wait_ge(s["wload"], 16 * 10)
            step(0, 0)
            step(1, 1)
            pairs(act, step, 2, NT)


def scan_coefficients(nc, ctx, sb, sems, ps, c, keep, small, head_rows):
    NH = NT * HEADS
    NA = NT * 2 * HALF
    hr = sb(ctx, "hr", [128, 3, HEADS])
    ea = sb(ctx, "ea", [128, HEADS])
    dtv = sb(ctx, "dtv", [128, NT, HEADS])
    ab = sb(ctx, "ab", [128, NT, HEADS])
    el = sb(ctx, "el", [128, NT, HEADS])
    cn = sb(ctx, "cn", [128, NT, HEADS])
    cx = sb(ctx, "cx", [128, NT, HEADS])
    dm = sb(ctx, "dm", [128, NT])
    th = sb(ctx, "th", [128, NT, HALF])
    ang = sb(ctx, "ang", [128, NT, 2, HALF])
    kf = sb(ctx, "kf", [128, NT, 2, HALF])
    ra = sb(ctx, "ra", [128, NT, HALF])
    rb = sb(ctx, "rb", [128, NT, HALF])
    rc = sb(ctx, "rc", [128, NT, HALF])
    rd = sb(ctx, "rd", [128, NT, HALF])
    bc = sb(ctx, "bc", [128, NT, STATE])
    gtt = sb(ctx, "gtt", [128, NT])
    s = sems("hload dchain abs_in abs_ok soft_ok sig_ok ea_ok cx_ok theta_ok phi_ok shift_ok ang_ok sin_ok pchain rotc_ok")
    phi = [ps[0:R, q, 0:NT // 2 * HALF].rearrange("p (t n) -> p t n", n=HALF) for q in range(2)]
    sh = ps[0:R, 2, 0:NH].rearrange("p (t n) -> p t n", n=HEADS)
    HT = NT // 2

    def r(t):
        return t[0:R]

    def over_tiles(ap, n):
        return ap.rearrange("p (o n) -> p o n", o=1).to_broadcast([R, NT, n])

    with nc.Block() as block:
        @block.sync
        def _(sp):
            sp.dma_start(hr[0:R], head_rows).then_inc(s["hload"], 16)

        @block.scalar
        def _(act):
            a = nc.scalar
            act.wait_ge(s["hload"], 16)
            a.activation(r(ea), hr[0:R, 0, :], ACT.Exp).then_inc(s["ea_ok"], 1)
            a.activation(r(el), small[0:R, :, 2 * STATE + HEADS:2 * STATE + 2 * HEADS], ACT.Exp, scale=-1.0).then_inc(s["sig_ok"], 1)
            act.wait_ge(s["abs_in"], 1)
            a.activation(r(ab), r(dtv), ACT.Abs).then_inc(s["abs_ok"], 1)
            act.wait_ge(s["abs_ok"], 1)
            a.activation(r(ab), r(ab), ACT.Exp, scale=-1.0).then_inc(s["abs_ok"], 1)
            act.wait_ge(s["abs_ok"], 2)
            a.activation(r(ab), r(ab), ACT.Ln, bias=1.0).then_inc(s["soft_ok"], 1)
            act.wait_ge(s["ang_ok"], 1)
            a.activation(r(ang), r(ang), ACT.Sin).then_inc(s["sin_ok"], 1)

        @block.tensor
        def _(pe):
            pe.wait_ge(s["theta_ok"], 1)
            for q in range(2):
                last = nc.tensor.matmul(phi[q], c("upto")[:, 0:R], th[0:R, q * HT:(q + 1) * HT, :], start=True, stop=True)
            last.then_inc(s["phi_ok"], 1)
            pe.wait_ge(s["cx_ok"], 1)
            nc.tensor.matmul(sh, c("shift")[:, 0:R], r(cx), start=True, stop=True).then_inc(s["shift_ok"], 1)

        @block.vector
        def _(dve):
            v = nc.vector
            n = [0]

            def link(ins):
                n[0] += 1
                ins.then_inc(s["dchain"], 1)
                dve.wait_ge(s["dchain"], n[0])

            dve.wait_ge(s["hload"], 16)
            v.tensor_tensor(r(dtv), small[0:R, :, 2 * STATE:2 * STATE + HEADS], over_tiles(hr[0:R, 1, :], HEADS), ALU.add).then_inc(s["abs_in"], 1)
            dve.wait_ge(s["sig_ok"], 1)
            link(v.tensor_scalar_add(r(el), r(el), 1.0))
            link(v.reciprocal(r(el), r(el)))
            dve.wait_ge(s["soft_ok"], 1)
            link(v.scalar_tensor_tensor(out=r(dtv), in0=r(dtv), scalar=0.0, in1=r(ab), op0=ALU.max, op1=ALU.add))
            link(v.reduce_sum(r(dm), r(dtv), AX.X))
            link(v.tensor_scalar(r(dm), r(dm), 1.0 / HEADS, None, ALU.mult))
            v.tensor_tensor(r(th), small[0:R, :, SMALL - HALF:SMALL], dm[0:R, :, None].to_broadcast([R, NT, HALF]), ALU.mult).then_inc(s["theta_ok"], 1)
            link(v.tensor_tensor(r(cn), r(dtv), r(el), ALU.mult))
            link(v.tensor_scalar(r(el), r(el), -1.0, 1.0, ALU.mult, ALU.add))
            v.tensor_tensor(r(cx), r(dtv), r(el), ALU.mult).then_inc(s["cx_ok"], 1)
            dve.wait_ge(s["ea_ok"], 1)
            link(v.tensor_tensor(r(keep["loga"]), r(dtv), over_tiles(r(ea), HEADS), ALU.mult))
            link(v.tensor_scalar(r(keep["loga"]), r(keep["loga"]), -1.0, None, ALU.mult))
            dve.wait_ge(s["phi_ok"], 1)
            for q in range(2):
                v.tensor_scalar_add(ang[0:R, q * HT:(q + 1) * HT, 0, :], phi[q], float(np.pi / 2))
                last = v.tensor_copy(ang[0:R, q * HT:(q + 1) * HT, 1, :], phi[q])
            link(last)
            link(v.tensor_scalar(r(kf), r(ang), 1.0 / TWO_PI, MAGIC, ALU.mult, ALU.add))
            link(v.tensor_scalar(r(kf), r(kf), MAGIC, None, ALU.subtract))
            for part in (PI_HI, PI_MD, PI_LO):
                link(v.scalar_tensor_tensor(out=ang[0:R].rearrange("p t a n -> p (t a n)"),
                                            in0=kf[0:R].rearrange("p t a n -> p (t a n)"), scalar=-part,
                                            in1=ang[0:R].rearrange("p t a n -> p (t a n)"), op0=ALU.mult, op1=ALU.add))
            v.tensor_scalar(r(ang), r(ang), PI_IN, -PI_IN, ALU.min, ALU.max).then_inc(s["ang_ok"], 1)
            dve.wait_ge(s["shift_ok"], 1)
            link(v.tensor_tensor(r(keep["coef"]), r(cn), sh, ALU.add))
            dve.wait_ge(s["sin_ok"], 1)
            re, im = small[0:R, :, 0:HALF], small[0:R, :, HALF:STATE]
            co, si = ang[0:R, :, 0, :], ang[0:R, :, 1, :]
            v.tensor_tensor(r(ra), re, co, ALU.mult)
            link(v.tensor_tensor(r(rb), im, si, ALU.mult))
            v.tensor_tensor(keep["rot"][0:R, :, 0, 0:HALF], r(ra), r(rb), ALU.subtract)
            v.tensor_tensor(r(kf)[:, :, 0, :], re, si, ALU.mult)
            link(v.tensor_tensor(r(kf)[:, :, 1, :], im, co, ALU.mult))
            link(v.tensor_tensor(keep["rot"][0:R, :, 0, HALF:STATE], r(kf)[:, :, 0, :], r(kf)[:, :, 1, :], ALU.add))
            dve.wait_ge(s["rotc_ok"], 1)
            link(v.tensor_tensor(r(bc), keep["rot"][0:R, :, 0, :], keep["rot"][0:R, :, 1, :], ALU.mult))
            link(v.reduce_sum(r(gtt), r(bc), AX.X))
            link(v.tensor_tensor(r(keep["diag"]), r(cn), gtt[0:R, :, None].to_broadcast([R, NT, HEADS]), ALU.mult))
            link(v.tensor_tensor(r(keep["diag"]), r(keep["diag"]), over_tiles(hr[0:R, 2, :], HEADS), ALU.add))

        @block.gpsimd
        def _(pool):
            g = nc.gpsimd
            pool.wait_ge(s["sin_ok"], 1)
            re, im = small[0:R, :, STATE:STATE + HALF], small[0:R, :, STATE + HALF:2 * STATE]
            co, si = ang[0:R, :, 0, :], ang[0:R, :, 1, :]
            g.tensor_tensor(r(rc), re, co, ALU.mult)
            g.tensor_tensor(r(rd), im, si, ALU.mult).then_inc(s["pchain"], 1)
            pool.wait_ge(s["pchain"], 1)
            g.tensor_tensor(keep["rot"][0:R, :, 1, 0:HALF], r(rc), r(rd), ALU.subtract).then_inc(s["pchain"], 1)
            pool.wait_ge(s["pchain"], 2)
            g.tensor_tensor(r(rc), re, si, ALU.mult)
            g.tensor_tensor(r(rd), im, co, ALU.mult).then_inc(s["pchain"], 1)
            pool.wait_ge(s["pchain"], 3)
            g.tensor_tensor(keep["rot"][0:R, :, 1, HALF:STATE], r(rc), r(rd), ALU.add).then_inc(s["rotc_ok"], 1)


def mix_tokens(nc, ctx, sb, sems, ps, c, keep, recs, logits, acc, w_out, w_gate):
    wo = sb(ctx, "wo", [128, YC, E])
    wg = sb(ctx, "wg", [128, KC, NE])
    rotb = sb(ctx, "rotb", [128, 2, 2, STATE])
    bct = sb(ctx, "bct", [STATE, 2, 2, R])
    gm = sb(ctx, "gm", [128, 2, R])
    la = sb(ctx, "la", [128, HEADS, L])
    dec = sb(ctx, "dec", [128, HEADS, L])
    wm = sb(ctx, "wm", [128, 2, HEADS * R])
    xc = sb(ctx, "xc", [128, 2, INNER])
    xq = sb(ctx, "xq", [128, INNER])
    yg = sb(ctx, "yg", [128, INNER])
    yt = sb(ctx, "yt", [128, YC, R])
    h1 = sb(ctx, "h1", [128, 2, E])
    xn = sb(ctx, "xn", [128, 2, E])
    xnt = sb(ctx, "xnt", [128, KC, R])
    st = sb(ctx, "st3", [128, 6])
    mv = sb(ctx, "mv3", [128, 2])
    rs = sb(ctx, "rs3", [128, 1])
    tmp = sb(ctx, "tmp3", [128, 1])
    s = sems("passed_b w2load rot_ok bct_ps bct_ok g_ok gm_ok la_ok d_ok dec_ok wm_ok xc_ok xq_ok y_ok y1_ok yg_ok yt_ps yt_ok o_ok "
             "h1_ok st3_ok mv3_ok p4 rs3_ok xn_ok rec_ok xnt_ps xnt_ok l_ok lg_ok out0 out1")
    YP = ps[0:R, 0, :]
    DP = ps[0:R, 1:3, 0:HEADS * L // 2]
    BP = ps[0:STATE, 3, 0:2 * R].rearrange("p (a r) -> p a r", a=2)
    GP, LP = ps[0:R, 4, 0:R], ps[0:R, 4, 128:128 + NE]
    TP = ps[:, 5, 0:YC * R].rearrange("p (a r) -> p a r", a=YC)
    OP = ps[0:R, 6, 0:E]
    XP = ps[:, 7, 0:KC * R].rearrange("p (a r) -> p a r", a=KC)
    outs = [s["out0"], s["out1"]]

    def run(eng, lead, step, tail):
        lead(0, 0)
        step(0, 0, True, False)
        step(1, 1, True, True)
        pairs(eng, lambda i, b: step(i, b, True, True), 2, NT - 2)
        step(NT - 2, 0, True, True)
        step(NT - 1, 1, False, True)
        tail(NT - 1, 1)

    def nothing(i, b):
        pass

    with nc.Block() as block:
        @block.sync
        def _(sp):
            sp.dma_start(wo[:], w_out).then_inc(s["w2load"], 16)
            sp.dma_start(wg[:], w_gate).then_inc(s["w2load"], 16)

            def store(i, b, rows=R):
                sp.wait_ge(s["h1_ok"], i + 1)
                sp.dma_start(acc[bass.ds(i * R, rows), :], h1[0:rows, b, :]).then_inc(outs[b], 16)
            store(0, 0)
            store(1, 1)
            pairs(sp, store, 2, NT - 2)
            store(NT - 2, 0)
            store(NT - 1, 1, LAST)
            for o in outs:
                sp.wait_ge(o, 16 * (NT // 2))

        @block.tensor
        def _(pe):
            ident = c("ident", 128)[0:R, 0:R]

            def scores_a(i, b):
                lag(pe, s["bct_ok"], i, 1)
                settle(pe, s["passed_b"])
                for q in range(2):
                    last = nc.tensor.transpose(BP[:, q, :], rotb[0:R, b, q, :], ident)
                last.then_inc(s["bct_ps"], 1)
                pe.wait_ge(s["la_ok"], i + 1)
                lag(pe, s["dec_ok"], i, 1)
                for q in range(2):
                    last = nc.tensor.matmul(DP[:, q, :], c("after")[:, 0:R],
                                            la[0:R, q * 8:(q + 1) * 8, :].rearrange("p h l -> p (h l)"), start=True, stop=True)
                last.then_inc(s["d_ok"], 1)

            def scores_b(i, b):
                pe.wait_ge(s["bct_ok"], i + 1)
                lag(pe, s["gm_ok"], i, 1)
                lag(pe, s["lg_ok"], i, 3)
                nc.tensor.matmul(GP, bct[:, b, 0, :], bct[:, b, 1, :], start=True, stop=True).then_inc(s["g_ok"], 1)

            def logits_a(i, b):
                pe.wait_ge(s["xn_ok"], i + 1)
                lag(pe, s["xnt_ok"], i, 1)
                for k in range(KC):
                    last = nc.tensor.transpose(XP[:, k, :], xn[0:R, b, k * 128:(k + 1) * 128], ident)
                last.then_inc(s["xnt_ps"], 1)

            def logits_b(i, b, scores):
                pe.wait_ge(s["xnt_ok"], i + 1)
                if scores:
                    pe.wait_ge(s["gm_ok"], i + 3)
                for k in range(KC):
                    last = nc.tensor.matmul(LP, xnt[:, k, :], wg[:, k, :], start=(k == 0), stop=(k == KC - 1))
                last.then_inc(s["l_ok"], 1)

            def step(n, b, more, before):
                pe.wait_ge(s["wm_ok"], n + 1)
                pe.wait_ge(s["xc_ok"], n + 1)
                lag(pe, s["y1_ok"], n, 1)
                for h in range(HEADS):
                    last = nc.tensor.matmul(YP[:, h * HD:(h + 1) * HD], wm[0:R, b, h * R:(h + 1) * R],
                                            xc[0:R, b, h * HD:(h + 1) * HD], start=True, stop=True)
                last.then_inc(s["y_ok"], 1)
                if more:
                    pe.wait_ge(s["rot_ok"], n + 2)
                    scores_a(n + 1, 1 - b)
                if before:
                    logits_a(n - 1, 1 - b)
                if more:
                    scores_b(n + 1, 1 - b)
                pe.wait_ge(s["yg_ok"], n + 1)
                lag(pe, s["yt_ok"], n, 1)
                for k in range(YC):
                    last = nc.tensor.transpose(TP[:, k, :], yg[0:R, k * 128:(k + 1) * 128], ident)
                last.then_inc(s["yt_ps"], 1)
                if before:
                    logits_b(n - 1, 1 - b, more)
                pe.wait_ge(s["yt_ok"], n + 1)
                lag(pe, s["h1_ok"], n, 1)
                for k in range(YC):
                    last = nc.tensor.matmul(OP, yt[:, k, :], wo[:, k, :], start=(k == 0), stop=(k == YC - 1))
                last.then_inc(s["o_ok"], 1)

            def lead(i, b):
                pe.wait_ge(s["rot_ok"], 1)
                scores_a(i, b)
                scores_b(i, b)

            def tail(i, b):
                logits_a(i, b)
                logits_b(i, b, False)

            pe.wait_ge(s["w2load"], 32)
            run(pe, lead, step, tail)

        @block.scalar
        def _(act):
            a = nc.scalar

            def scores(i, b):
                act.wait_ge(s["bct_ps"], i + 1)
                a.activation(bct[:, b, :, :], BP, ACT.Copy).then_inc(s["bct_ok"], 1)
                act.wait_ge(s["d_ok"], i + 1)
                lag(act, s["wm_ok"], i, 1)
                a.activation(dec[0:R].rearrange("p (q h) l -> p q (h l)", q=2), DP, ACT.Exp).then_inc(s["dec_ok"], 1)

            def logit(i, b):
                act.wait_ge(s["xnt_ps"], i + 1)
                lag(act, s["l_ok"], i, 1)
                a.activation(xnt[:], XP, ACT.Copy).then_inc(s["xnt_ok"], 1)

            def step(n, b, more, before):
                if more:
                    scores(n + 1, 1 - b)
                if before:
                    logit(n - 1, 1 - b)
                act.wait_ge(s["yt_ps"], n + 1)
                lag(act, s["o_ok"], n, 1)
                a.activation(yt[:], TP, ACT.Copy).then_inc(s["yt_ok"], 1)

            run(act, scores, step, logit)

        @block.vector
        def _(dve):
            v = nc.vector

            def scores(i, b):
                dve.wait_ge(s["g_ok"], i + 1)
                v.tensor_tensor(gm[0:R, b, :], GP, c("causal")[:, 0:R], ALU.mult).then_inc(s["gm_ok"], 1)
                dve.wait_ge(s["gm_ok"], i + 1)
                dve.wait_ge(s["dec_ok"], i + 1)
                lag(dve, s["y_ok"], i, 2)
                v.tensor_tensor(wm[0:R, b, :].rearrange("p (h g l) -> p h g l", h=HEADS, g=G3),
                                dec[0:R, :, None, :].to_broadcast([R, HEADS, G3, L]),
                                gm[0:R, b, None, :].rearrange("p o (g l) -> p o g l", g=G3).to_broadcast([R, HEADS, G3, L]),
                                ALU.mult).then_inc(s["wm_ok"], 1)

            def logit(i, b):
                dve.wait_ge(s["l_ok"], i + 1)
                v.tensor_copy(row(logits, i), LP).then_inc(s["lg_ok"], 1)

            def step(n, b, more, before):
                dve.wait_ge(s["y_ok"], n + 1)
                dve.wait_ge(s["xq_ok"], n + 1)
                lag(dve, s["yt_ps"], n, 1)
                v.tensor_tensor(yg[0:R, :], YP, xq[0:R, :], ALU.add).then_inc(s["y1_ok"], 1)
                dve.wait_ge(s["y1_ok"], n + 1)
                v.tensor_tensor(yg[0:R, :], yg[0:R, :], row(keep["xz"], n)[:, INNER:], ALU.mult).then_inc(s["yg_ok"], 1)
                if more:
                    scores(n + 1, 1 - b)
                if before:
                    logit(n - 1, 1 - b)
                dve.wait_ge(s["o_ok"], n + 1)
                if not isinstance(n, int) or n >= 2:
                    dve.wait_ge(outs[b], 8 * (n - b))
                v.tensor_tensor(h1[0:R, b, :], OP, row(keep["hu"], n), ALU.add).then_inc(s["h1_ok"], 1)
                dve.wait_ge(s["h1_ok"], n + 1)
                v.bn_stats(st[0:R, :], h1[0:R, b, :]).then_inc(s["st3_ok"], 1)
                dve.wait_ge(s["st3_ok"], n + 1)
                settle(dve, s["passed_b"])
                v.bn_aggr(mv[0:R, :], st[0:R, :]).then_inc(s["mv3_ok"], 1)
                dve.wait_ge(s["rs3_ok"], n + 1)
                v.tensor_scalar(xn[0:R, b, :], h1[0:R, b, :], mv[0:R, 0:1], rs[0:R, :], ALU.subtract, ALU.mult).then_inc(s["xn_ok"], 1)

            run(dve, scores, step, logit)

        @block.gpsimd
        def _(pool):
            g = nc.gpsimd

            def scores(i, b):
                lag(pool, s["bct_ps"], i, 2)
                g.tensor_copy(rotb[0:R, b].rearrange("p a n -> p (a n)"),
                              row(keep["rot"][:].rearrange("p t a n -> p t (a n)"), i)).then_inc(s["rot_ok"], 1)
                lag(pool, s["d_ok"], i, 1)
                g.tensor_tensor(la[0:R], row(keep["loga"], i)[:, :, None].to_broadcast([R, HEADS, L]),
                                c("step")[:, None, :].to_broadcast([R, HEADS, L]), ALU.mult).then_inc(s["la_ok"], 1)
                lag(pool, s["y_ok"], i, 2)
                g.tensor_tensor(xc[0:R, b, :].rearrange("p (h d) -> p h d", h=HEADS),
                                row(keep["xz"], i)[:, 0:INNER].rearrange("p (h d) -> p h d", h=HEADS),
                                row(keep["coef"], i)[:, :, None].to_broadcast([R, HEADS, HD]), ALU.mult).then_inc(s["xc_ok"], 1)

            def diagonal(i, b):
                lag(pool, s["y1_ok"], i, 1)
                g.tensor_tensor(xq[0:R, :].rearrange("p (h d) -> p h d", h=HEADS),
                                row(keep["xz"], i)[:, 0:INNER].rearrange("p (h d) -> p h d", h=HEADS),
                                row(keep["diag"], i)[:, :, None].to_broadcast([R, HEADS, HD]), ALU.mult).then_inc(s["xq_ok"], 1)

            def step(n, b, more, before):
                diagonal(n, b)
                if more:
                    scores(n + 1, 1 - b)
                if before:
                    record(n - 1, 1 - b)
                pool.wait_ge(s["mv3_ok"], n + 1)
                g.tensor_tensor(tmp[0:R, :], mv[0:R, 1:2], c("eps5"), ALU.add).then_inc(s["p4"], 1)
                pool.wait_ge(s["p4"], n + 1)
                g.tensor_tensor(rs[0:R, :], tmp[0:R, :], c("neghalf"), ALU.pow).then_inc(s["rs3_ok"], 1)

            def record(i, b):
                pool.wait_ge(s["xn_ok"], i + 1)
                g.tensor_copy(row(recs, i)[:, 0:E], xn[0:R, b, :]).then_inc(s["rec_ok"], 1)

            run(pool, scores, step, record)


def route(nc, ctx, sb, sems, ps, c, recs, logits, posi, tab, upto_e, onehot, rec):
    mx = sb(ctx, "mx", [128, NT])
    pr = sb(ctx, "pr", [128, NT, NE])
    gt = sb(ctx, "gt", [128, NT, NE, NE])
    eq = sb(ctx, "eq", [128, NT, NE, NE])
    rank = sb(ctx, "rank", [128, NT, NE])
    sel = sb(ctx, "sel", [128, NT, NE])
    tot = sb(ctx, "tot", [128, NE, NT])
    run_ = sb(ctx, "run_", [128, NE, NT])
    cmp_ = sb(ctx, "cmp_", [128, NE, TOK // 128])
    te = sb(ctx, "te", [128, NE])
    ti = sb(ctx, "ti", [128, NE])
    pos = sb(ctx, "pos", [128, NT, NE])
    pk = sb(ctx, "pk", [128, NT, NE])
    pf = sb(ctx, "pf", [128, NT, 2])
    mk = sb(ctx, "mk", [128, NT, 2])
    et = sb(ctx, "et", [128, ST, NE - 1])
    ef = sb(ctx, "ef", [128, 2, ST])
    s = sems("ls_ok ex_ok sel_ok cnt_ok rchain ready scattered")
    WP = ps[0:R, 0, 0:NT * NE].rearrange("p (t e) -> p t e", e=NE)
    TPS = ps[:, 1, 0:NT * NE].rearrange("p (t e) -> p e t", e=NE)

    def r(t):
        return t[0:R]

    with nc.Block() as block:
        @block.scalar
        def _(act):
            act.wait_ge(s["ls_ok"], 1)
            nc.scalar.activation(r(pr), r(pr), ACT.Exp).then_inc(s["ex_ok"], 1)

        @block.tensor
        def _(pe):
            pe.wait_ge(s["sel_ok"], 1)
            flat = sel[0:R].rearrange("p t e -> p (t e)")
            nc.tensor.matmul(ps[0:R, 0, 0:NT * NE], c("before")[:, 0:R], flat, start=True, stop=True)
            nc.tensor.matmul(ps[:, 1, 0:NT * NE], c("ones"), flat, start=True, stop=True).then_inc(s["cnt_ok"], 1)

        @block.vector
        def _(dve):
            v = nc.vector
            n = [0]

            def link(ins):
                n[0] += 1
                ins.then_inc(s["rchain"], 1)
                dve.wait_ge(s["rchain"], n[0])

            shape4 = [R, NT, NE, NE]
            link(v.reduce_max(r(mx), r(logits), AX.X))
            v.tensor_tensor(r(pr), r(logits), mx[0:R, :, None].to_broadcast([R, NT, NE]), ALU.subtract).then_inc(s["ls_ok"], 1)
            dve.wait_ge(s["ex_ok"], 1)
            link(v.reduce_sum(r(mx), r(pr), AX.X))
            link(v.reciprocal(r(mx), r(mx)))
            link(v.tensor_tensor(r(pr), r(pr), mx[0:R, :, None].to_broadcast([R, NT, NE]), ALU.mult))
            pj, pe_ = pr[0:R, :, None, :].to_broadcast(shape4), pr[0:R, :, :, None].to_broadcast(shape4)
            v.tensor_tensor(r(gt), pj, pe_, ALU.is_gt)
            link(v.tensor_tensor(r(eq), pj, pe_, ALU.is_equal))
            link(v.tensor_tensor(eq[0:R].rearrange("p t a b -> p t (a b)"), eq[0:R].rearrange("p t a b -> p t (a b)"),
                                 c("lower")[:, None, :].to_broadcast([R, NT, NE * NE]), ALU.mult))
            link(v.tensor_tensor(r(gt), r(gt), r(eq), ALU.add))
            link(v.reduce_sum(r(rank), r(gt), AX.X))
            link(v.tensor_scalar(r(sel), r(rank), 2.0, None, ALU.is_lt))
            comb = recs[0:R, :, CW:CW + NE]
            link(v.tensor_tensor(comb, r(sel), r(pr), ALU.mult))
            link(v.reduce_sum(r(mx), comb, AX.X))
            link(v.reciprocal(r(mx), r(mx)))
            link(v.tensor_tensor(comb, comb, mx[0:R, :, None].to_broadcast([R, NT, NE]), ALU.mult))
            link(v.tensor_copy(recs[0:R, :, ID:ID + 1], c("rowid")[:, :, None]))
            v.memset(recs[0:R, :, CW + NE:RECW], 0.0)
            v.tensor_tensor(r(sel), r(sel), c("valid")[:, :, None].to_broadcast([R, NT, NE]), ALU.mult).then_inc(s["sel_ok"], 1)
            dve.wait_ge(s["cnt_ok"], 1)
            link(v.tensor_copy(tot[:], TPS))
            link(v.tensor_tensor_scan(run_[:].rearrange("p e t -> p (e t)"), c("carry", 128), tot[:].rearrange("p e t -> p (e t)"),
                                      0.0, ALU.mult, ALU.add))
            link(v.tensor_tensor(cmp_[:], run_[:, :, NT - 1:NT].to_broadcast([128, NE, TOK // 128]),
                                 c("by128", 128)[:, None, :].to_broadcast([128, NE, TOK // 128]), ALU.is_gt))
            link(v.reduce_sum(te[:], cmp_[:], AX.X))
            link(v.tensor_tensor_scan(ti[:], c("ones", 128)[:, 0:NE], te[:], 0.0, ALU.mult, ALU.add))
            v.tensor_copy(upto_e[:], ti[:])
            link(v.tensor_tensor(run_[:], run_[:], tot[:], ALU.subtract))
            link(v.tensor_tensor(te[:], ti[:], te[:], ALU.subtract))
            link(v.tensor_scalar(te[:], te[:], 128.0, None, ALU.mult))
            link(v.tensor_tensor(r(pos), WP, run_[0:R].rearrange("p e t -> p t e"), ALU.add))
            link(v.tensor_tensor(r(pos), r(pos), te[0:R, None, :].to_broadcast([R, NT, NE]), ALU.add))
            for k in range(2):
                link(v.tensor_scalar(r(pk), r(rank), float(k), None, ALU.is_equal))
                link(v.tensor_tensor(r(pk), r(pk), r(pos), ALU.mult))
                link(v.reduce_sum(pf[0:R, :, k], r(pk), AX.X))
            link(v.tensor_tensor(r(pf), r(pf), c("valid")[:, :, None].to_broadcast([R, NT, 2]), ALU.mult))
            link(v.tensor_scalar(mk[0:R, :, 0], c("valid"), -1.0, 1.0, ALU.mult, ALU.add))
            v.tensor_scalar(mk[0:R, :, 1], mk[0:R, :, 0], c("spare")[:, 1:2], None, ALU.mult)
            link(v.tensor_scalar(mk[0:R, :, 0], mk[0:R, :, 0], c("spare")[:, 0:1], None, ALU.mult))
            link(v.tensor_tensor(r(pf), r(pf), r(mk), ALU.add))
            v.tensor_copy(posi[0:R], r(pf)).then_inc(s["ready"], 1)
            link(v.tensor_tensor(et[:], c("tiles", 128)[:, :, None].to_broadcast([128, ST, NE - 1]),
                                 ti[:, None, 0:NE - 1].to_broadcast([128, ST, NE - 1]), ALU.is_ge))
            link(v.reduce_sum(ef[:, 0, :], et[:], AX.X))
            link(v.tensor_scalar(ef[:, 1, :], ef[:, 0, :], float(SLOTS), -float(SLOTS), ALU.is_ge, ALU.mult))
            link(v.tensor_tensor(ef[:, 1, :], ef[:, 1, :], ef[:, 0, :], ALU.add))
            v.tensor_copy(tab[:], ef[:])
            v.tensor_tensor(onehot[:], ef[:, 0, :, None].to_broadcast([128, ST, NE]),
                            c("experts", 128)[:, None, :].to_broadcast([128, ST, NE]), ALU.is_equal)

        @block.gpsimd
        def _(pool):
            pool.wait_ge(s["ready"], 1)
            for t in range(NT):
                for k in range(2):
                    nc.gpsimd.indirect_dma_start(
                        out=rec, out_offset=bass.IndirectOffsetOnAxis(ap=posi[0:R, t, k:k + 1], axis=0),
                        in_=recs[0:R, t, :], in_offset=None).then_inc(s["scattered"], 16)
            pool.wait_ge(s["scattered"], 16 * 2 * NT)


def experts(nc, ctx, sb, sems, ps, c, tab, upto_e, onehot, rec, acc, w_experts, out):
    wts = sb(ctx, "wts", [128, SLOTS, WEXP])
    xr = sb(ctx, "xr", [128, 2, RECW])
    xt = sb(ctx, "xt4", [128, 2, KC, 128])
    sg = sb(ctx, "sg", [128, 2, HFF])
    hh = sb(ctx, "hh", [128, 2, HFF])
    ht = sb(ctx, "ht", [128, 2, 4, 128])
    ys = sb(ctx, "ys", [128, 2, E])
    wj = sb(ctx, "wj", [128, NE])
    ws = sb(ctx, "ws", [128, 2])
    ids = sb(ctx, "ids", [128, 2], i32)
    s = sems("passed_c wdma w_ready rec0 rec1 xt4_ps xt4_ok gu_ok sg_ok hh_ok ht_ps ht_ok dn_ok wj_ok ws_ok ys_ok add0 add1 copied")
    recd, added = [s["rec0"], s["rec1"]], [s["add0"], s["add1"]]
    GUP = [[ps[:, 2 * q, :], ps[:, 2 * q + 1, :]] for q in range(2)]
    HT = [ps[:, 4 + q, :].rearrange("p (a r) -> p a r", a=4) for q in range(2)]
    YP = ps[:, 6, 0:E]
    XP = ps[:, 7, 0:KC * 128].rearrange("p (a r) -> p a r", a=KC)

    def each_tile(eng, step):
        step(0, 0, False, True)
        step(1, 1, True, True)
        pairs(eng, lambda i, b: step(i, b, True, True), 2, ST - 1)
        step(ST - 1, 0, True, False)

    def add_done(eng, t, b):
        if not isinstance(t, int) or t >= 2:
            eng.wait_ge(added[b], 8 * (t - b))

    with nc.Block() as block:
        @block.sync
        def _(sp):
            for e in range(NE):
                if e >= SLOTS:
                    tiles = sp.value_load(upto_e[0:1, e - SLOTS:e - SLOTS + 1], min_val=0, max_val=ST)
                    sp.wait_ge(s["dn_ok"], 2 * tiles + 1)
                sp.dma_start(wts[:, e % SLOTS, :], w_experts[e]).then_inc(s["wdma"], 16)
                sp.wait_ge(s["wdma"], 16 * (e + 1))
                sp.sem_inc(s["w_ready"], 1)
            for q in range(2):
                sp.wait_ge(added[q], 16 * ((ST + 1 - q) // 2))
            sp.dma_start(out.rearrange("b l e -> (b l) e"), acc[0:TOK, :]).then_inc(s["copied"], 16)
            sp.wait_ge(s["copied"], 16)

        @block.gpsimd
        def _(pool):
            def record(t, b):
                pool.dma_start(xr[:, b, :], rec[bass.ds(t * 128, 128), :]).then_inc(recd[b], 16)

            def step(i, b, before, more):
                if not isinstance(i, int) or i < ST - 2:
                    pool.wait_ge(s["ws_ok"], i + 1)
                    pool.wait_ge(s["xt4_ps"], i + 1)
                    record(i + 2, b)
                if before:
                    scatter(i - 1, 1 - b)

            def scatter(t, b):
                pool.wait_ge(s["ys_ok"], t + 1)
                if not isinstance(t, int) or t >= 1:
                    pool.wait_ge(added[1 - b], 8 * t if b == 0 else 8 * (t + 1))
                settle(pool, s["passed_c"])
                nc.gpsimd.indirect_dma_start(
                    out=acc, out_offset=bass.IndirectOffsetOnAxis(ap=ids[:, b:b + 1], axis=0),
                    in_=ys[:, b, :], in_offset=None, compute_op=ALU.add).then_inc(added[b], 16)

            record(0, 0)
            record(1, 1)
            step(0, 0, False, True)
            step(1, 1, True, True)
            pairs(pool, lambda i, b: step(i, b, True, True), 2, ST - 3)
            step(ST - 3, 0, True, True)
            step(ST - 2, 1, True, True)
            step(ST - 1, 0, True, False)
            scatter(ST - 1, 0)

        @block.tensor
        def _(pe):
            ident = c("ident", 128)

            def features(t, b):
                pe.wait_ge(recd[b], 8 * (t + 2 - b))
                lag(pe, s["xt4_ok"], t, 1)
                for k in range(KC):
                    last = nc.tensor.transpose(XP[:, k, :], xr[:, b, k * 128:(k + 1) * 128], ident)
                last.then_inc(s["xt4_ps"], 1)

            def gate_up(i, b, q, place):
                if q == 0:
                    pe.wait_ge(s["xt4_ok"], i + 1)
                if not isinstance(i, int) or i >= 1:
                    pe.wait_ge(s["hh_ok"], 2 * i + q - 1)
                for k in range(KC):
                    for u in range(2):
                        at = OFF_GU + k * 2 * FF + u * FF + q * HFF
                        last = nc.tensor.matmul(GUP[q][u], xt[:, b, k, :], row(wts, place, 128)[:, at:at + HFF],
                                                start=(k == 0), stop=(k == KC - 1))
                last.then_inc(s["gu_ok"], 1)

            def turn(i, q):
                pe.wait_ge(s["hh_ok"], 2 * i + q + 1)
                if not isinstance(i, int) or i >= 1:
                    pe.wait_ge(s["ht_ok"], 2 * i + q - 1)
                for a in range(4):
                    last = nc.tensor.transpose(HT[q][:, a, :], hh[:, q, a * 128:(a + 1) * 128], ident)
                last.then_inc(s["ht_ps"], 1)

            def down(i, q, place):
                pe.wait_ge(s["ht_ok"], 2 * i + q + 1)
                if q == 0:
                    lag(pe, s["ys_ok"], i, 1)
                for a in range(4):
                    at = OFF_DN + (4 * q + a) * E
                    last = nc.tensor.matmul(YP, ht[:, q, a, :], row(wts, place, 128)[:, at:at + E],
                                            start=(q == 0 and a == 0), stop=(q == 1 and a == 3))
                last.then_inc(s["dn_ok"], 1)

            def place_of(t):
                return pe.value_load(tab[0:1, 1, bass.ds(t, 1)], min_val=0, max_val=SLOTS - 1)

            def step(i, b, before, more):
                place = place_of(i)
                expert = pe.value_load(tab[0:1, 0, bass.ds(i, 1)], min_val=0, max_val=NE - 1)
                pe.wait_ge(s["w_ready"], expert + 1)
                gate_up(i, b, 0, place)
                if before:
                    last_place = place_of(i - 1)
                    turn(i - 1, 1)
                    down(i - 1, 0, last_place)
                gate_up(i, b, 1, place)
                if more:
                    features(i + 1, 1 - b)
                turn(i, 0)
                if before:
                    down(i - 1, 1, last_place)

            pe.sem_inc(s["dn_ok"], 1)
            features(0, 0)
            each_tile(pe, step)
            turn(ST - 1, 1)
            last_place = place_of(ST - 1)
            down(ST - 1, 0, last_place)
            down(ST - 1, 1, last_place)

        @block.scalar
        def _(act):
            a = nc.scalar

            def gate(i, q):
                act.wait_ge(s["gu_ok"], 2 * i + q + 1)
                if not isinstance(i, int) or i >= 1:
                    act.wait_ge(s["hh_ok"], 2 * i + q - 1)
                a.activation(sg[:, q, :], GUP[q][0], ACT.Silu).then_inc(s["sg_ok"], 1)

            def turned(i, q):
                act.wait_ge(s["ht_ps"], 2 * i + q + 1)
                if not isinstance(i, int) or i >= 1:
                    act.wait_ge(s["dn_ok"], 2 * i + q)
                a.activation(ht[:, q], HT[q], ACT.Copy).then_inc(s["ht_ok"], 1)

            def step(i, b, before, more):
                gate(i, 0)
                if before:
                    turned(i - 1, 1)
                gate(i, 1)
                turned(i, 0)

            each_tile(act, step)
            turned(ST - 1, 1)

        @block.vector
        def _(dve):
            v = nc.vector

            def features(t, b):
                dve.wait_ge(s["xt4_ps"], t + 1)
                if not isinstance(t, int) or t >= 2:
                    dve.wait_ge(s["gu_ok"], 2 * t - 2)
                v.tensor_copy(xt[:, b], XP).then_inc(s["xt4_ok"], 1)

            def gated(i, q):
                dve.wait_ge(s["sg_ok"], 2 * i + q + 1)
                if not isinstance(i, int) or i >= 1:
                    dve.wait_ge(s["ht_ps"], 2 * i + q - 1)
                v.tensor_tensor(hh[:, q, :], sg[:, q, :], GUP[q][1], ALU.mult).then_inc(s["hh_ok"], 1)

            def weights(t, b):
                dve.wait_ge(recd[b], 8 * (t + 2 - b))
                add_done(dve, t, b)
                v.tensor_tensor(wj[:], xr[:, b, CW:CW + NE], row(onehot, t, 128), ALU.mult).then_inc(s["wj_ok"], 1)
                dve.wait_ge(s["wj_ok"], t + 1)
                v.reduce_sum(ws[:, b:b + 1], wj[:], AX.X)
                v.tensor_copy(ids[:, b:b + 1], xr[:, b, ID:ID + 1]).then_inc(s["ws_ok"], 1)

            def result(t, b):
                dve.wait_ge(s["dn_ok"], 2 * t + 3)
                dve.wait_ge(s["ws_ok"], t + 1)
                v.tensor_scalar(ys[:, b, :], YP, ws[:, b:b + 1], None, ALU.mult).then_inc(s["ys_ok"], 1)

            def step(i, b, before, more):
                gated(i, 0)
                weights(i, b)
                gated(i, 1)
                if more:
                    features(i + 1, 1 - b)
                if before:
                    result(i - 1, 1 - b)

            features(0, 0)
            each_tile(dve, step)
            result(ST - 1, 0)


def kernel(x, cls_tok, L0_tok_W, L0_tok_b, L0_tok_cls_token, L0_tok_pos_embedding, L0_tok_gamma, L0_tok_beta,
           L0_attn_norm_scale, L0_attn_norm_bias, L0_attn_in_proj_w, L0_attn_A_log, L0_attn_dt_bias,
           L0_attn_bcB_scale, L0_attn_bcC_scale, L0_attn_B_bias, L0_attn_C_bias, L0_attn_theta_w, L0_attn_D,
           L0_attn_out_proj_w, L0_ffn_gate_w, L0_ffn_gate_up_proj, L0_ffn_down_proj):
    import concourse.bacc as bacc
    from concourse.bass_utils import run_bass_kernel_spmd

    def f(a):
        return np.asarray(a)

    p = f(x).reshape(BATCH, CH, HP, PATCH, HP, PATCH).transpose(1, 3, 5, 0, 2, 4).reshape(D, BATCH, NP)
    full = np.zeros((D, NT * G3, L), p.dtype)
    full[:, :BATCH, 2:] = p
    patches = full.reshape(DC, 128, NT, R).transpose(2, 1, 0, 3).reshape(NT, 128, DC * R)
    pos = f(L0_tok_pos_embedding)[0]
    base_a = np.tile(np.concatenate([np.zeros_like(pos[:1]), pos], 0), (G3, 1))
    base_b = np.tile(np.concatenate([f(cls_tok)[0], f(L0_tok_cls_token)[0], np.broadcast_to(f(L0_tok_b), (NP, E))], 0), (G3, 1))
    gam = np.tile(np.concatenate([np.ones_like(pos[:1]), np.broadcast_to(f(L0_tok_gamma), (L - 1, E))], 0), (G3, 1))
    bet = np.tile(np.concatenate([np.zeros_like(pos[:1]), np.broadcast_to(f(L0_tok_beta), (L - 1, E))], 0), (G3, 1))

    def chunks(w):
        return w.reshape(-1, 128, w.shape[-1]).transpose(1, 0, 2)

    def spread(rows_):
        return np.broadcast_to(np.stack(rows_)[None], (R, len(rows_), rows_[0].shape[-1]))

    gu = f(L0_ffn_gate_up_proj).transpose(0, 2, 1).reshape(NE, KC, 128, 2 * FF).transpose(0, 2, 1, 3).reshape(NE, 128, -1)
    dn = f(L0_ffn_down_proj).transpose(0, 2, 1).reshape(NE, FC, 128, E).transpose(0, 2, 1, 3).reshape(NE, 128, -1)
    arrays = dict(
        patches=patches, base_a=base_a, base_b=base_b, gammas=gam, betas=bet,
        w_tok=chunks(f(L0_tok_W)), w_in=chunks(f(L0_attn_in_proj_w)), w_theta=chunks(f(L0_attn_theta_w)),
        norm_cols=np.stack([f(L0_attn_norm_scale).reshape(KC, 128).T, f(L0_attn_norm_bias).reshape(KC, 128).T], 1),
        head_rows=spread([f(L0_attn_A_log), f(L0_attn_dt_bias), f(L0_attn_D)]),
        bc_rows=spread([f(L0_attn_bcB_scale), f(L0_attn_bcC_scale), f(L0_attn_B_bias), f(L0_attn_C_bias)]),
        w_out=chunks(f(L0_attn_out_proj_w)), w_gate=chunks(f(L0_ffn_gate_w).T),
        w_experts=np.concatenate([gu, dn], 2), consts=CONSTS)
    nc = bacc.Bacc("TRN2", target_bir_lowering=False, num_devices=1)
    fed, args = {}, {}
    for name, a in arrays.items():
        fed["in_" + name] = np.ascontiguousarray(a)
        args[name] = nc.dram_tensor("in_" + name, a.shape, mybir.dt.from_np(a.dtype), kind="ExternalInput").ap()
    out = nc.dram_tensor("result", (BATCH, L, E), f32, kind="ExternalOutput").ap()
    program(nc, out=out, **args)
    return run_bass_kernel_spmd(nc, [fed], core_ids=[0]).results[0]["result"]
```

```python
import concourse.bass as bass
from concourse import mybir
from concourse.alu_op_type import AluOpType as ALU
from contextlib import ExitStack
import numpy as np

BATCH, CH, IMG, PATCH = 64, 3, 96, 16
E = 256
HP = IMG // PATCH
NP = HP * HP
D = CH * PATCH * PATCH
L = NP + 2
G3 = 3
R = G3 * L
NT = -(-BATCH // G3)
LAST = (BATCH - G3 * (NT - 1)) * L
TOK = BATCH * L
INNER, STATE, HEADS = 512, 64, 16
HD = INNER // HEADS
HALF = STATE // 2
SMALL = 2 * STATE + 2 * HEADS + HALF
PROJ = 2 * INNER + 2 * STATE + 2 * HEADS
DC, KC, YC = D // 128, E // 128, INNER // 128
NE, FF = 8, 1024
FC = FF // 128
HFF = FF // 2
ST = TOK * 2 // 128 + NE - 1
RECW = E + NE
CW = E
ACC = TOK + 128
WEXP = KC * 2 * FF + FC * E
SLOTS = 4
OFF_GU, OFF_DN = 0, KC * 2 * FF

f32, i32 = mybir.dt.float32, mybir.dt.int32
ACT = mybir.ActivationFunctionType
AX = mybir.AxisListType
TWO_PI = 2.0 * np.pi
MAGIC = 1.5 * 2.0 ** 23
PI_HI = float(np.float32(6.28125))
PI_MD = float(np.float32(TWO_PI - 6.28125))
PI_LO = float(TWO_PI - 6.28125 - np.float32(TWO_PI - 6.28125))
PI_IN = 3.1415925

CONST = {}


def constants():
    k = np.arange(128)
    kk, ss = np.meshgrid(k, k, indexing="ij")
    same = (kk // L == ss // L) & (kk < R) & (ss < R)
    parts = [
        ("ident", np.eye(128)),
        ("causal", same & (kk < ss)),
        ("upto", same & (kk <= ss)),
        ("after", same & (kk > ss)),
        ("shift", same & (kk == ss + 1)),
        ("before", kk < ss),
        ("ones", np.ones((128, 128))),
        ("step", (k[:, None] % L) <= np.arange(L)[None, :]),
        ("lower", np.broadcast_to((np.arange(NE)[None, :] < np.arange(NE)[:, None]).reshape(1, -1), (128, NE * NE))),
        ("normed", (k % L != 0)[:, None]),
        ("raw", (k % L == 0)[:, None]),
        ("valid", (np.arange(NT)[None, :] * R + k[:, None] < TOK)),
        ("far", (np.arange(NT)[None, :] * R + k[:, None] >= TOK) * -1000.0),
        ("rowid1", np.arange(NT)[None, :] * R + k[:, None] + 1),
        ("spare1", (TOK + k + 1)[:, None]),
        ("lanes", np.broadcast_to(k[None, :], (128, 128))),
        ("carry", np.broadcast_to((np.arange(NT) != 0)[None, None, :], (128, NE, NT)).reshape(128, -1)),
        ("carry8", np.broadcast_to((np.arange(NE) != 0)[None, :], (128, NE))),
        ("by128", np.broadcast_to(np.arange(TOK // 128)[None, :] * 128.0, (128, TOK // 128))),
        ("tiles", np.broadcast_to(np.arange(ST)[None, :], (128, ST))),
        ("experts", np.broadcast_to(np.arange(NE)[None, :], (128, NE))),
        ("neghalf", np.full((128, 1), -0.5)),
        ("eps5", np.full((128, 1), 1e-5)),
        ("eps6", np.full((128, 2), 1e-6)),
        ("halfpi", np.full((128, 1), np.pi / 2)),
    ]
    at = 0
    for name, a in parts:
        CONST[name] = (at, at + a.shape[1])
        at += a.shape[1]
    return np.concatenate([np.asarray(a, np.float32) for _, a in parts], 1)


CONSTS = constants()


def program(nc, patches, base_a, base_b, gammas, betas, w_tok, w_in, w_theta, norm_cols, head_rows,
            bc_rows, w_out, w_gate, w_experts, consts, out):
    rec = nc.dram_tensor("records", (ACC, RECW), f32, kind="Internal").ap()
    acc = nc.dram_tensor("accumulator", (ACC, E), f32, kind="Internal").ap()
    with ExitStack() as top:
        def sb(ctx, name, shape, dt=f32):
            return ctx.enter_context(nc.sbuf_tensor(name, shape, dt))

        def sems(names):
            return {n: top.enter_context(nc.semaphore(n)) for n in names.split()}

        ps = top.enter_context(nc.psum_tensor("ps", [128, 8, 512], f32))
        cst = sb(top, "cst", [128, CONSTS.shape[1]])
        slot_row = sb(top, "slot_row", [128, ST], i32)
        logits = sb(top, "logits", [128, NT, NE])
        tab = sb(top, "tab", [128, 2, ST], i32)
        upto_e = sb(top, "upto_e", [128, NE], i32)
        onehot = sb(top, "onehot", [128, ST, NE])

        def c(name, rows=R):
            a, b = CONST[name]
            return cst[0:rows, a:b]

        with ExitStack() as mid:
            keep = dict(
                xz=sb(mid, "xz", [128, NT, 2 * INNER]), hu=sb(mid, "hu", [128, NT, E]),
                rot=sb(mid, "rot", [128, NT, 2, STATE]), loga=sb(mid, "loga", [128, NT, HEADS]),
                coef=sb(mid, "coef", [128, NT, HEADS]), diag=sb(mid, "diag", [128, NT, HEADS]))
            with ExitStack() as first:
                small = sb(first, "small", [128, NT, SMALL])
                with ExitStack() as ctx:
                    embed_and_project(nc, ctx, sb, sems, ps, cst, c, keep, small, rec, acc, patches, base_a, base_b,
                                      gammas, betas, w_tok, w_in, w_theta, norm_cols, bc_rows, consts)
                with ExitStack() as ctx:
                    scan_coefficients(nc, ctx, sb, sems, ps, c, keep, small, head_rows)
            with ExitStack() as ctx:
                mix_tokens(nc, ctx, sb, sems, ps, c, keep, rec, logits, acc, w_out, w_gate)
        with ExitStack() as ctx:
            wts = sb(ctx, "wts", [128, SLOTS, WEXP])
            wload = sems("wdma w_ready")
            with ExitStack() as inner:
                route(nc, inner, sb, sems, ps, c, logits, slot_row, tab, upto_e, onehot, rec, wts, wload, w_experts)
            experts(nc, ctx, sb, sems, ps, c, slot_row, tab, upto_e, onehot, rec, acc, wts, wload, w_experts, out)


def lag(eng, sem, i, n):
    if not isinstance(i, int) or i >= n:
        eng.wait_ge(sem, i - n + 1)


def settle(eng, sem):
    eng.sem_inc(sem, 1)


def row(t, i, rows=R):
    return t[0:rows, bass.ds(i, 1), :].rearrange("p o n -> p (o n)")


def live(i):
    return not isinstance(i, int) or 0 <= i < NT


def steps(eng, step, ahead, behind):
    lo = (behind + 3) // 2 * 2
    hi = (NT - ahead) // 2 * 2
    for n in range(-ahead, lo):
        step(n, n % 2)
    pairs(eng, step, lo, hi)
    for n in range(hi, NT + behind):
        step(n, n % 2)


def pairs(eng, step, first, last):
    assert (last - first) % 2 == 0 and first % 2 == 0
    with eng.Fori(first // 2, last // 2) as j:
        step(2 * j, 0)
        step(2 * j + 1, 1)


def embed_and_project(nc, ctx, sb, sems, ps, cst, c, keep, small, rec, acc, patches, base_a, base_b, gammas,
                      betas, w_tok, w_in, w_theta, norm_cols, bc_rows, consts):
    pin = sb(ctx, "pin", [128, 2, DC * R])
    wt = sb(ctx, "wt", [128, DC, E])
    wi = sb(ctx, "wi", [128, KC, PROJ])
    wth = sb(ctx, "wth", [128, KC, HALF])
    base = sb(ctx, "base", [128, E])
    gam = sb(ctx, "gam", [128, E])
    bet = sb(ctx, "bet", [128, E])
    ncol = sb(ctx, "ncol", [128, 2, KC])
    bcr = sb(ctx, "bcr", [128, 4, STATE])
    pre = sb(ctx, "pre", [128, E])
    hid = sb(ctx, "hid", [128, 2, E])
    ux = sb(ctx, "ux", [128, 2, 2, E])
    xt = sb(ctx, "xt", [128, 2, 4, R])
    bcw = sb(ctx, "bcw", [128, 2, STATE])
    junk = sb(ctx, "junk", [128, 2, STATE])
    st = sb(ctx, "st", [128, 6])
    mv1 = sb(ctx, "mv1", [128, 2, 2])
    mv2 = sb(ctx, "mv2", [128, 2, 2])
    rs1 = sb(ctx, "rs1", [128, 2])
    rs2 = sb(ctx, "rs2", [128, 2, 2])
    rcp = sb(ctx, "rcp", [128, 1])
    ms = sb(ctx, "ms", [128, 2])
    empty = sb(ctx, "empty", [128, RECW])
    s = sems("passed_a wload tokload base_ok patch0 patch1 embedded pre_ok st1 mv1_ok var1_ok mean1_ok rs1_ok m1 n1 n2 "
             "hid_ok st2 mv2_ok var2_ok rcp_ok var3_ok rs2_ok u_ok ux_ok xt_ps xt_ok proj_ok silu_ok small_ok bcw_ok "
             "ms_ok rms_ok bn0 bn_ok hu_ok empty0 empty_out")
    patch = [s["patch0"], s["patch1"]]
    tok = [ps[0:R, b, 0:E] for b in range(2)]
    tps = [ps[:, 2 + b, 0:4 * R].rearrange("p (a r) -> p a r", a=4) for b in range(2)]
    XP, ZP, SP_ = ps[0:R, 4, :], ps[0:R, 5, :], ps[0:R, 6, 0:SMALL]

    with nc.Block() as block:
        @block.sync
        def _(sp):
            sp.dma_start(pin[:, 0, :], patches[0]).then_inc(patch[0], 16)
            sp.dma_start(wt[:], w_tok).then_inc(s["tokload"], 16)
            sp.dma_start(pin[:, 1, :], patches[1]).then_inc(patch[1], 16)
            for dst, src in ((base[0:R, :], base_a), (pre[0:R, :], base_b), (cst[:], consts), (gam[0:R, :], gammas),
                             (bet[0:R, :], betas), (ncol[:], norm_cols), (wi[:], w_in), (wth[:], w_theta),
                             (bcr[0:R], bc_rows)):
                sp.dma_start(dst, src).then_inc(s["wload"], 16)

            def step(i, b):
                sp.wait_ge(s["embedded"], i - 1)
                sp.dma_start(pin[:, b, :], patches[bass.ds(i, 1)].rearrange("o p n -> p (o n)")).then_inc(patch[b], 16)
            pairs(sp, step, 2, NT)
            sp.wait_ge(s["empty0"], 1)
            sp.dma_start(rec[TOK:ACC, :], empty[:]).then_inc(s["empty_out"], 16)
            sp.dma_start(acc[TOK:ACC, :], empty[:, 0:E]).then_inc(s["empty_out"], 16)
            sp.wait_ge(s["empty_out"], 32)

        @block.tensor
        def _(pe):
            ident = c("ident", 128)[0:R, 0:R]

            def embed(i, b):
                pe.wait_ge(patch[b], 8 * (i + 2 - b))
                lag(pe, s["pre_ok"], i, 2)
                for k in range(DC):
                    last = nc.tensor.matmul(tok[b], pin[:, b, k * R:(k + 1) * R], wt[:, k, :],
                                            start=(k == 0), stop=(k == DC - 1))
                last.then_inc(s["embedded"], 1)

            def turn(i, b):
                pe.wait_ge(s["ux_ok"], i + 1)
                lag(pe, s["xt_ok"], i, 2)
                for a in range(4):
                    last = nc.tensor.transpose(tps[b][:, a, :], ux[0:R, b, a // 2, (a % 2) * 128:(a % 2) * 128 + 128], ident)
                last.then_inc(s["xt_ps"], 1)

            def step(n, b):
                if live(n + 2):
                    embed(n + 2, b)
                if live(n + 1):
                    turn(n + 1, 1 - b)
                if live(n):
                    pe.wait_ge(s["xt_ok"], n + 1)
                    lag(pe, s["silu_ok"], n, 1)
                    lag(pe, s["small_ok"], n, 1)
                    if isinstance(n, int) and n == 0:
                        pe.wait_ge(s["wload"], 16 * 9)
                    for k in range(KC):
                        x = xt[:, b, 2 + k, :]
                        first, end = k == 0, k == KC - 1
                        nc.tensor.matmul(XP, x, wi[:, k, 0:INNER], start=first, stop=end)
                        nc.tensor.matmul(ZP, x, wi[:, k, INNER:2 * INNER], start=first, stop=end)
                        nc.tensor.matmul(SP_[:, 0:SMALL - HALF], x, wi[:, k, 2 * INNER:], start=first, stop=end)
                    for k in range(KC):
                        last = nc.tensor.matmul(SP_[:, SMALL - HALF:], xt[:, b, k, :], wth[:, k, :], start=(k == 0),
                                                stop=(k == KC - 1))
                    last.then_inc(s["proj_ok"], 1)

            pe.wait_ge(s["tokload"], 16)
            steps(pe, step, 2, 0)

        @block.vector
        def _(dve):
            v = nc.vector
            v.memset(empty[:], 0.0).then_inc(s["empty0"], 1)
            dve.wait_ge(s["wload"], 16 * 9)
            v.tensor_tensor(base[0:R, :], base[0:R, :], pre[0:R, :], ALU.add).then_inc(s["base_ok"], 1)
            dve.wait_ge(s["base_ok"], 1)

            def statistics(i, b):
                if not live(i):
                    return
                m1 = mv1[0:R, b, :]
                dve.wait_ge(s["embedded"], i + 1)
                lag(dve, s["n1"], i, 1)
                v.tensor_tensor(pre[0:R, :], tok[b], base[0:R, :], ALU.add).then_inc(s["pre_ok"], 1)
                dve.wait_ge(s["pre_ok"], i + 1)
                v.bn_stats(st[0:R, :], pre[0:R, :]).then_inc(s["st1"], 1)
                dve.wait_ge(s["st1"], i + 1)
                settle(dve, s["passed_a"])
                v.bn_aggr(m1, st[0:R, :]).then_inc(s["mv1_ok"], 1)
                dve.wait_ge(s["mv1_ok"], i + 1)
                v.tensor_scalar_add(rs1[0:R, b:b + 1], m1[:, 1:2], 1e-5).then_inc(s["var1_ok"], 1)
                v.tensor_tensor(m1[:, 0:1], m1[:, 0:1], c("normed"), ALU.mult).then_inc(s["mean1_ok"], 1)

            def tokenizer_norm(i, b):
                if not live(i):
                    return
                h, m1, m2, r1 = hid[0:R, b, :], mv1[0:R, b, :], mv2[0:R, b, :], rs1[0:R, b:b + 1]
                dve.wait_ge(s["rs1_ok"], i + 1)
                v.tensor_scalar(r1, r1, c("normed"), c("raw"), ALU.mult, ALU.add).then_inc(s["m1"], 1)
                dve.wait_ge(s["m1"], i + 1)
                lag(dve, s["hu_ok"], i, 2)
                v.tensor_scalar(h, pre[0:R, :], m1[:, 0:1], r1, ALU.subtract, ALU.mult).then_inc(s["n1"], 1)
                dve.wait_ge(s["n1"], i + 1)
                v.tensor_tensor(h, h, gam[0:R, :], ALU.mult).then_inc(s["n2"], 1)
                dve.wait_ge(s["n2"], i + 1)
                v.tensor_tensor(h, h, bet[0:R, :], ALU.add).then_inc(s["hid_ok"], 1)
                dve.wait_ge(s["hid_ok"], i + 1)
                v.bn_stats(st[0:R, :], h).then_inc(s["st2"], 1)
                dve.wait_ge(s["st2"], i + 1)
                settle(dve, s["passed_a"])
                v.bn_aggr(m2, st[0:R, :]).then_inc(s["mv2_ok"], 1)
                dve.wait_ge(s["mv2_ok"], i + 1)
                v.tensor_scalar_add(rs2[0:R, b, 0:1], m2[:, 1:2], 1e-5).then_inc(s["var2_ok"], 1)
                dve.wait_ge(s["var2_ok"], i + 1)
                v.reciprocal(rcp[0:R, :], rs2[0:R, b, 0:1]).then_inc(s["rcp_ok"], 1)
                dve.wait_ge(s["rcp_ok"], i + 1)
                v.tensor_scalar(rs2[0:R, b, 1:2], rcp[0:R, :], m2[:, 1:2], 1e-6, ALU.mult, ALU.add).then_inc(s["var3_ok"], 1)

            def mixer_norms(i, b):
                if not live(i):
                    return
                u, xh = ux[0:R, b, 0, :], ux[0:R, b, 1, :]
                dve.wait_ge(s["rs2_ok"], i + 1)
                lag(dve, s["xt_ps"], i, 2)
                v.tensor_scalar(u, hid[0:R, b, :], mv2[0:R, b, 0:1], rs2[0:R, b, 0:1], ALU.subtract, ALU.mult).then_inc(s["u_ok"], 1)
                dve.wait_ge(s["u_ok"], i + 1)
                v.tensor_scalar(xh, u, rs2[0:R, b, 1:2], None, ALU.mult).then_inc(s["ux_ok"], 1)

            def take_small(i, b):
                if not live(i):
                    return
                dve.wait_ge(s["proj_ok"], i + 1)
                lag(dve, s["bn_ok"], i, 1)
                v.tensor_copy(bcw[0:R].rearrange("p a n -> p (a n)"), SP_[:, 0:2 * STATE]).then_inc(s["bcw_ok"], 1)
                v.tensor_copy(row(small, i)[:, 2 * STATE:], SP_[:, 2 * STATE:]).then_inc(s["small_ok"], 1)
                dve.wait_ge(s["bcw_ok"], i + 1)
                for a in range(2):
                    last = v.tensor_tensor_reduce(out=junk[0:R, a, :], in0=bcw[0:R, a, :], in1=bcw[0:R, a, :], scale=1.0 / STATE,
                                                  scalar=1e-6, op0=ALU.mult, op1=ALU.add, accum_out=ms[0:R, a:a + 1])
                last.then_inc(s["ms_ok"], 1)

            def norm_small(i, b):
                if not live(i):
                    return
                dve.wait_ge(s["rms_ok"], i + 1)
                for a in range(2):
                    last = v.scalar_tensor_tensor(out=bcw[0:R, a, :], in0=bcw[0:R, a, :], scalar=ms[0:R, a:a + 1],
                                                  in1=bcr[0:R, a, :], op0=ALU.mult, op1=ALU.mult)
                last.then_inc(s["bn0"], 1)
                dve.wait_ge(s["bn0"], i + 1)
                v.tensor_tensor(row(small, i)[:, 0:2 * STATE], bcw[0:R].rearrange("p a n -> p (a n)"),
                                bcr[0:R, 2:4, :].rearrange("p a n -> p (a n)"), ALU.add).then_inc(s["bn_ok"], 1)

            def step(n, b):
                statistics(n + 2, b)
                take_small(n - 1, 1 - b)
                tokenizer_norm(n + 2, b)
                norm_small(n - 1, 1 - b)
                mixer_norms(n + 2, b)

            steps(dve, step, 2, 1)

        @block.gpsimd
        def _(pool):
            g = nc.gpsimd
            half = c("neghalf")
            pool.wait_ge(s["wload"], 16 * 9)

            def step(n, b):
                if live(n + 2):
                    i = n + 2
                    r1, r2 = rs1[0:R, b:b + 1], rs2[0:R, b, :]
                    pool.wait_ge(s["var1_ok"], i + 1)
                    g.tensor_tensor(r1, r1, half, ALU.pow).then_inc(s["rs1_ok"], 1)
                if live(n - 1):
                    pool.wait_ge(s["ms_ok"], n)
                    g.tensor_tensor(ms[0:R, :], ms[0:R, :], half.to_broadcast([R, 2]), ALU.pow).then_inc(s["rms_ok"], 1)
                if live(n + 2):
                    pool.wait_ge(s["var3_ok"], i + 1)
                    g.tensor_tensor(r2, r2, half.to_broadcast([R, 2]), ALU.pow).then_inc(s["rs2_ok"], 1)
                    pool.wait_ge(s["ux_ok"], i + 1)
                    g.tensor_tensor(row(keep["hu"], i), hid[0:R, b, :], ux[0:R, b, 0, :], ALU.add).then_inc(s["hu_ok"], 1)

            steps(pool, step, 2, 1)

        @block.scalar
        def _(act):
            a = nc.scalar

            def step(n, b):
                if live(n + 1):
                    i, q = n + 1, 1 - b
                    act.wait_ge(s["xt_ps"], i + 1)
                    lag(act, s["proj_ok"], i, 2)
                    a.activation(xt[:, q, 0:2, :], tps[q][:, 0:2, :], ACT.Copy)
                    for k in range(KC):
                        last = a.activation(xt[:, q, 2 + k, :], tps[q][:, 2 + k, :], ACT.Identity, scale=ncol[:, 0, k:k + 1],
                                            bias=ncol[:, 1, k:k + 1])
                    last.then_inc(s["xt_ok"], 1)
                if live(n):
                    act.wait_ge(s["proj_ok"], n + 1)
                    a.activation(row(keep["xz"], n)[:, 0:INNER], XP, ACT.Silu)
                    a.activation(row(keep["xz"], n)[:, INNER:], ZP, ACT.Silu).then_inc(s["silu_ok"], 1)

            act.wait_ge(s["wload"], 16 * 9)
            steps(act, step, 1, 0)


def scan_coefficients(nc, ctx, sb, sems, ps, c, keep, small, head_rows):
    NH = NT * HEADS
    NA = NT * 2 * HALF
    hr = sb(ctx, "hr", [128, 3, HEADS])
    ea = sb(ctx, "ea", [128, HEADS])
    dtv = sb(ctx, "dtv", [128, NT, HEADS])
    ab = sb(ctx, "ab", [128, NT, HEADS])
    el = sb(ctx, "el", [128, NT, HEADS])
    cn = sb(ctx, "cn", [128, NT, HEADS])
    cx = sb(ctx, "cx", [128, NT, HEADS])
    dm = sb(ctx, "dm", [128, NT])
    th = sb(ctx, "th", [128, NT, HALF])
    ang = sb(ctx, "ang", [128, NT, 2, HALF])
    kf = sb(ctx, "kf", [128, NT, 2, HALF])
    ra = sb(ctx, "ra", [128, NT, HALF])
    rb = sb(ctx, "rb", [128, NT, HALF])
    rc = sb(ctx, "rc", [128, NT, HALF])
    rd = sb(ctx, "rd", [128, NT, HALF])
    bc = sb(ctx, "bc", [128, NT, STATE])
    gtt = sb(ctx, "gtt", [128, NT])
    s = sems("hload dchain abs_in abs_ok soft_ok sig_ok ea_ok cx_ok theta_ok phi_ok shift_ok ang_ok sin_ok pchain rotc_ok")
    phi = [ps[0:R, q, 0:NT // 2 * HALF].rearrange("p (t n) -> p t n", n=HALF) for q in range(2)]
    sh = ps[0:R, 2, 0:NH].rearrange("p (t n) -> p t n", n=HEADS)
    HT = NT // 2

    def r(t):
        return t[0:R]

    def over_tiles(ap, n):
        return ap.rearrange("p (o n) -> p o n", o=1).to_broadcast([R, NT, n])

    with nc.Block() as block:
        @block.sync
        def _(sp):
            sp.dma_start(hr[0:R], head_rows).then_inc(s["hload"], 16)

        @block.scalar
        def _(act):
            a = nc.scalar
            act.wait_ge(s["hload"], 16)
            a.activation(r(ea), hr[0:R, 0, :], ACT.Exp).then_inc(s["ea_ok"], 1)
            a.activation(r(el), small[0:R, :, 2 * STATE + HEADS:2 * STATE + 2 * HEADS], ACT.Exp, scale=-1.0).then_inc(s["sig_ok"], 1)
            act.wait_ge(s["abs_in"], 1)
            a.activation(r(ab), r(dtv), ACT.Abs).then_inc(s["abs_ok"], 1)
            act.wait_ge(s["abs_ok"], 1)
            a.activation(r(ab), r(ab), ACT.Exp, scale=-1.0).then_inc(s["abs_ok"], 1)
            act.wait_ge(s["abs_ok"], 2)
            a.activation(r(ab), r(ab), ACT.Ln, bias=1.0).then_inc(s["soft_ok"], 1)
            act.wait_ge(s["ang_ok"], 1)
            a.activation(r(ang), r(ang), ACT.Sin).then_inc(s["sin_ok"], 1)

        @block.tensor
        def _(pe):
            pe.wait_ge(s["theta_ok"], 1)
            for q in range(2):
                last = nc.tensor.matmul(phi[q], c("upto")[:, 0:R], th[0:R, q * HT:(q + 1) * HT, :], start=True, stop=True)
            last.then_inc(s["phi_ok"], 1)
            pe.wait_ge(s["cx_ok"], 1)
            nc.tensor.matmul(sh, c("shift")[:, 0:R], r(cx), start=True, stop=True).then_inc(s["shift_ok"], 1)

        @block.vector
        def _(dve):
            v = nc.vector
            n = [0]

            def link(ins):
                n[0] += 1
                ins.then_inc(s["dchain"], 1)
                dve.wait_ge(s["dchain"], n[0])

            dve.wait_ge(s["hload"], 16)
            v.tensor_tensor(r(dtv), small[0:R, :, 2 * STATE:2 * STATE + HEADS], over_tiles(hr[0:R, 1, :], HEADS), ALU.add).then_inc(s["abs_in"], 1)
            dve.wait_ge(s["sig_ok"], 1)
            link(v.tensor_scalar_add(r(el), r(el), 1.0))
            link(v.reciprocal(r(el), r(el)))
            dve.wait_ge(s["soft_ok"], 1)
            link(v.scalar_tensor_tensor(out=r(dtv), in0=r(dtv), scalar=0.0, in1=r(ab), op0=ALU.max, op1=ALU.add))
            link(v.reduce_sum(r(dm), r(dtv), AX.X))
            link(v.tensor_scalar(r(dm), r(dm), 1.0 / HEADS, None, ALU.mult))
            v.tensor_tensor(r(th), small[0:R, :, SMALL - HALF:SMALL], dm[0:R, :, None].to_broadcast([R, NT, HALF]), ALU.mult).then_inc(s["theta_ok"], 1)
            link(v.tensor_tensor(r(cn), r(dtv), r(el), ALU.mult))
            link(v.tensor_scalar(r(el), r(el), -1.0, 1.0, ALU.mult, ALU.add))
            v.tensor_tensor(r(cx), r(dtv), r(el), ALU.mult).then_inc(s["cx_ok"], 1)
            dve.wait_ge(s["ea_ok"], 1)
            link(v.tensor_tensor(r(keep["loga"]), r(dtv), over_tiles(r(ea), HEADS), ALU.mult))
            link(v.tensor_scalar(r(keep["loga"]), r(keep["loga"]), -1.0, None, ALU.mult))
            dve.wait_ge(s["phi_ok"], 1)
            for q in range(2):
                v.tensor_scalar_add(ang[0:R, q * HT:(q + 1) * HT, 0, :], phi[q], float(np.pi / 2))
                last = v.tensor_copy(ang[0:R, q * HT:(q + 1) * HT, 1, :], phi[q])
            link(last)
            link(v.tensor_scalar(r(kf), r(ang), 1.0 / TWO_PI, MAGIC, ALU.mult, ALU.add))
            link(v.tensor_scalar(r(kf), r(kf), MAGIC, None, ALU.subtract))
            for part in (PI_HI, PI_MD, PI_LO):
                link(v.scalar_tensor_tensor(out=ang[0:R].rearrange("p t a n -> p (t a n)"),
                                            in0=kf[0:R].rearrange("p t a n -> p (t a n)"), scalar=-part,
                                            in1=ang[0:R].rearrange("p t a n -> p (t a n)"), op0=ALU.mult, op1=ALU.add))
            v.tensor_scalar(r(ang), r(ang), PI_IN, -PI_IN, ALU.min, ALU.max).then_inc(s["ang_ok"], 1)
            dve.wait_ge(s["shift_ok"], 1)
            link(v.tensor_tensor(r(keep["coef"]), r(cn), sh, ALU.add))
            dve.wait_ge(s["sin_ok"], 1)
            re, im = small[0:R, :, 0:HALF], small[0:R, :, HALF:STATE]
            co, si = ang[0:R, :, 0, :], ang[0:R, :, 1, :]
            v.tensor_tensor(r(ra), re, co, ALU.mult)
            link(v.tensor_tensor(r(rb), im, si, ALU.mult))
            v.tensor_tensor(keep["rot"][0:R, :, 0, 0:HALF], r(ra), r(rb), ALU.subtract)
            v.tensor_tensor(r(kf)[:, :, 0, :], re, si, ALU.mult)
            link(v.tensor_tensor(r(kf)[:, :, 1, :], im, co, ALU.mult))
            link(v.tensor_tensor(keep["rot"][0:R, :, 0, HALF:STATE], r(kf)[:, :, 0, :], r(kf)[:, :, 1, :], ALU.add))
            dve.wait_ge(s["rotc_ok"], 1)
            link(v.tensor_tensor(r(bc), keep["rot"][0:R, :, 0, :], keep["rot"][0:R, :, 1, :], ALU.mult))
            link(v.reduce_sum(r(gtt), r(bc), AX.X))
            link(v.tensor_tensor(r(keep["diag"]), r(cn), gtt[0:R, :, None].to_broadcast([R, NT, HEADS]), ALU.mult))
            link(v.tensor_tensor(r(keep["diag"]), r(keep["diag"]), over_tiles(hr[0:R, 2, :], HEADS), ALU.add))

        @block.gpsimd
        def _(pool):
            g = nc.gpsimd
            pool.wait_ge(s["sin_ok"], 1)
            re, im = small[0:R, :, STATE:STATE + HALF], small[0:R, :, STATE + HALF:2 * STATE]
            co, si = ang[0:R, :, 0, :], ang[0:R, :, 1, :]
            g.tensor_tensor(r(rc), re, co, ALU.mult)
            g.tensor_tensor(r(rd), im, si, ALU.mult).then_inc(s["pchain"], 1)
            pool.wait_ge(s["pchain"], 1)
            g.tensor_tensor(keep["rot"][0:R, :, 1, 0:HALF], r(rc), r(rd), ALU.subtract).then_inc(s["pchain"], 1)
            pool.wait_ge(s["pchain"], 2)
            g.tensor_tensor(r(rc), re, si, ALU.mult)
            g.tensor_tensor(r(rd), im, co, ALU.mult).then_inc(s["pchain"], 1)
            pool.wait_ge(s["pchain"], 3)
            g.tensor_tensor(keep["rot"][0:R, :, 1, HALF:STATE], r(rc), r(rd), ALU.add).then_inc(s["rotc_ok"], 1)


def mix_tokens(nc, ctx, sb, sems, ps, c, keep, rec, logits, acc, w_out, w_gate):
    wo = sb(ctx, "wo", [128, YC, E])
    wg = sb(ctx, "wg", [128, KC, NE])
    rotb = sb(ctx, "rotb", [128, 2, 2, STATE])
    bct = sb(ctx, "bct", [STATE, 2, 2, R])
    gm = sb(ctx, "gm", [128, 2, R])
    la = sb(ctx, "la", [128, HEADS, L])
    dec = sb(ctx, "dec", [128, 2, HEADS, L])
    wm = sb(ctx, "wm", [128, 2, HEADS * R])
    xc = sb(ctx, "xc", [128, 2, INNER])
    xq = sb(ctx, "xq", [128, 2, INNER])
    yg = sb(ctx, "yg", [128, INNER])
    yt = sb(ctx, "yt", [128, YC, R])
    h1 = sb(ctx, "h1", [128, 2, E])
    xn = sb(ctx, "xn", [128, 2, E])
    xnt = sb(ctx, "xnt", [128, KC, R])
    st = sb(ctx, "st3", [128, 6])
    mv = sb(ctx, "mv3", [128, 2])
    rs = sb(ctx, "rs3", [128, 1])
    s = sems("passed_b w2load rot_ok bct_ps bct_ok g_ok gm_ok la_ok d_ok dec_ok wm_ok xc_ok xq_ok y_ok y1_ok yg_ok yt_ps yt_ok o_ok "
             "h1_ok st3_ok mv3_ok var4_ok rs3_ok xn_ok xnt_ps xnt_ok l_ok lg_ok h1_out0 h1_out1 xn_out0 xn_out1")
    YP = ps[0:R, 0, :]
    DP = ps[0:R, 1:3, 0:HEADS * L // 2]
    BP = ps[0:STATE, 3, 0:2 * R].rearrange("p (a r) -> p a r", a=2)
    GP, LP = ps[0:R, 4, 0:R], ps[0:R, 4, 128:128 + NE]
    TP = ps[:, 5, 0:YC * R].rearrange("p (a r) -> p a r", a=YC)
    OP = ps[0:R, 6, 0:E]
    XP = ps[:, 7, 0:KC * R].rearrange("p (a r) -> p a r", a=KC)
    h1_out, xn_out = [s["h1_out0"], s["h1_out1"]], [s["xn_out0"], s["xn_out1"]]
    AHEAD, BEHIND = 3, 2

    with nc.Block() as block:
        @block.sync
        def _(sp):
            sp.dma_start(wo[:], w_out).then_inc(s["w2load"], 16)
            sp.dma_start(wg[:], w_gate).then_inc(s["w2load"], 16)

            def store(i, b, rows=R):
                sp.wait_ge(s["h1_ok"], i + 1)
                sp.dma_start(acc[bass.ds(i * R, rows), :], h1[0:rows, b, :]).then_inc(h1_out[b], 16)
                sp.wait_ge(s["xn_ok"], i + 1)
                sp.dma_start(rec[bass.ds(i * R, rows), 0:E], xn[0:rows, b, :]).then_inc(xn_out[b], 16)
            store(0, 0)
            store(1, 1)
            pairs(sp, store, 2, NT - 2)
            store(NT - 2, 0)
            store(NT - 1, 1, LAST)
            for o in h1_out + xn_out:
                sp.wait_ge(o, 16 * (NT // 2))

        @block.tensor
        def _(pe):
            ident = c("ident", 128)[0:R, 0:R]

            def turn_bc(i, b):
                pe.wait_ge(s["rot_ok"], i + 1)
                lag(pe, s["bct_ok"], i, 1)
                settle(pe, s["passed_b"])
                for q in range(2):
                    last = nc.tensor.transpose(BP[:, q, :], rotb[0:R, b, q, :], ident)
                last.then_inc(s["bct_ps"], 1)

            def decays(i, b):
                pe.wait_ge(s["la_ok"], i + 1)
                lag(pe, s["dec_ok"], i, 1)
                for q in range(2):
                    last = nc.tensor.matmul(DP[:, q, :], c("after")[:, 0:R],
                                            la[0:R, q * 8:(q + 1) * 8, :].rearrange("p h l -> p (h l)"), start=True, stop=True)
                last.then_inc(s["d_ok"], 1)

            def scores(i, b):
                pe.wait_ge(s["bct_ok"], i + 1)
                lag(pe, s["gm_ok"], i, 1)
                lag(pe, s["lg_ok"], i, 5)
                nc.tensor.matmul(GP, bct[:, b, 0, :], bct[:, b, 1, :], start=True, stop=True).then_inc(s["g_ok"], 1)

            def scan(i, b):
                pe.wait_ge(s["wm_ok"], i + 1)
                pe.wait_ge(s["xc_ok"], i + 1)
                lag(pe, s["y1_ok"], i, 1)
                for h in range(HEADS):
                    last = nc.tensor.matmul(YP[:, h * HD:(h + 1) * HD], wm[0:R, b, h * R:(h + 1) * R],
                                            xc[0:R, b, h * HD:(h + 1) * HD], start=True, stop=True)
                last.then_inc(s["y_ok"], 1)

            def turn_y(i, b):
                pe.wait_ge(s["yg_ok"], i + 1)
                lag(pe, s["yt_ok"], i, 1)
                for k in range(YC):
                    last = nc.tensor.transpose(TP[:, k, :], yg[0:R, k * 128:(k + 1) * 128], ident)
                last.then_inc(s["yt_ps"], 1)

            def out_proj(i, b):
                pe.wait_ge(s["yt_ok"], i + 1)
                lag(pe, s["h1_ok"], i, 1)
                for k in range(YC):
                    last = nc.tensor.matmul(OP, yt[:, k, :], wo[:, k, :], start=(k == 0), stop=(k == YC - 1))
                last.then_inc(s["o_ok"], 1)

            def turn_x(i, b):
                pe.wait_ge(s["xn_ok"], i + 1)
                lag(pe, s["xnt_ok"], i, 1)
                for k in range(KC):
                    last = nc.tensor.transpose(XP[:, k, :], xn[0:R, b, k * 128:(k + 1) * 128], ident)
                last.then_inc(s["xnt_ps"], 1)

            def gate(i, b):
                pe.wait_ge(s["xnt_ok"], i + 1)
                lag(pe, s["lg_ok"], i, 1)
                if isinstance(i, int) and i + 4 >= NT:
                    pe.wait_ge(s["gm_ok"], NT)
                for k in range(KC):
                    last = nc.tensor.matmul(LP, xnt[:, k, :], wg[:, k, :], start=(k == 0), stop=(k == KC - 1))
                last.then_inc(s["l_ok"], 1)

            def step(n, b):
                for stage, i, q in ((turn_bc, n + 2, b), (decays, n + 2, b), (turn_y, n - 1, 1 - b), (turn_x, n - 2, b),
                                    (scan, n, b), (scores, n + 2, b), (out_proj, n - 1, 1 - b), (gate, n - 2, b)):
                    if live(i):
                        stage(i, q)

            pe.wait_ge(s["w2load"], 32)
            steps(pe, step, AHEAD, BEHIND)

        @block.scalar
        def _(act):
            a = nc.scalar

            def step(n, b):
                if live(n + 2):
                    i = n + 2
                    act.wait_ge(s["bct_ps"], i + 1)
                    lag(act, s["g_ok"], i, 2)
                    a.activation(bct[:, b, :, :], BP, ACT.Copy).then_inc(s["bct_ok"], 1)
                    act.wait_ge(s["d_ok"], i + 1)
                    lag(act, s["wm_ok"], i, 2)
                    a.activation(dec[0:R, b].rearrange("p (q h) l -> p q (h l)", q=2), DP, ACT.Exp).then_inc(s["dec_ok"], 1)
                if live(n - 1):
                    act.wait_ge(s["yt_ps"], n)
                    lag(act, s["o_ok"], n - 1, 1)
                    a.activation(yt[:], TP, ACT.Copy).then_inc(s["yt_ok"], 1)
                if live(n - 2):
                    act.wait_ge(s["xnt_ps"], n - 1)
                    lag(act, s["l_ok"], n - 2, 1)
                    a.activation(xnt[:], XP, ACT.Copy).then_inc(s["xnt_ok"], 1)

            steps(act, step, AHEAD, BEHIND)

        @block.vector
        def _(dve):
            v = nc.vector

            def weights(i, b):
                dve.wait_ge(s["g_ok"], i + 1)
                lag(dve, s["wm_ok"], i, 2)
                v.tensor_tensor(gm[0:R, b, :], GP, c("causal")[:, 0:R], ALU.mult).then_inc(s["gm_ok"], 1)
                dve.wait_ge(s["gm_ok"], i + 1)
                dve.wait_ge(s["dec_ok"], i + 1)
                lag(dve, s["y_ok"], i, 2)
                v.tensor_tensor(wm[0:R, b, :].rearrange("p (h g l) -> p h g l", h=HEADS, g=G3),
                                dec[0:R, b, :, None, :].to_broadcast([R, HEADS, G3, L]),
                                gm[0:R, b, None, :].rearrange("p o (g l) -> p o g l", g=G3).to_broadcast([R, HEADS, G3, L]),
                                ALU.mult).then_inc(s["wm_ok"], 1)

            def gated(i, b):
                dve.wait_ge(s["y_ok"], i + 1)
                dve.wait_ge(s["xq_ok"], i + 1)
                lag(dve, s["yt_ps"], i, 1)
                v.tensor_tensor(yg[0:R, :], YP, xq[0:R, b, :], ALU.add).then_inc(s["y1_ok"], 1)
                dve.wait_ge(s["y1_ok"], i + 1)
                v.tensor_tensor(yg[0:R, :], yg[0:R, :], row(keep["xz"], i)[:, INNER:], ALU.mult).then_inc(s["yg_ok"], 1)

            def residual(i, b):
                dve.wait_ge(s["o_ok"], i + 1)
                lag(dve, s["xn_ok"], i, 1)
                if not isinstance(i, int) or i >= 2:
                    dve.wait_ge(h1_out[b], 8 * (i - b))
                v.tensor_tensor(h1[0:R, b, :], OP, row(keep["hu"], i), ALU.add).then_inc(s["h1_ok"], 1)
                dve.wait_ge(s["h1_ok"], i + 1)
                v.bn_stats(st[0:R, :], h1[0:R, b, :]).then_inc(s["st3_ok"], 1)
                dve.wait_ge(s["st3_ok"], i + 1)
                settle(dve, s["passed_b"])
                v.bn_aggr(mv[0:R, :], st[0:R, :]).then_inc(s["mv3_ok"], 1)
                dve.wait_ge(s["mv3_ok"], i + 1)
                v.tensor_scalar_add(rs[0:R, :], mv[0:R, 1:2], 1e-5).then_inc(s["var4_ok"], 1)

            def take_logits(i, b):
                dve.wait_ge(s["l_ok"], i + 1)
                v.tensor_copy(row(logits, i), LP).then_inc(s["lg_ok"], 1)

            def expert_norm(i, b):
                dve.wait_ge(s["rs3_ok"], i + 1)
                lag(dve, s["xnt_ps"], i, 2)
                if not isinstance(i, int) or i >= 2:
                    dve.wait_ge(xn_out[b], 8 * (i - b))
                v.tensor_scalar(xn[0:R, b, :], h1[0:R, b, :], mv[0:R, 0:1], rs[0:R, :], ALU.subtract, ALU.mult).then_inc(s["xn_ok"], 1)

            def step(n, b):
                for stage, i, q in ((weights, n + 1, 1 - b), (gated, n, b), (residual, n - 1, 1 - b),
                                    (take_logits, n - 2, b), (expert_norm, n - 1, 1 - b)):
                    if live(i):
                        stage(i, q)

            steps(dve, step, AHEAD, BEHIND)

        @block.gpsimd
        def _(pool):
            g = nc.gpsimd

            def heads(ap):
                return ap.rearrange("p (h d) -> p h d", h=HEADS)

            def step(n, b):
                if live(n + 3):
                    i, q = n + 3, 1 - b
                    lag(pool, s["bct_ps"], i, 2)
                    g.tensor_copy(rotb[0:R, q].rearrange("p a n -> p (a n)"),
                                  row(keep["rot"][:].rearrange("p t a n -> p t (a n)"), i)).then_inc(s["rot_ok"], 1)
                    lag(pool, s["d_ok"], i, 1)
                    g.tensor_tensor(la[0:R], row(keep["loga"], i)[:, :, None].to_broadcast([R, HEADS, L]),
                                    c("step")[:, None, :].to_broadcast([R, HEADS, L]), ALU.mult).then_inc(s["la_ok"], 1)
                if live(n + 1):
                    i, q = n + 1, 1 - b
                    lag(pool, s["y_ok"], i, 2)
                    g.tensor_tensor(heads(xc[0:R, q, :]), heads(row(keep["xz"], i)[:, 0:INNER]),
                                    row(keep["coef"], i)[:, :, None].to_broadcast([R, HEADS, HD]), ALU.mult).then_inc(s["xc_ok"], 1)
                    lag(pool, s["y1_ok"], i, 2)
                    g.tensor_tensor(heads(xq[0:R, q, :]), heads(row(keep["xz"], i)[:, 0:INNER]),
                                    row(keep["diag"], i)[:, :, None].to_broadcast([R, HEADS, HD]), ALU.mult).then_inc(s["xq_ok"], 1)
                if live(n - 1):
                    pool.wait_ge(s["var4_ok"], n)
                    g.tensor_tensor(rs[0:R, :], rs[0:R, :], c("neghalf"), ALU.pow).then_inc(s["rs3_ok"], 1)

            steps(pool, step, AHEAD, BEHIND)


def route(nc, ctx, sb, sems, ps, c, logits, slot_row, tab, upto_e, onehot, rec, wts, wload, w_experts):
    mx = sb(ctx, "mx", [128, NT])
    pr = sb(ctx, "pr", [128, NT, NE])
    gt = sb(ctx, "gt", [128, NT, NE, NE])
    eq = sb(ctx, "eq", [128, NT, NE, NE])
    rank = sb(ctx, "rank", [128, NT, NE])
    comb = sb(ctx, "comb", [128, NT, NE])
    sel = sb(ctx, "sel", [128, NT, NE])
    tot = sb(ctx, "tot", [128, NE, NT])
    run_ = sb(ctx, "run_", [128, NE, NT])
    cmp_ = sb(ctx, "cmp_", [128, NE, TOK // 128])
    te = sb(ctx, "te", [128, NE])
    ti = sb(ctx, "ti", [128, NE])
    own = sb(ctx, "own", [128, NT, NE])
    whole = sb(ctx, "whole", [128, NT, NE])
    pk = sb(ctx, "pk", [128, NT, NE])
    lo = sb(ctx, "lo", [128, NT, 2])
    hi = sb(ctx, "hi", [128, NT, 2])
    in_tile = sb(ctx, "in_tile", [128, NT, 2, 128])
    of_tile = sb(ctx, "of_tile", [128, NT, 2, ST])
    sf = sb(ctx, "sf", [128, 2, ST])
    et = sb(ctx, "et", [128, ST, NE - 1])
    ef = sb(ctx, "ef", [128, 2, ST])
    s = sems("ls_ok ex_ok comb_ok sel_ok cnt_ok rchain lo_ok place_ok slot_ok comb_out")
    WP = ps[0:R, 0, 0:NT * NE].rearrange("p (t e) -> p t e", e=NE)
    TPS = ps[:, 1, 0:NT * NE].rearrange("p (t e) -> p e t", e=NE)
    SLOT = ps[:, 2, 0:ST]
    PARTS = 2
    TH = NT // PARTS

    def r(t):
        return t[0:R]

    with nc.Block() as block:
        @block.sync
        def _(sp):
            for e in range(SLOTS):
                sp.dma_start(wts[:, e, :], w_experts[e]).then_inc(wload["wdma"], 16)
                if e == 0:
                    sp.wait_ge(s["comb_ok"], 1)
                    sp.dma_start(rec[0:(NT - 1) * R, CW:RECW].rearrange("(t p) w -> p t w", p=R),
                                 comb[0:R, 0:NT - 1, :]).then_inc(s["comb_out"], 16)
                    sp.dma_start(rec[(NT - 1) * R:TOK, CW:RECW], comb[0:LAST, NT - 1, :]).then_inc(s["comb_out"], 16)
                sp.wait_ge(wload["wdma"], 16 * (e + 1))
                sp.sem_inc(wload["w_ready"], 1)
            sp.wait_ge(s["comb_out"], 32)

        @block.scalar
        def _(act):
            act.wait_ge(s["ls_ok"], 1)
            nc.scalar.activation(r(pr), r(pr), ACT.Exp).then_inc(s["ex_ok"], 1)

        @block.tensor
        def _(pe):
            pe.wait_ge(s["sel_ok"], 1)
            flat = sel[0:R].rearrange("p t e -> p (t e)")
            nc.tensor.matmul(ps[0:R, 0, 0:NT * NE], c("before")[:, 0:R], flat, start=True, stop=True)
            nc.tensor.matmul(ps[:, 1, 0:NT * NE], c("ones"), flat, start=True, stop=True).then_inc(s["cnt_ok"], 1)
            for h in range(PARTS):
                pe.wait_ge(s["place_ok"], h + 1)
                for t in range(h * TH, (h + 1) * TH):
                    for k in range(2):
                        last = nc.tensor.matmul(SLOT, in_tile[0:R, t, k, :], of_tile[0:R, t, k, :],
                                                start=(t == 0 and k == 0), stop=(t == NT - 1 and k == 1))
            last.then_inc(s["slot_ok"], 1)

        @block.vector
        def _(dve):
            v = nc.vector
            n = [0]

            def link(ins):
                n[0] += 1
                ins.then_inc(s["rchain"], 1)
                dve.wait_ge(s["rchain"], n[0])

            shape4 = [R, NT, NE, NE]
            link(v.reduce_max(r(mx), r(logits), AX.X))
            v.tensor_tensor(r(pr), r(logits), mx[0:R, :, None].to_broadcast([R, NT, NE]), ALU.subtract).then_inc(s["ls_ok"], 1)
            dve.wait_ge(s["ex_ok"], 1)
            link(v.reduce_sum(r(mx), r(pr), AX.X))
            link(v.reciprocal(r(mx), r(mx)))
            link(v.tensor_tensor(r(pr), r(pr), mx[0:R, :, None].to_broadcast([R, NT, NE]), ALU.mult))
            pj, pe_ = pr[0:R, :, None, :].to_broadcast(shape4), pr[0:R, :, :, None].to_broadcast(shape4)
            v.tensor_tensor(r(gt), pj, pe_, ALU.is_gt)
            link(v.tensor_tensor(r(eq), pj, pe_, ALU.is_equal))
            link(v.tensor_tensor(eq[0:R].rearrange("p t a b -> p t (a b)"), eq[0:R].rearrange("p t a b -> p t (a b)"),
                                 c("lower")[:, None, :].to_broadcast([R, NT, NE * NE]), ALU.mult))
            link(v.tensor_tensor(r(gt), r(gt), r(eq), ALU.add))
            link(v.reduce_sum(r(rank), r(gt), AX.X))
            link(v.tensor_scalar(r(comb), r(rank), 2.0, None, ALU.is_lt))
            v.tensor_tensor(r(sel), r(comb), c("valid")[:, :, None].to_broadcast([R, NT, NE]), ALU.mult).then_inc(s["sel_ok"], 1)
            dve.wait_ge(s["sel_ok"], 1)
            link(v.tensor_tensor(r(comb), r(comb), r(pr), ALU.mult))
            link(v.reduce_sum(r(mx), r(comb), AX.X))
            link(v.reciprocal(r(mx), r(mx)))
            v.tensor_tensor(r(comb), r(comb), mx[0:R, :, None].to_broadcast([R, NT, NE]), ALU.mult).then_inc(s["comb_ok"], 1)
            dve.wait_ge(s["cnt_ok"], 1)
            link(v.tensor_copy(tot[:], TPS))
            link(v.tensor_tensor_scan(run_[:].rearrange("p e t -> p (e t)"), c("carry", 128), tot[:].rearrange("p e t -> p (e t)"),
                                      0.0, ALU.mult, ALU.add))
            link(v.tensor_tensor(cmp_[:], run_[:, :, NT - 1:NT].to_broadcast([128, NE, TOK // 128]),
                                 c("by128", 128)[:, None, :].to_broadcast([128, NE, TOK // 128]), ALU.is_gt))
            link(v.reduce_sum(te[:], cmp_[:], AX.X))
            link(v.tensor_tensor_scan(ti[:], c("ones", 128)[:, 0:NE], te[:], 0.0, ALU.mult, ALU.add))
            v.tensor_copy(upto_e[:], ti[:])
            link(v.tensor_tensor(run_[:], run_[:], tot[:], ALU.subtract))
            link(v.tensor_tensor(te[:], ti[:], te[:], ALU.subtract))
            link(v.tensor_tensor(r(own), WP, run_[0:R].rearrange("p e t -> p t e"), ALU.add))
            link(v.tensor_scalar(r(whole), r(own), -63.5, 1.0 / 128, ALU.add, ALU.mult))
            link(v.tensor_scalar(r(whole), r(whole), MAGIC, MAGIC, ALU.add, ALU.subtract))
            link(v.scalar_tensor_tensor(out=r(own), in0=r(whole), scalar=-128.0, in1=r(own), op0=ALU.mult, op1=ALU.add))
            link(v.tensor_tensor(r(whole), r(whole), te[0:R, None, :].to_broadcast([R, NT, NE]), ALU.add))
            for k in range(2):
                for of, to in ((own, lo), (whole, hi)):
                    link(v.scalar_tensor_tensor(out=r(pk), in0=r(rank), scalar=float(k), in1=r(of), op0=ALU.is_equal, op1=ALU.mult))
                    link(v.reduce_sum(to[0:R, :, k], r(pk), AX.X))
            v.tensor_tensor(r(lo), r(lo), c("valid")[:, :, None].to_broadcast([R, NT, 2]), ALU.mult).then_inc(s["lo_ok"], 1)
            dve.wait_ge(s["lo_ok"], 1)
            link(v.tensor_tensor(r(hi), r(hi), c("far")[:, :, None].to_broadcast([R, NT, 2]), ALU.add))
            for h in range(PARTS):
                t = slice(h * TH, (h + 1) * TH)
                link(v.tensor_tensor(of_tile[0:R, t], hi[0:R, t, :, None].to_broadcast([R, TH, 2, ST]),
                                     c("tiles")[:, None, None, :].to_broadcast([R, TH, 2, ST]), ALU.is_equal))
                v.tensor_tensor(of_tile[0:R, t].rearrange("p t k s -> p t (k s)"), of_tile[0:R, t].rearrange("p t k s -> p t (k s)"),
                                c("rowid1")[:, t, None].to_broadcast([R, TH, 2 * ST]), ALU.mult)
                v.tensor_tensor(in_tile[0:R, t], lo[0:R, t, :, None].to_broadcast([R, TH, 2, 128]),
                                c("lanes")[:, None, None, :].to_broadcast([R, TH, 2, 128]), ALU.is_equal).then_inc(s["place_ok"], 1)
            link(v.tensor_tensor(et[:], c("tiles", 128)[:, :, None].to_broadcast([128, ST, NE - 1]),
                                 ti[:, None, 0:NE - 1].to_broadcast([128, ST, NE - 1]), ALU.is_ge))
            link(v.reduce_sum(ef[:, 0, :], et[:], AX.X))
            link(v.tensor_scalar(ef[:, 1, :], ef[:, 0, :], float(SLOTS), -float(SLOTS), ALU.is_ge, ALU.mult))
            link(v.tensor_tensor(ef[:, 1, :], ef[:, 1, :], ef[:, 0, :], ALU.add))
            v.tensor_copy(tab[:], ef[:])
            v.tensor_tensor(onehot[:], ef[:, 0, :, None].to_broadcast([128, ST, NE]),
                            c("experts", 128)[:, None, :].to_broadcast([128, ST, NE]), ALU.is_equal)
            dve.wait_ge(s["slot_ok"], 1)
            link(v.tensor_scalar(sf[:, 0, :], SLOT, 0.0, None, ALU.is_equal))
            link(v.scalar_tensor_tensor(out=sf[:, 1, :], in0=sf[:, 0, :], scalar=c("spare1", 128), in1=SLOT, op0=ALU.mult, op1=ALU.add))
            v.tensor_scalar(slot_row[:], sf[:, 1, :], -1.0, None, ALU.add)


def experts(nc, ctx, sb, sems, ps, c, slot_row, tab, upto_e, onehot, rec, acc, wts, wload, w_experts, out):
    xr = sb(ctx, "xr", [128, 2, RECW])
    xt = sb(ctx, "xt4", [128, 2, KC, 128])
    sg = sb(ctx, "sg", [128, 2, HFF])
    hh = sb(ctx, "hh", [128, 2, HFF])
    ht = sb(ctx, "ht", [128, 2, 4, 128])
    ys = sb(ctx, "ys", [128, 2, E])
    wj = sb(ctx, "wj", [128, NE])
    ws = sb(ctx, "ws", [128, 2])
    take = sb(ctx, "take", [128, 2], i32)
    give = sb(ctx, "give", [128, 2], i32)
    s = sems("passed_c take_ok rec0 rec1 xt4_ps xt4_ok gu_ok sg_ok hh_ok ht_ps ht_ok dn_ok wj_ok ws_ok ys_ok add0 add1 copied")
    recd, added = [s["rec0"], s["rec1"]], [s["add0"], s["add1"]]
    GUP = [[ps[:, 2 * q, :], ps[:, 2 * q + 1, :]] for q in range(2)]
    HT = [ps[:, 4 + q, :].rearrange("p (a r) -> p a r", a=4) for q in range(2)]
    YP = ps[:, 6, 0:E]
    XP = ps[:, 7, 0:KC * 128].rearrange("p (a r) -> p a r", a=KC)

    def each_tile(eng, step):
        step(0, 0, False, True)
        step(1, 1, True, True)
        pairs(eng, lambda i, b: step(i, b, True, True), 2, ST - 3)
        step(ST - 3, 0, True, True)
        step(ST - 2, 1, True, True)
        step(ST - 1, 0, True, False)

    def add_done(eng, t, b):
        if not isinstance(t, int) or t >= 2:
            eng.wait_ge(added[b], 8 * (t - b))

    with nc.Block() as block:
        @block.sync
        def _(sp):
            for e in range(SLOTS, NE):
                tiles = sp.value_load(upto_e[0:1, e - SLOTS:e - SLOTS + 1], min_val=0, max_val=ST)
                sp.wait_ge(s["dn_ok"], 2 * tiles + 1)
                sp.dma_start(wts[:, e % SLOTS, :], w_experts[e]).then_inc(wload["wdma"], 16)
                sp.wait_ge(wload["wdma"], 16 * (e + 1))
                sp.sem_inc(wload["w_ready"], 1)
            for q in range(2):
                sp.wait_ge(added[q], 16 * ((ST + 1 - q) // 2))
            sp.dma_start(out.rearrange("b l e -> (b l) e"), acc[0:TOK, :]).then_inc(s["copied"], 16)
            sp.wait_ge(s["copied"], 16)

        @block.gpsimd
        def _(pool):
            def record(t, b):
                pool.wait_ge(s["take_ok"], t + 1)
                settle(pool, s["passed_c"])
                nc.gpsimd.indirect_dma_start(
                    out=xr[:, b, :], out_offset=None, in_=rec,
                    in_offset=bass.IndirectOffsetOnAxis(ap=take[:, b:b + 1], axis=0)).then_inc(recd[b], 16)

            def step(i, b, before, more):
                if not isinstance(i, int) or i < ST - 2:
                    pool.wait_ge(s["ws_ok"], i + 1)
                    pool.wait_ge(s["xt4_ps"], i + 1)
                    record(i + 2, b)
                if before:
                    scatter(i - 1, 1 - b)

            def scatter(t, b):
                pool.wait_ge(s["ys_ok"], t + 1)
                if not isinstance(t, int) or t >= 1:
                    pool.wait_ge(added[1 - b], 8 * t if b == 0 else 8 * (t + 1))
                settle(pool, s["passed_c"])
                nc.gpsimd.indirect_dma_start(
                    out=acc, out_offset=bass.IndirectOffsetOnAxis(ap=give[:, b:b + 1], axis=0),
                    in_=ys[:, b, :], in_offset=None, compute_op=ALU.add).then_inc(added[b], 16)

            record(0, 0)
            record(1, 1)
            each_tile(pool, step)
            scatter(ST - 1, 0)

        @block.tensor
        def _(pe):
            ident = c("ident", 128)

            def features(t, b):
                pe.wait_ge(recd[b], 8 * (t + 2 - b))
                lag(pe, s["xt4_ok"], t, 1)
                for k in range(KC):
                    last = nc.tensor.transpose(XP[:, k, :], xr[:, b, k * 128:(k + 1) * 128], ident)
                last.then_inc(s["xt4_ps"], 1)

            def gate_up(i, b, q, place):
                if q == 0:
                    pe.wait_ge(s["xt4_ok"], i + 1)
                if not isinstance(i, int) or i >= 1:
                    pe.wait_ge(s["hh_ok"], 2 * i + q - 1)
                for k in range(KC):
                    for u in range(2):
                        at = OFF_GU + k * 2 * FF + u * FF + q * HFF
                        last = nc.tensor.matmul(GUP[q][u], xt[:, b, k, :], row(wts, place, 128)[:, at:at + HFF],
                                                start=(k == 0), stop=(k == KC - 1))
                last.then_inc(s["gu_ok"], 1)

            def turn(i, q):
                pe.wait_ge(s["hh_ok"], 2 * i + q + 1)
                if not isinstance(i, int) or i >= 1:
                    pe.wait_ge(s["ht_ok"], 2 * i + q - 1)
                for a in range(4):
                    last = nc.tensor.transpose(HT[q][:, a, :], hh[:, q, a * 128:(a + 1) * 128], ident)
                last.then_inc(s["ht_ps"], 1)

            def down(i, q, place):
                pe.wait_ge(s["ht_ok"], 2 * i + q + 1)
                if q == 0:
                    lag(pe, s["ys_ok"], i, 1)
                for a in range(4):
                    at = OFF_DN + (4 * q + a) * E
                    last = nc.tensor.matmul(YP, ht[:, q, a, :], row(wts, place, 128)[:, at:at + E],
                                            start=(q == 0 and a == 0), stop=(q == 1 and a == 3))
                last.then_inc(s["dn_ok"], 1)

            def place_of(t):
                return pe.value_load(tab[0:1, 1, bass.ds(t, 1)], min_val=0, max_val=SLOTS - 1)

            def step(i, b, before, more):
                place = place_of(i)
                expert = pe.value_load(tab[0:1, 0, bass.ds(i, 1)], min_val=0, max_val=NE - 1)
                pe.wait_ge(wload["w_ready"], expert + 1)
                gate_up(i, b, 0, place)
                if before:
                    last_place = place_of(i - 1)
                    turn(i - 1, 1)
                    down(i - 1, 0, last_place)
                gate_up(i, b, 1, place)
                if more:
                    features(i + 1, 1 - b)
                turn(i, 0)
                if before:
                    down(i - 1, 1, last_place)

            pe.sem_inc(s["dn_ok"], 1)
            features(0, 0)
            each_tile(pe, step)
            turn(ST - 1, 1)
            last_place = place_of(ST - 1)
            down(ST - 1, 0, last_place)
            down(ST - 1, 1, last_place)

        @block.scalar
        def _(act):
            a = nc.scalar

            def gate(i, q):
                act.wait_ge(s["gu_ok"], 2 * i + q + 1)
                if not isinstance(i, int) or i >= 1:
                    act.wait_ge(s["hh_ok"], 2 * i + q - 1)
                a.activation(sg[:, q, :], GUP[q][0], ACT.Silu).then_inc(s["sg_ok"], 1)

            def turned(i, q):
                act.wait_ge(s["ht_ps"], 2 * i + q + 1)
                if not isinstance(i, int) or i >= 1:
                    act.wait_ge(s["dn_ok"], 2 * i + q)
                a.activation(ht[:, q], HT[q], ACT.Copy).then_inc(s["ht_ok"], 1)

            def step(i, b, before, more):
                gate(i, 0)
                if before:
                    turned(i - 1, 1)
                gate(i, 1)
                turned(i, 0)

            each_tile(act, step)
            turned(ST - 1, 1)

        @block.vector
        def _(dve):
            v = nc.vector

            def features(t, b):
                dve.wait_ge(s["xt4_ps"], t + 1)
                if not isinstance(t, int) or t >= 2:
                    dve.wait_ge(s["gu_ok"], 2 * t - 2)
                v.tensor_copy(xt[:, b], XP).then_inc(s["xt4_ok"], 1)

            def gated(i, q):
                dve.wait_ge(s["sg_ok"], 2 * i + q + 1)
                if not isinstance(i, int) or i >= 1:
                    dve.wait_ge(s["ht_ps"], 2 * i + q - 1)
                v.tensor_tensor(hh[:, q, :], sg[:, q, :], GUP[q][1], ALU.mult).then_inc(s["hh_ok"], 1)

            def weights(t, b):
                dve.wait_ge(recd[b], 8 * (t + 2 - b))
                add_done(dve, t, b)
                v.tensor_tensor(wj[:], xr[:, b, CW:CW + NE], row(onehot, t, 128), ALU.mult).then_inc(s["wj_ok"], 1)
                dve.wait_ge(s["wj_ok"], t + 1)
                v.reduce_sum(ws[:, b:b + 1], wj[:], AX.X)
                v.tensor_copy(give[:, b:b + 1], slot_row[:, bass.ds(t, 1)]).then_inc(s["ws_ok"], 1)

            def result(t, b):
                dve.wait_ge(s["dn_ok"], 2 * t + 3)
                dve.wait_ge(s["ws_ok"], t + 1)
                v.tensor_scalar(ys[:, b, :], YP, ws[:, b:b + 1], None, ALU.mult).then_inc(s["ys_ok"], 1)

            def taking(t, b):
                if not isinstance(t, int) or t >= 2:
                    dve.wait_ge(recd[b], 8 * (t - b))
                v.tensor_copy(take[:, b:b + 1], slot_row[:, bass.ds(t, 1)]).then_inc(s["take_ok"], 1)

            def step(i, b, before, more):
                gated(i, 0)
                weights(i, b)
                if not isinstance(i, int) or i < ST - 2:
                    taking(i + 2, b)
                gated(i, 1)
                if more:
                    features(i + 1, 1 - b)
                if before:
                    result(i - 1, 1 - b)

            taking(0, 0)
            taking(1, 1)
            features(0, 0)
            each_tile(dve, step)
            result(ST - 1, 0)


def kernel(x, cls_tok, L0_tok_W, L0_tok_b, L0_tok_cls_token, L0_tok_pos_embedding, L0_tok_gamma, L0_tok_beta,
           L0_attn_norm_scale, L0_attn_norm_bias, L0_attn_in_proj_w, L0_attn_A_log, L0_attn_dt_bias,
           L0_attn_bcB_scale, L0_attn_bcC_scale, L0_attn_B_bias, L0_attn_C_bias, L0_attn_theta_w, L0_attn_D,
           L0_attn_out_proj_w, L0_ffn_gate_w, L0_ffn_gate_up_proj, L0_ffn_down_proj):
    import concourse.bacc as bacc
    from concourse.bass_utils import run_bass_kernel_spmd

    def f(a):
        return np.asarray(a)

    p = f(x).reshape(BATCH, CH, HP, PATCH, HP, PATCH).transpose(1, 3, 5, 0, 2, 4).reshape(D, BATCH, NP)
    full = np.zeros((D, NT * G3, L), p.dtype)
    full[:, :BATCH, 2:] = p
    patches = full.reshape(DC, 128, NT, R).transpose(2, 1, 0, 3).reshape(NT, 128, DC * R)
    pos = f(L0_tok_pos_embedding)[0]
    base_a = np.tile(np.concatenate([np.zeros_like(pos[:1]), pos], 0), (G3, 1))
    base_b = np.tile(np.concatenate([f(cls_tok)[0], f(L0_tok_cls_token)[0], np.broadcast_to(f(L0_tok_b), (NP, E))], 0), (G3, 1))
    gam = np.tile(np.concatenate([np.ones_like(pos[:1]), np.broadcast_to(f(L0_tok_gamma), (L - 1, E))], 0), (G3, 1))
    bet = np.tile(np.concatenate([np.zeros_like(pos[:1]), np.broadcast_to(f(L0_tok_beta), (L - 1, E))], 0), (G3, 1))

    def chunks(w):
        return w.reshape(-1, 128, w.shape[-1]).transpose(1, 0, 2)

    def spread(rows_):
        return np.broadcast_to(np.stack(rows_)[None], (R, len(rows_), rows_[0].shape[-1]))

    gu = f(L0_ffn_gate_up_proj).transpose(0, 2, 1).reshape(NE, KC, 128, 2 * FF).transpose(0, 2, 1, 3).reshape(NE, 128, -1)
    dn = f(L0_ffn_down_proj).transpose(0, 2, 1).reshape(NE, FC, 128, E).transpose(0, 2, 1, 3).reshape(NE, 128, -1)
    arrays = dict(
        patches=patches, base_a=base_a, base_b=base_b, gammas=gam, betas=bet,
        w_tok=chunks(f(L0_tok_W)), w_in=chunks(f(L0_attn_in_proj_w)), w_theta=chunks(f(L0_attn_theta_w)),
        norm_cols=np.stack([f(L0_attn_norm_scale).reshape(KC, 128).T, f(L0_attn_norm_bias).reshape(KC, 128).T], 1),
        head_rows=spread([f(L0_attn_A_log), f(L0_attn_dt_bias), f(L0_attn_D)]),
        bc_rows=spread([f(L0_attn_bcB_scale), f(L0_attn_bcC_scale), f(L0_attn_B_bias), f(L0_attn_C_bias)]),
        w_out=chunks(f(L0_attn_out_proj_w)), w_gate=chunks(f(L0_ffn_gate_w).T),
        w_experts=np.concatenate([gu, dn], 2), consts=CONSTS)
    nc = bacc.Bacc("TRN2", target_bir_lowering=False, num_devices=1)
    fed, args = {}, {}
    for name, a in arrays.items():
        fed["in_" + name] = np.ascontiguousarray(a)
        args[name] = nc.dram_tensor("in_" + name, a.shape, mybir.dt.from_np(a.dtype), kind="ExternalInput").ap()
    out = nc.dram_tensor("result", (BATCH, L, E), f32, kind="ExternalOutput").ap()
    program(nc, out=out, **args)
    return run_bass_kernel_spmd(nc, [fed], core_ids=[0]).results[0]["result"]
```

```python
import concourse.bass as bass
from concourse import mybir
from concourse.alu_op_type import AluOpType as ALU
from contextlib import ExitStack
import numpy as np

BATCH, CH, IMG, PATCH = 64, 3, 96, 16
E = 256
HP = IMG // PATCH
NP = HP * HP
D = CH * PATCH * PATCH
L = NP + 2
G3 = 3
R = G3 * L
NT = -(-BATCH // G3)
LAST = (BATCH - G3 * (NT - 1)) * L
TOK = BATCH * L
INNER, STATE, HEADS = 512, 64, 16
HD = INNER // HEADS
HALF = STATE // 2
SMALL = 2 * STATE + 2 * HEADS + HALF
PROJ = 2 * INNER + 2 * STATE + 2 * HEADS
DC, KC, YC = D // 128, E // 128, INNER // 128
NE, FF = 8, 1024
FC = FF // 128
HFF = FF // 2
ST = TOK * 2 // 128 + NE - 1
STP = ST + ST % 2
RECW = E + NE
CW = E
ACC = TOK + 128
WEXP = KC * 2 * FF + FC * E
TURNS = 12
EARLY = 1
SLOTS = 3
PIECES = 2 * NT
PIECE = -(-NE * WEXP // PIECES)
OFF_GU, OFF_DN = 0, KC * 2 * FF
PRODUCTS = [(0, 0), (0, 1), (1, 0)]

f32, i32, f32r = mybir.dt.float32, mybir.dt.int32, mybir.dt.float32r
ACT = mybir.ActivationFunctionType
AX = mybir.AxisListType
TWO_PI = 2.0 * np.pi
MAGIC = 1.5 * 2.0 ** 23
PI_HI = float(np.float32(6.28125))
PI_MD = float(np.float32(TWO_PI - 6.28125))
PI_LO = float(TWO_PI - 6.28125 - np.float32(TWO_PI - 6.28125))
PI_IN = 3.1415925

CONST = {}


def constants():
    k = np.arange(128)
    kk, ss = np.meshgrid(k, k, indexing="ij")
    same = (kk // L == ss // L) & (kk < R) & (ss < R)
    parts = [
        ("ident", np.eye(128)),
        ("causal", same & (kk < ss)),
        ("upto", same & (kk <= ss)),
        ("after", same & (kk > ss)),
        ("shift", same & (kk == ss + 1)),
        ("before", kk < ss),
        ("ones", np.ones((128, 128))),
        ("step", (k[:, None] % L) <= np.arange(L)[None, :]),
        ("early", np.broadcast_to(NE - np.arange(NE)[None, :], (128, NE))),
        ("normed", (k % L != 0)[:, None]),
        ("raw", (k % L == 0)[:, None]),
        ("valid", (np.arange(NT)[None, :] * R + k[:, None] < TOK)),
        ("far", (np.arange(NT)[None, :] * R + k[:, None] >= TOK) * -1000.0),
        ("rowid1", np.arange(NT)[None, :] * R + k[:, None] + 1),
        ("spare1", (TOK + k + 1)[:, None]),
        ("lanes", np.broadcast_to(k[None, :], (128, 128))),
        ("carry", np.broadcast_to((np.arange(NT) != 0)[None, None, :], (128, NE, NT)).reshape(128, -1)),
        ("carry8", np.broadcast_to((np.arange(NE) != 0)[None, :], (128, NE))),
        ("by128", np.broadcast_to(np.array([-1] + [128 * i for i in range(1, TOK // 128)])[None, :], (128, TOK // 128))),
        ("tiles", np.broadcast_to(np.arange(STP)[None, :], (128, STP))),
        ("experts", np.broadcast_to(np.arange(NE)[None, :], (128, NE))),
        ("neghalf", np.full((128, 1), -0.5)),
        ("eps5", np.full((128, 1), 1e-5)),
        ("eps6", np.full((128, 2), 1e-6)),
        ("halfpi", np.full((128, 1), np.pi / 2)),
    ]
    at = 0
    for name, a in parts:
        CONST[name] = (at, at + a.shape[1])
        at += a.shape[1]
    return np.concatenate([np.asarray(a, np.float32) for _, a in parts], 1)


CONSTS = constants()


def program(nc, patches, base_a, base_b, gammas, betas, w_tok, w_in, w_theta, norm_cols, head_rows,
            bc_rows, w_out, w_gate, w_experts, consts, out):
    rec = nc.dram_tensor("records", (ACC, RECW), f32, kind="Internal").ap()
    acc = nc.dram_tensor("accumulator", (ACC, E), f32, kind="Internal").ap()
    parts = [nc.dram_tensor("weights_" + n, (128, PIECES * PIECE), f32, kind="Internal").ap() for n in ("high", "low")]
    with ExitStack() as top:
        def sb(ctx, name, shape, dt=f32):
            return ctx.enter_context(nc.sbuf_tensor(name, shape, dt))

        def sems(names):
            return {n: top.enter_context(nc.semaphore(n)) for n in names.split()}

        ps = top.enter_context(nc.psum_tensor("ps", [128, 8, 512], f32))
        cst = sb(top, "cst", [128, CONSTS.shape[1]])
        slot_row = sb(top, "slot_row", [128, ST], i32)
        logits = sb(top, "logits", [128, NT, NE])
        tab = sb(top, "tab", [128, 2, ST], i32)
        upto_e = sb(top, "upto_e", [128, NE], i32)
        onehot = sb(top, "onehot", [128, ST, NE])

        def c(name, rows=R):
            a, b = CONST[name]
            return cst[0:rows, a:b]

        with ExitStack() as mid:
            keep = dict(
                xz=sb(mid, "xz", [128, NT, 2 * INNER]),
                rot=sb(mid, "rot", [128, NT, 2, STATE]), loga=sb(mid, "loga", [128, NT, HEADS]),
                coef=sb(mid, "coef", [128, NT, HEADS]), diag=sb(mid, "diag", [128, NT, HEADS]))
            cut = dict(sems("whole_in0 whole_in1 high_ok low_ok high_out0 high_out1 low_out0 low_out1"),
                       whole=sb(mid, "whole_piece", [128, 2, PIECE]), high=sb(mid, "high_piece", [128, 2, PIECE], f32r))
            with ExitStack() as first:
                small = sb(first, "small", [128, NT, SMALL])
                hr = sb(first, "hr", [128, 3, HEADS])
                with ExitStack() as ctx:
                    embed_and_project(nc, ctx, sb, sems, ps, cst, c, keep, small, cut, parts, w_experts, rec, acc, patches,
                                      base_a, base_b, gammas, betas, w_tok, w_in, w_theta, norm_cols, bc_rows, consts,
                                      hr, head_rows)
                with ExitStack() as ctx:
                    scan_coefficients(nc, ctx, sb, sems, ps, c, keep, small, hr)
            with ExitStack() as ctx:
                mix_tokens(nc, ctx, sb, sems, ps, c, keep, cut, parts, w_experts, rec, logits, acc, w_out, w_gate)
        with ExitStack() as ctx:
            wts = sb(ctx, "wts", [128, SLOTS, 2 * WEXP], f32r)
            wload = sems("wdma0 wdma1 w_ready")
            with ExitStack() as inner:
                route(nc, inner, sb, sems, ps, c, logits, slot_row, tab, upto_e, onehot, rec, wts, wload, parts)
            experts(nc, ctx, sb, sems, ps, c, slot_row, tab, upto_e, onehot, rec, acc, wts, wload, parts, out)


def lag(eng, sem, i, n):
    if not isinstance(i, int) or i >= n:
        eng.wait_ge(sem, i - n + 1)


def settle(eng, sem):
    eng.sem_inc(sem, 1)


def row(t, i, rows=R):
    return t[0:rows, bass.ds(i, 1), :].rearrange("p o n -> p (o n)")


def live(i):
    return not isinstance(i, int) or 0 <= i < NT


def steps(eng, step, ahead, behind):
    lo = (behind + 3) // 2 * 2
    hi = (NT - ahead) // 2 * 2
    for n in range(-ahead, lo):
        step(n, n % 2)
    pairs(eng, step, lo, hi)
    for n in range(hi, NT + behind):
        step(n, n % 2)


def pairs(eng, step, first, last):
    assert (last - first) % 2 == 0 and first % 2 == 0
    with eng.Fori(first // 2, last // 2) as j:
        step(2 * j, 0)
        step(2 * j + 1, 1)


def load_piece(sp, cut, w_experts, p, b):
    if not isinstance(p, int) or p >= 2:
        sp.wait_ge(cut[f"low_out{b}"], 8 * (p - b))
    sp.dma_start(cut["whole"][:, b, :], w_experts[:, bass.ds(p * PIECE, PIECE)]).then_inc(cut[f"whole_in{b}"], 16)


def store_piece(sp, cut, parts, p, b):
    sp.wait_ge(cut["high_ok"], p + 1)
    sp.dma_start(parts[0][:, bass.ds(p * PIECE, PIECE)], cut["high"][:, b, :].bitcast(f32)).then_inc(cut[f"high_out{b}"], 16)
    sp.wait_ge(cut["low_ok"], p + 1)
    sp.dma_start(parts[1][:, bass.ds(p * PIECE, PIECE)], cut["whole"][:, b, :]).then_inc(cut[f"low_out{b}"], 16)


def high_of_piece(nc, act, cut, p, b):
    act.wait_ge(cut[f"whole_in{b}"], 8 * (p + 2 - b))
    if not isinstance(p, int) or p >= 2:
        act.wait_ge(cut[f"high_out{b}"], 8 * (p - b))
    nc.scalar.activation(cut["high"][:, b, :], cut["whole"][:, b, :], ACT.Copy).then_inc(cut["high_ok"], 1)


def low_of_piece(engine, eng, cut, p, b):
    eng.wait_ge(cut["high_ok"], p + 1)
    engine.tensor_tensor(cut["whole"][:, b, :], cut["whole"][:, b, :], cut["high"][:, b, :].bitcast(f32),
                         ALU.subtract).then_inc(cut["low_ok"], 1)


def embed_and_project(nc, ctx, sb, sems, ps, cst, c, keep, small, cut, parts, w_experts, rec, acc, patches,
                      base_a, base_b, gammas, betas, w_tok, w_in, w_theta, norm_cols, bc_rows, consts,
                      hr, head_rows):
    pin = sb(ctx, "pin", [128, 2, DC * R])
    wt = sb(ctx, "wt", [128, DC, E])
    wi = sb(ctx, "wi", [128, KC, PROJ])
    wth = sb(ctx, "wth", [128, KC, HALF])
    base = sb(ctx, "base", [128, E])
    gam = sb(ctx, "gam", [128, E])
    bet = sb(ctx, "bet", [128, E])
    ncol = sb(ctx, "ncol", [128, 2, KC])
    bcr = sb(ctx, "bcr", [128, 4, STATE])
    pre = sb(ctx, "pre", [128, E])
    hid = sb(ctx, "hid", [128, 2, E])
    hu = sb(ctx, "hu", [128, 2, E])
    ux = sb(ctx, "ux", [128, 2, 2, E])
    xt = sb(ctx, "xt", [128, 2, 4, R])
    bcw = sb(ctx, "bcw", [128, 2, STATE])
    junk = sb(ctx, "junk", [128, 2, STATE])
    st = sb(ctx, "st", [128, 6])
    mv1 = sb(ctx, "mv1", [128, 2, 2])
    mv2 = sb(ctx, "mv2", [128, 2, 2])
    rs1 = sb(ctx, "rs1", [128, 2])
    rs2 = sb(ctx, "rs2", [128, 2, 2])
    rcp = sb(ctx, "rcp", [128, 1])
    ms = sb(ctx, "ms", [128, 2])
    empty = sb(ctx, "empty", [128, RECW])
    s = sems("passed_a rowload wload tokload base_ok patch0 patch1 embedded pre_ok st1 mv1_ok var1_ok mean1_ok rs1_ok m1 n1 n2 "
             "hid_ok st2 mv2_ok var2_ok rcp_ok var3_ok rs2_ok u_ok ux_ok xt_ps xt_ok proj_ok silu_ok small_ok bcw_ok "
             "ms_ok rms_ok bn0 bn_ok hu_ok hu_out0 hu_out1 empty0 empty_out")
    patch, hu_out = [s["patch0"], s["patch1"]], [s["hu_out0"], s["hu_out1"]]
    tok = [ps[0:R, b, 0:E] for b in range(2)]
    tps = [ps[:, 2 + b, 0:4 * R].rearrange("p (a r) -> p a r", a=4) for b in range(2)]
    XP, ZP, SP_ = ps[0:R, 4, :], ps[0:R, 5, :], ps[0:R, 6, 0:SMALL]

    with nc.Block() as block:
        @block.sync
        def _(sp):
            sp.dma_start(pin[:, 0, :], patches[0]).then_inc(patch[0], 16)
            sp.dma_start(wt[:], w_tok).then_inc(s["tokload"], 16)
            sp.dma_start(pin[:, 1, :], patches[1]).then_inc(patch[1], 16)
            for dst, src in ((base[0:R, :], base_a), (pre[0:R, :], base_b), (cst[:], consts), (gam[0:R, :], gammas),
                             (bet[0:R, :], betas), (ncol[:], norm_cols)):
                sp.dma_start(dst, src).then_inc(s["rowload"], 16)
            for dst, src in ((wi[:], w_in), (wth[:], w_theta), (bcr[0:R], bc_rows), (hr[0:R], head_rows)):
                sp.dma_start(dst, src).then_inc(s["wload"], 16)
            sp.wait_ge(s["empty0"], 1)
            sp.dma_start(rec[TOK:ACC, :], empty[:]).then_inc(s["empty_out"], 16)
            sp.dma_start(acc[TOK:ACC, :], empty[:, 0:E]).then_inc(s["empty_out"], 16)

            def store_hu(i, b):
                sp.wait_ge(s["hu_ok"], i + 1)
                rows = LAST if isinstance(i, int) and i == NT - 1 else R
                sp.dma_start(acc[bass.ds(i * R, rows), :], hu[0:rows, b, :]).then_inc(hu_out[b], 16)

            def step(n, b):
                if live(n + 1):
                    load_piece(sp, cut, w_experts, n + 1, 1 - b)
                if live(n + 4) and not (isinstance(n, int) and n + 4 < 2):
                    sp.wait_ge(s["embedded"], n + 3)
                    sp.dma_start(pin[:, b, :], patches[bass.ds(n + 4, 1)].rearrange("o p n -> p (o n)")).then_inc(patch[b], 16)
                if live(n):
                    store_hu(n, b)
                if live(n):
                    store_piece(sp, cut, parts, n, b)

            steps(sp, step, 4, 0)
            sp.wait_ge(s["empty_out"], 32)
            for o in hu_out:
                sp.wait_ge(o, 16 * (NT // 2))

        @block.tensor
        def _(pe):
            ident = c("ident", 128)[0:R, 0:R]

            def embed(i, b):
                pe.wait_ge(patch[b], 8 * (i + 2 - b))
                lag(pe, s["pre_ok"], i, 2)
                for k in range(DC):
                    last = nc.tensor.matmul(tok[b], pin[:, b, k * R:(k + 1) * R], wt[:, k, :],
                                            start=(k == 0), stop=(k == DC - 1))
                last.then_inc(s["embedded"], 1)

            def turn(i, b):
                if isinstance(i, int) and i == 0:
                    pe.wait_ge(s["rowload"], 16 * 6)
                pe.wait_ge(s["ux_ok"], i + 1)
                lag(pe, s["xt_ok"], i, 2)
                for a in range(4):
                    last = nc.tensor.transpose(tps[b][:, a, :], ux[0:R, b, a // 2, (a % 2) * 128:(a % 2) * 128 + 128], ident)
                last.then_inc(s["xt_ps"], 1)

            def step(n, b):
                if live(n + 2):
                    embed(n + 2, b)
                if live(n + 1):
                    turn(n + 1, 1 - b)
                if live(n):
                    pe.wait_ge(s["xt_ok"], n + 1)
                    lag(pe, s["silu_ok"], n, 1)
                    lag(pe, s["small_ok"], n, 1)
                    if isinstance(n, int) and n == 0:
                        pe.wait_ge(s["wload"], 16 * 4)
                    for k in range(KC):
                        x = xt[:, b, 2 + k, :]
                        first, end = k == 0, k == KC - 1
                        nc.tensor.matmul(XP, x, wi[:, k, 0:INNER], start=first, stop=end)
                        nc.tensor.matmul(ZP, x, wi[:, k, INNER:2 * INNER], start=first, stop=end)
                        nc.tensor.matmul(SP_[:, 0:SMALL - HALF], x, wi[:, k, 2 * INNER:], start=first, stop=end)
                    for k in range(KC):
                        last = nc.tensor.matmul(SP_[:, SMALL - HALF:], xt[:, b, k, :], wth[:, k, :], start=(k == 0),
                                                stop=(k == KC - 1))
                    last.then_inc(s["proj_ok"], 1)

            pe.wait_ge(s["tokload"], 16)
            steps(pe, step, 2, 0)

        @block.vector
        def _(dve):
            v = nc.vector
            v.memset(empty[:], 0.0).then_inc(s["empty0"], 1)
            dve.wait_ge(s["rowload"], 16 * 6)
            v.tensor_tensor(base[0:R, :], base[0:R, :], pre[0:R, :], ALU.add).then_inc(s["base_ok"], 1)
            dve.wait_ge(s["base_ok"], 1)

            def embed_sum(i, b):
                dve.wait_ge(s["embedded"], i + 1)
                lag(dve, s["n1"], i, 1)
                v.tensor_tensor(pre[0:R, :], tok[b], base[0:R, :], ALU.add).then_inc(s["pre_ok"], 1)

            def embed_stats(i, b):
                dve.wait_ge(s["pre_ok"], i + 1)
                v.bn_stats(st[0:R, :], pre[0:R, :]).then_inc(s["st1"], 1)

            def embed_mean(i, b):
                dve.wait_ge(s["st1"], i + 1)
                settle(dve, s["passed_a"])
                v.bn_aggr(mv1[0:R, b, :], st[0:R, :]).then_inc(s["mv1_ok"], 1)

            def embed_var(i, b):
                m1 = mv1[0:R, b, :]
                dve.wait_ge(s["mv1_ok"], i + 1)
                v.tensor_scalar_add(rs1[0:R, b:b + 1], m1[:, 1:2], 1e-5).then_inc(s["var1_ok"], 1)
                v.tensor_tensor(m1[:, 0:1], m1[:, 0:1], c("normed"), ALU.mult).then_inc(s["mean1_ok"], 1)

            def tokenizer_scale(i, b):
                r1 = rs1[0:R, b:b + 1]
                dve.wait_ge(s["rs1_ok"], i + 1)
                v.tensor_scalar(r1, r1, c("normed"), c("raw"), ALU.mult, ALU.add).then_inc(s["m1"], 1)

            def tokenizer_norm(i, b):
                h, m1, m2, r1 = hid[0:R, b, :], mv1[0:R, b, :], mv2[0:R, b, :], rs1[0:R, b:b + 1]
                dve.wait_ge(s["m1"], i + 1)
                lag(dve, s["hu_ok"], i, 2)
                v.tensor_scalar(h, pre[0:R, :], m1[:, 0:1], r1, ALU.subtract, ALU.mult).then_inc(s["n1"], 1)
                dve.wait_ge(s["n1"], i + 1)
                v.tensor_tensor(h, h, gam[0:R, :], ALU.mult).then_inc(s["n2"], 1)
                dve.wait_ge(s["n2"], i + 1)
                v.tensor_tensor(h, h, bet[0:R, :], ALU.add).then_inc(s["hid_ok"], 1)
                dve.wait_ge(s["hid_ok"], i + 1)
                v.bn_stats(st[0:R, :], h).then_inc(s["st2"], 1)
                dve.wait_ge(s["st2"], i + 1)
                settle(dve, s["passed_a"])
                v.bn_aggr(m2, st[0:R, :]).then_inc(s["mv2_ok"], 1)
                dve.wait_ge(s["mv2_ok"], i + 1)
                v.tensor_scalar_add(rs2[0:R, b, 0:1], m2[:, 1:2], 1e-5).then_inc(s["var2_ok"], 1)
                dve.wait_ge(s["var2_ok"], i + 1)
                v.reciprocal(rcp[0:R, :], rs2[0:R, b, 0:1]).then_inc(s["rcp_ok"], 1)
                dve.wait_ge(s["rcp_ok"], i + 1)
                v.tensor_scalar(rs2[0:R, b, 1:2], rcp[0:R, :], m2[:, 1:2], 1e-6, ALU.mult, ALU.add).then_inc(s["var3_ok"], 1)

            def layer_norm(i, b):
                dve.wait_ge(s["rs2_ok"], i + 1)
                lag(dve, s["xt_ps"], i, 2)
                v.tensor_scalar(ux[0:R, b, 0, :], hid[0:R, b, :], mv2[0:R, b, 0:1], rs2[0:R, b, 0:1], ALU.subtract,
                                ALU.mult).then_inc(s["u_ok"], 1)

            def mixer_norm(i, b):
                dve.wait_ge(s["u_ok"], i + 1)
                v.tensor_scalar(ux[0:R, b, 1, :], ux[0:R, b, 0, :], rs2[0:R, b, 1:2], None, ALU.mult).then_inc(s["ux_ok"], 1)

            def take_bc(i, b):
                dve.wait_ge(s["proj_ok"], i + 1)
                lag(dve, s["bn_ok"], i, 1)
                v.tensor_copy(bcw[0:R].rearrange("p a n -> p (a n)"), SP_[:, 0:2 * STATE]).then_inc(s["bcw_ok"], 1)

            def take_rest(i, b):
                v.tensor_copy(row(small, i)[:, 2 * STATE:], SP_[:, 2 * STATE:]).then_inc(s["small_ok"], 1)

            def mean_square(i, b, a):
                if a == 0:
                    dve.wait_ge(s["bcw_ok"], i + 1)
                last = v.tensor_tensor_reduce(out=junk[0:R, a, :], in0=bcw[0:R, a, :], in1=bcw[0:R, a, :], scale=1.0 / STATE,
                                              scalar=1e-6, op0=ALU.mult, op1=ALU.add, accum_out=ms[0:R, a:a + 1])
                if a == 1:
                    last.then_inc(s["ms_ok"], 1)

            def scale_bc(i, b):
                if isinstance(i, int) and i == 0:
                    dve.wait_ge(s["wload"], 16 * 4)
                dve.wait_ge(s["rms_ok"], i + 1)
                for a in range(2):
                    last = v.scalar_tensor_tensor(out=bcw[0:R, a, :], in0=bcw[0:R, a, :], scalar=ms[0:R, a:a + 1],
                                                  in1=bcr[0:R, a, :], op0=ALU.mult, op1=ALU.mult)
                last.then_inc(s["bn0"], 1)

            def shift_bc(i, b):
                dve.wait_ge(s["bn0"], i + 1)
                v.tensor_tensor(row(small, i)[:, 0:2 * STATE], bcw[0:R].rearrange("p a n -> p (a n)"),
                                bcr[0:R, 2:4, :].rearrange("p a n -> p (a n)"), ALU.add).then_inc(s["bn_ok"], 1)

            def step(n, b):
                new, out_ = (n + 2, b), (n - 1, 1 - b)
                is_new, is_next, is_out = live(n + 2), live(n + 1), live(n - 1)
                if is_out:
                    take_bc(*out_)
                if is_next:
                    layer_norm(n + 1, 1 - b)
                if is_out:
                    take_rest(*out_)
                    mean_square(*out_, 0)
                if is_next:
                    mixer_norm(n + 1, 1 - b)
                if is_out:
                    mean_square(*out_, 1)
                if is_new:
                    embed_sum(*new)
                    embed_stats(*new)
                    embed_mean(*new)
                    embed_var(*new)
                if is_out:
                    scale_bc(*out_)
                if is_new:
                    tokenizer_scale(*new)
                if is_out:
                    shift_bc(*out_)
                if is_new:
                    tokenizer_norm(*new)
                if live(n):
                    low_of_piece(v, dve, cut, n, b)

            steps(dve, step, 2, 1)

        @block.gpsimd
        def _(pool):
            g = nc.gpsimd
            half = c("neghalf")
            pool.wait_ge(s["rowload"], 16 * 6)

            def step(n, b):
                i, r1, r2 = n + 2, rs1[0:R, b:b + 1], rs2[0:R, b, :]
                if live(n - 1):
                    pool.wait_ge(s["ms_ok"], n)
                    g.tensor_tensor(ms[0:R, :], ms[0:R, :], half.to_broadcast([R, 2]), ALU.pow).then_inc(s["rms_ok"], 1)
                if live(i):
                    pool.wait_ge(s["var1_ok"], i + 1)
                    g.tensor_tensor(r1, r1, half, ALU.pow).then_inc(s["rs1_ok"], 1)
                if live(i):
                    pool.wait_ge(s["var3_ok"], i + 1)
                    g.tensor_tensor(r2, r2, half.to_broadcast([R, 2]), ALU.pow).then_inc(s["rs2_ok"], 1)
                if live(n + 1):
                    i, q = n + 1, 1 - b
                    pool.wait_ge(s["ux_ok"], i + 1)
                    if not isinstance(i, int) or i >= 2:
                        pool.wait_ge(hu_out[q], 8 * (i - q))
                    g.tensor_tensor(hu[0:R, q, :], hid[0:R, q, :], ux[0:R, q, 0, :], ALU.add).then_inc(s["hu_ok"], 1)

            steps(pool, step, 2, 1)

        @block.scalar
        def _(act):
            a = nc.scalar

            def step(n, b):
                if live(n + 1):
                    i, q = n + 1, 1 - b
                    act.wait_ge(s["xt_ps"], i + 1)
                    lag(act, s["proj_ok"], i, 2)
                    a.activation(xt[:, q, 0:2, :], tps[q][:, 0:2, :], ACT.Copy)
                    for k in range(KC):
                        last = a.activation(xt[:, q, 2 + k, :], tps[q][:, 2 + k, :], ACT.Identity, scale=ncol[:, 0, k:k + 1],
                                            bias=ncol[:, 1, k:k + 1])
                    last.then_inc(s["xt_ok"], 1)
                if live(n):
                    act.wait_ge(s["proj_ok"], n + 1)
                    a.activation(row(keep["xz"], n)[:, 0:INNER], XP, ACT.Silu)
                    a.activation(row(keep["xz"], n)[:, INNER:], ZP, ACT.Silu).then_inc(s["silu_ok"], 1)
                if live(n + 1):
                    high_of_piece(nc, act, cut, n + 1, 1 - b)

            act.wait_ge(s["rowload"], 16 * 6)
            steps(act, step, 1, 0)


def scan_coefficients(nc, ctx, sb, sems, ps, c, keep, small, hr):
    NH = NT * HEADS
    NA = NT * 2 * HALF
    ea = sb(ctx, "ea", [128, HEADS])
    dtv = sb(ctx, "dtv", [128, NT, HEADS])
    ab = sb(ctx, "ab", [128, NT, HEADS])
    el = sb(ctx, "el", [128, NT, HEADS])
    cn = sb(ctx, "cn", [128, NT, HEADS])
    cx = sb(ctx, "cx", [128, NT, HEADS])
    dm = sb(ctx, "dm", [128, NT])
    th = sb(ctx, "th", [128, NT, HALF])
    ang = sb(ctx, "ang", [128, NT, HALF])
    far = sb(ctx, "far", [128, NT, HALF])
    trig = sb(ctx, "trig", [128, 2, NT, HALF])
    kf = sb(ctx, "kf", [128, 2, NT, HALF])
    ra = sb(ctx, "ra", [128, NT, HALF])
    rb = sb(ctx, "rb", [128, NT, HALF])
    rc = sb(ctx, "rc", [128, NT, HALF])
    rd = sb(ctx, "rd", [128, NT, HALF])
    bc = sb(ctx, "bc", [128, NT, STATE])
    gtt = sb(ctx, "gtt", [128, NT])
    rest = sb(ctx, "rest", [128, NT, HEADS])
    s = sems("bc_ok dt_ok nea_ok dchain abs_in abs_ok soft_ok sig_ok ea_ok cx_ok theta_ok phi_ok shift_ok ang_ok far_ok sin_ok pchain")
    phi = [ps[0:R, q, 0:NT // 2 * HALF].rearrange("p (t n) -> p t n", n=HALF) for q in range(2)]
    PHI = ps[0:R, 0:2, 0:NT // 2 * HALF]
    sh = ps[0:R, 2, 0:NH].rearrange("p (t n) -> p t n", n=HEADS)
    HT = NT // 2

    def r(t):
        return t[0:R]

    def over_tiles(ap, n):
        return ap.rearrange("p (o n) -> p o n", o=1).to_broadcast([R, NT, n])

    with nc.Block() as block:
        @block.scalar
        def _(act):
            a = nc.scalar
            a.activation(r(ea), hr[0:R, 0, :], ACT.Exp).then_inc(s["ea_ok"], 1)
            a.activation(r(el), small[0:R, :, 2 * STATE + HEADS:2 * STATE + 2 * HEADS], ACT.Exp, scale=-1.0).then_inc(s["sig_ok"], 1)
            act.wait_ge(s["abs_in"], 1)
            a.activation(r(ab), r(dtv), ACT.Abs).then_inc(s["abs_ok"], 1)
            act.wait_ge(s["abs_ok"], 1)
            a.activation(r(ab), r(ab), ACT.Exp, scale=-1.0).then_inc(s["abs_ok"], 1)
            act.wait_ge(s["abs_ok"], 2)
            a.activation(r(ab), r(ab), ACT.Ln, bias=1.0).then_inc(s["soft_ok"], 1)
            act.wait_ge(s["ang_ok"], 1)
            a.activation(r(trig)[:, 1], r(ang), ACT.Sin)
            a.activation(r(far), r(ang), ACT.Abs).then_inc(s["far_ok"], 1)
            act.wait_ge(s["far_ok"], 1)
            a.activation(r(trig)[:, 0], r(far), ACT.Sin, scale=-1.0, bias=c("halfpi")).then_inc(s["sin_ok"], 1)

        @block.tensor
        def _(pe):
            pe.wait_ge(s["theta_ok"], 1)
            for q in range(2):
                last = nc.tensor.matmul(phi[q], c("upto")[:, 0:R], th[0:R, q * HT:(q + 1) * HT, :], start=True, stop=True)
            last.then_inc(s["phi_ok"], 1)
            pe.wait_ge(s["cx_ok"], 1)
            nc.tensor.matmul(sh, c("shift")[:, 0:R], r(cx), start=True, stop=True).then_inc(s["shift_ok"], 1)

        @block.vector
        def _(dve):
            v = nc.vector
            n = [0]

            def link(ins):
                n[0] += 1
                ins.then_inc(s["dchain"], 1)
                dve.wait_ge(s["dchain"], n[0])

            v.tensor_tensor(r(dtv), small[0:R, :, 2 * STATE:2 * STATE + HEADS], over_tiles(hr[0:R, 1, :], HEADS), ALU.add).then_inc(s["abs_in"], 1)
            dve.wait_ge(s["ea_ok"], 1)
            v.tensor_scalar(r(ea), r(ea), -1.0, None, ALU.mult).then_inc(s["nea_ok"], 1)
            dve.wait_ge(s["sig_ok"], 1)
            link(v.tensor_scalar_add(r(el), r(el), 1.0))
            link(v.reciprocal(r(el), r(el)))
            link(v.tensor_scalar(r(rest), r(el), -1.0, 1.0, ALU.mult, ALU.add))
            dve.wait_ge(s["soft_ok"], 1)
            v.scalar_tensor_tensor(out=r(dtv), in0=r(dtv), scalar=0.0, in1=r(ab), op0=ALU.max, op1=ALU.add).then_inc(s["dt_ok"], 1)
            dve.wait_ge(s["dt_ok"], 1)
            link(v.reduce_sum(r(dm), r(dtv), AX.X))
            v.scalar_tensor_tensor(out=r(th), in0=small[0:R, :, SMALL - HALF:SMALL], scalar=1.0 / HEADS,
                                   in1=dm[0:R, :, None].to_broadcast([R, NT, HALF]), op0=ALU.mult, op1=ALU.mult).then_inc(s["theta_ok"], 1)
            v.tensor_tensor(r(cx), r(dtv), r(rest), ALU.mult).then_inc(s["cx_ok"], 1)
            link(v.tensor_tensor(r(cn), r(dtv), r(el), ALU.mult))
            dve.wait_ge(s["phi_ok"], 1)
            turns = kf[0:R, 0].rearrange("p t n -> p (t n)")
            halves = turns.rearrange("p (q m) -> p q m", q=2)
            flat = ang[0:R].rearrange("p t n -> p (t n)")
            link(v.tensor_scalar(halves, PHI, 1.0 / TWO_PI, MAGIC, ALU.mult, ALU.add))
            link(v.tensor_scalar(turns, turns, MAGIC, None, ALU.subtract))
            link(v.scalar_tensor_tensor(out=flat.rearrange("p (q m) -> p q m", q=2), in0=halves, scalar=-PI_HI, in1=PHI,
                                        op0=ALU.mult, op1=ALU.add))
            for part in (PI_MD, PI_LO):
                link(v.scalar_tensor_tensor(out=flat, in0=turns, scalar=-part, in1=flat, op0=ALU.mult, op1=ALU.add))
            v.tensor_scalar(r(ang), r(ang), PI_IN, -PI_IN, ALU.min, ALU.max).then_inc(s["ang_ok"], 1)
            dve.wait_ge(s["shift_ok"], 1)
            link(v.tensor_tensor(r(keep["coef"]), r(cn), sh, ALU.add))
            dve.wait_ge(s["bc_ok"], 1)
            link(v.reduce_sum(r(gtt), r(bc), AX.X))
            link(v.tensor_tensor(r(keep["diag"]), r(cn), gtt[0:R, :, None].to_broadcast([R, NT, HEADS]), ALU.mult))
            link(v.tensor_tensor(r(keep["diag"]), r(keep["diag"]), over_tiles(hr[0:R, 2, :], HEADS), ALU.add))
            dve.wait_ge(s["sin_ok"], 1)
            re, im = small[0:R, :, 0:HALF], small[0:R, :, HALF:STATE]
            co, si = trig[0:R, 0], trig[0:R, 1]
            v.tensor_tensor(r(ra), re, co, ALU.mult)
            v.tensor_tensor(r(rb), im, si, ALU.mult)
            v.tensor_tensor(r(kf)[:, 0], re, si, ALU.mult)
            link(v.tensor_tensor(r(kf)[:, 1], im, co, ALU.mult))
            v.tensor_tensor(keep["rot"][0:R, :, 0, 0:HALF], r(ra), r(rb), ALU.subtract)
            link(v.tensor_tensor(keep["rot"][0:R, :, 0, HALF:STATE], r(kf)[:, 0], r(kf)[:, 1], ALU.add))
            re, im = small[0:R, :, STATE:STATE + HALF], small[0:R, :, STATE + HALF:2 * STATE]
            v.tensor_tensor(r(ra), re, si, ALU.mult)
            link(v.tensor_tensor(r(rb), im, co, ALU.mult))
            v.tensor_tensor(keep["rot"][0:R, :, 1, HALF:STATE], r(ra), r(rb), ALU.add)

        @block.gpsimd
        def _(pool):
            g = nc.gpsimd
            g.tensor_tensor(r(bc), small[0:R, :, 0:STATE], small[0:R, :, STATE:2 * STATE], ALU.mult).then_inc(s["bc_ok"], 1)
            pool.wait_ge(s["nea_ok"], 1)
            pool.wait_ge(s["dt_ok"], 1)
            g.tensor_tensor(r(keep["loga"]), r(dtv), over_tiles(r(ea), HEADS), ALU.mult)
            pool.wait_ge(s["sin_ok"], 1)
            re, im = small[0:R, :, STATE:STATE + HALF], small[0:R, :, STATE + HALF:2 * STATE]
            co, si = trig[0:R, 0], trig[0:R, 1]
            g.tensor_tensor(r(rc), re, co, ALU.mult)
            g.tensor_tensor(r(rd), im, si, ALU.mult).then_inc(s["pchain"], 1)
            pool.wait_ge(s["pchain"], 1)
            g.tensor_tensor(keep["rot"][0:R, :, 1, 0:HALF], r(rc), r(rd), ALU.subtract)


def mix_tokens(nc, ctx, sb, sems, ps, c, keep, cut, parts, w_experts, rec, logits, acc, w_out, w_gate):
    wo = sb(ctx, "wo", [128, YC, E])
    wg = sb(ctx, "wg", [128, KC, NE])
    rotb = sb(ctx, "rotb", [128, 2, 2, STATE])
    bct = sb(ctx, "bct", [STATE, 2, 2, R])
    gm = sb(ctx, "gm", [128, 2, R])
    la = sb(ctx, "la", [128, HEADS, L])
    dec = sb(ctx, "dec", [128, 2, HEADS, L])
    wm = sb(ctx, "wm", [128, 2, HEADS * R])
    xc = sb(ctx, "xc", [128, 2, INNER])
    xq = sb(ctx, "xq", [128, 2, INNER])
    yg = sb(ctx, "yg", [128, 2, INNER])
    yt = sb(ctx, "yt", [128, YC, R])
    hu = sb(ctx, "hu3", [128, 2, E])
    h1 = sb(ctx, "h1", [128, 2, E])
    xn = sb(ctx, "xn", [128, 2, E])
    xnt = sb(ctx, "xnt", [128, KC, R])
    st = sb(ctx, "st3", [128, 6])
    mv = sb(ctx, "mv3", [128, 2])
    rs = sb(ctx, "rs3", [128, 1])
    s = sems("passed_b w2load rot_ok bct_ps bct_ok g_ok gm_ok la_ok d_ok dec_ok wm_ok xc_ok xq_ok y_ok y1_ok yg_ok yt_ps yt_ok o_ok "
             "h1_ok st3_ok mv3_ok var4_ok rs3_ok xn_ok xnt_ps xnt_ok l_ok lg_ok h1_out0 h1_out1 xn_out0 xn_out1 hu_in0 hu_in1")
    YP = ps[0:R, 0, :]
    DP = ps[0:R, 1:3, 0:HEADS * L // 2]
    BP = ps[0:STATE, 3, 0:2 * R].rearrange("p (a r) -> p a r", a=2)
    GP, LP = ps[0:R, 4, 0:R], ps[0:R, 4, 128:128 + NE]
    TP = ps[:, 5, 0:YC * R].rearrange("p (a r) -> p a r", a=YC)
    OP = ps[0:R, 6, 0:E]
    XP = ps[:, 7, 0:KC * R].rearrange("p (a r) -> p a r", a=KC)
    h1_out, xn_out = [s["h1_out0"], s["h1_out1"]], [s["xn_out0"], s["xn_out1"]]
    hu_in = [s["hu_in0"], s["hu_in1"]]
    AHEAD, BEHIND = 3, 3

    with nc.Block() as block:
        @block.sync
        def _(sp):
            sp.dma_start(wo[:], w_out).then_inc(s["w2load"], 16)
            sp.dma_start(wg[:], w_gate).then_inc(s["w2load"], 16)

            def load_hu(i, b):
                lag(sp, s["h1_ok"], i, 2)
                rows = LAST if isinstance(i, int) and i == NT - 1 else R
                sp.dma_start(hu[0:rows, b, :], acc[bass.ds(i * R, rows), :]).then_inc(hu_in[b], 16)

            def store(i, b):
                rows = LAST if isinstance(i, int) and i == NT - 1 else R
                sp.wait_ge(s["h1_ok"], i + 1)
                sp.dma_start(acc[bass.ds(i * R, rows), :], h1[0:rows, b, :]).then_inc(h1_out[b], 16)
                sp.wait_ge(s["xn_ok"], i + 1)
                sp.dma_start(rec[bass.ds(i * R, rows), 0:E], xn[0:rows, b, :]).then_inc(xn_out[b], 16)

            def step(n, b):
                if live(n + 1):
                    load_piece(sp, cut, w_experts, NT + n + 1, 1 - b)
                if live(n - 1):
                    load_hu(n - 1, 1 - b)
                if live(n - 3):
                    store(n - 3, 1 - b)
                if live(n):
                    store_piece(sp, cut, parts, NT + n, b)

            steps(sp, step, 1, 3)
            for o in h1_out + xn_out:
                sp.wait_ge(o, 16 * (NT // 2))
            for o in ("high_out0", "high_out1", "low_out0", "low_out1"):
                sp.wait_ge(cut[o], 16 * NT)

        @block.tensor
        def _(pe):
            ident = c("ident", 128)[0:R, 0:R]

            def turn_bc(i, b):
                pe.wait_ge(s["rot_ok"], i + 1)
                lag(pe, s["bct_ok"], i, 1)
                settle(pe, s["passed_b"])
                for q in range(2):
                    last = nc.tensor.transpose(BP[:, q, :], rotb[0:R, b, q, :], ident)
                last.then_inc(s["bct_ps"], 1)

            def decays(i, b):
                pe.wait_ge(s["la_ok"], i + 1)
                lag(pe, s["dec_ok"], i, 1)
                for q in range(2):
                    last = nc.tensor.matmul(DP[:, q, :], c("after")[:, 0:R],
                                            la[0:R, q * 8:(q + 1) * 8, :].rearrange("p h l -> p (h l)"), start=True, stop=True)
                last.then_inc(s["d_ok"], 1)

            def scores(i, b):
                pe.wait_ge(s["bct_ok"], i + 1)
                lag(pe, s["gm_ok"], i, 1)
                lag(pe, s["lg_ok"], i, 6)
                nc.tensor.matmul(GP, bct[:, b, 0, :], bct[:, b, 1, :], start=True, stop=True).then_inc(s["g_ok"], 1)

            def turn_y(i, b):
                pe.wait_ge(s["yg_ok"], i + 1)
                lag(pe, s["yt_ok"], i, 1)
                for k in range(YC):
                    last = nc.tensor.transpose(TP[:, k, :], yg[0:R, b, k * 128:(k + 1) * 128], ident)
                last.then_inc(s["yt_ps"], 1)

            def scan_and_out_proj(n, b):
                if live(n):
                    pe.wait_ge(s["wm_ok"], n + 1)
                    pe.wait_ge(s["xc_ok"], n + 1)
                    lag(pe, s["y1_ok"], n, 1)
                if isinstance(n, int) and n == 2:
                    pe.wait_ge(s["w2load"], 32)
                if live(n - 2):
                    pe.wait_ge(s["yt_ok"], n - 1)
                    lag(pe, s["h1_ok"], n - 2, 1)
                for k in range(YC):
                    if live(n - 2):
                        last_o = nc.tensor.matmul(OP, yt[:, k, :], wo[:, k, :], start=(k == 0), stop=(k == YC - 1))
                    if live(n):
                        for h in range(k * HEADS // YC, (k + 1) * HEADS // YC):
                            last = nc.tensor.matmul(YP[:, h * HD:(h + 1) * HD], wm[0:R, b, h * R:(h + 1) * R],
                                                    xc[0:R, b, h * HD:(h + 1) * HD], start=True, stop=True)
                if live(n - 2):
                    last_o.then_inc(s["o_ok"], 1)
                if live(n):
                    last.then_inc(s["y_ok"], 1)

            def turn_x(i, b):
                pe.wait_ge(s["xn_ok"], i + 1)
                lag(pe, s["xnt_ok"], i, 1)
                for k in range(KC):
                    last = nc.tensor.transpose(XP[:, k, :], xn[0:R, b, k * 128:(k + 1) * 128], ident)
                last.then_inc(s["xnt_ps"], 1)

            def gate(i, b):
                pe.wait_ge(s["xnt_ok"], i + 1)
                lag(pe, s["lg_ok"], i, 1)
                if isinstance(i, int) and i + 5 >= NT:
                    pe.wait_ge(s["gm_ok"], NT)
                for k in range(KC):
                    last = nc.tensor.matmul(LP, xnt[:, k, :], wg[:, k, :], start=(k == 0), stop=(k == KC - 1))
                last.then_inc(s["l_ok"], 1)

            def step(n, b):
                if live(n + 2):
                    turn_bc(n + 2, b)
                    decays(n + 2, b)
                scan_and_out_proj(n, b)
                if live(n - 3):
                    turn_x(n - 3, 1 - b)
                if live(n - 1):
                    turn_y(n - 1, 1 - b)
                if live(n + 2):
                    scores(n + 2, b)
                if live(n - 3):
                    gate(n - 3, 1 - b)

            steps(pe, step, AHEAD, BEHIND)

        @block.scalar
        def _(act):
            a = nc.scalar

            def step(n, b):
                if live(n + 2):
                    i = n + 2
                    act.wait_ge(s["bct_ps"], i + 1)
                    lag(act, s["g_ok"], i, 2)
                    a.activation(bct[:, b, :, :], BP, ACT.Copy).then_inc(s["bct_ok"], 1)
                    act.wait_ge(s["d_ok"], i + 1)
                    lag(act, s["wm_ok"], i, 2)
                    a.activation(dec[0:R, b].rearrange("p (q h) l -> p q (h l)", q=2), DP, ACT.Exp).then_inc(s["dec_ok"], 1)
                if live(n - 3):
                    act.wait_ge(s["xnt_ps"], n - 2)
                    lag(act, s["l_ok"], n - 3, 1)
                    a.activation(xnt[:], XP, ACT.Copy).then_inc(s["xnt_ok"], 1)
                if live(n - 1):
                    act.wait_ge(s["yt_ps"], n)
                    lag(act, s["o_ok"], n - 1, 1)
                    a.activation(yt[:], TP, ACT.Copy).then_inc(s["yt_ok"], 1)
                if live(n + 1):
                    high_of_piece(nc, act, cut, NT + n + 1, 1 - b)

            steps(act, step, AHEAD, BEHIND)

        @block.vector
        def _(dve):
            v = nc.vector

            def weights(i, b):
                dve.wait_ge(s["g_ok"], i + 1)
                lag(dve, s["wm_ok"], i, 2)
                v.tensor_tensor(gm[0:R, b, :], GP, c("causal")[:, 0:R], ALU.mult).then_inc(s["gm_ok"], 1)
                dve.wait_ge(s["gm_ok"], i + 1)
                dve.wait_ge(s["dec_ok"], i + 1)
                lag(dve, s["y_ok"], i, 2)
                v.tensor_tensor(wm[0:R, b, :].rearrange("p (h g l) -> p h g l", h=HEADS, g=G3),
                                dec[0:R, b, :, None, :].to_broadcast([R, HEADS, G3, L]),
                                gm[0:R, b, None, :].rearrange("p o (g l) -> p o g l", g=G3).to_broadcast([R, HEADS, G3, L]),
                                ALU.mult).then_inc(s["wm_ok"], 1)

            def gated(i, b):
                dve.wait_ge(s["y_ok"], i + 1)
                dve.wait_ge(s["xq_ok"], i + 1)
                lag(dve, s["yt_ps"], i, 2)
                v.tensor_tensor(yg[0:R, b, :], YP, xq[0:R, b, :], ALU.add).then_inc(s["y1_ok"], 1)
                dve.wait_ge(s["y1_ok"], i + 1)
                v.tensor_tensor(yg[0:R, b, :], yg[0:R, b, :], row(keep["xz"], i)[:, INNER:], ALU.mult).then_inc(s["yg_ok"], 1)

            def low_part(i, b):
                low_of_piece(v, dve, cut, NT + i, b)

            def residual(i, b):
                dve.wait_ge(s["o_ok"], i + 1)
                dve.wait_ge(hu_in[b], 8 * (i + 2 - b))
                lag(dve, s["xn_ok"], i, 1)
                if not isinstance(i, int) or i >= 2:
                    dve.wait_ge(h1_out[b], 8 * (i - b))
                v.tensor_tensor(h1[0:R, b, :], OP, hu[0:R, b, :], ALU.add).then_inc(s["h1_ok"], 1)
                dve.wait_ge(s["h1_ok"], i + 1)
                v.bn_stats(st[0:R, :], h1[0:R, b, :]).then_inc(s["st3_ok"], 1)
                dve.wait_ge(s["st3_ok"], i + 1)
                settle(dve, s["passed_b"])
                v.bn_aggr(mv[0:R, :], st[0:R, :]).then_inc(s["mv3_ok"], 1)
                dve.wait_ge(s["mv3_ok"], i + 1)
                v.tensor_scalar_add(rs[0:R, :], mv[0:R, 1:2], 1e-5).then_inc(s["var4_ok"], 1)

            def take_logits(i, b):
                dve.wait_ge(s["l_ok"], i + 1)
                v.tensor_copy(row(logits, i), LP).then_inc(s["lg_ok"], 1)

            def expert_norm(i, b):
                dve.wait_ge(s["rs3_ok"], i + 1)
                lag(dve, s["xnt_ps"], i, 2)
                if not isinstance(i, int) or i >= 2:
                    dve.wait_ge(xn_out[b], 8 * (i - b))
                v.tensor_scalar(xn[0:R, b, :], h1[0:R, b, :], mv[0:R, 0:1], rs[0:R, :], ALU.subtract, ALU.mult).then_inc(s["xn_ok"], 1)

            def step(n, b):
                for stage, i, q in ((weights, n + 1, 1 - b), (low_part, n, b), (residual, n - 2, b), (gated, n, b),
                                    (take_logits, n - 3, 1 - b), (expert_norm, n - 2, b)):
                    if live(i):
                        stage(i, q)

            steps(dve, step, AHEAD, BEHIND)

        @block.gpsimd
        def _(pool):
            g = nc.gpsimd

            def heads(ap):
                return ap.rearrange("p (h d) -> p h d", h=HEADS)

            def step(n, b):
                if live(n + 3):
                    i, q = n + 3, 1 - b
                    lag(pool, s["bct_ps"], i, 2)
                    g.tensor_copy(rotb[0:R, q].rearrange("p a n -> p (a n)"),
                                  row(keep["rot"][:].rearrange("p t a n -> p t (a n)"), i)).then_inc(s["rot_ok"], 1)
                    lag(pool, s["d_ok"], i, 1)
                    g.tensor_tensor(la[0:R], row(keep["loga"], i)[:, :, None].to_broadcast([R, HEADS, L]),
                                    c("step")[:, None, :].to_broadcast([R, HEADS, L]), ALU.mult).then_inc(s["la_ok"], 1)
                if live(n + 1):
                    i, q = n + 1, 1 - b
                    lag(pool, s["y_ok"], i, 2)
                    g.tensor_tensor(heads(xc[0:R, q, :]), heads(row(keep["xz"], i)[:, 0:INNER]),
                                    row(keep["coef"], i)[:, :, None].to_broadcast([R, HEADS, HD]), ALU.mult).then_inc(s["xc_ok"], 1)
                    lag(pool, s["y1_ok"], i, 2)
                    g.tensor_tensor(heads(xq[0:R, q, :]), heads(row(keep["xz"], i)[:, 0:INNER]),
                                    row(keep["diag"], i)[:, :, None].to_broadcast([R, HEADS, HD]), ALU.mult).then_inc(s["xq_ok"], 1)
                if live(n - 2):
                    pool.wait_ge(s["var4_ok"], n - 1)
                    g.tensor_tensor(rs[0:R, :], rs[0:R, :], c("neghalf"), ALU.pow).then_inc(s["rs3_ok"], 1)

            steps(pool, step, AHEAD, BEHIND)


def load_expert(sp, wts, wload, parts, e):
    for turn in range(TURNS):
        part, at = divmod(turn * 2 * WEXP // TURNS, WEXP)
        upto = at + 2 * WEXP // TURNS
        if turn > 1:
            sp.wait_ge(wload[f"wdma{turn % 2}"], 8 * (e * TURNS + turn - turn % 2))
        sp.dma_start(wts[:, e % SLOTS, part * WEXP + at:part * WEXP + upto].bitcast(f32),
                     parts[part][:, e * WEXP + at:e * WEXP + upto]).then_inc(wload[f"wdma{turn % 2}"], 16)
    for k in range(2):
        sp.wait_ge(wload[f"wdma{k}"], 8 * TURNS * (e + 1))
    sp.sem_inc(wload["w_ready"], 1)


def route(nc, ctx, sb, sems, ps, c, logits, slot_row, tab, upto_e, onehot, rec, wts, wload, parts):
    mx = sb(ctx, "mx", [128, NT])
    pr = sb(ctx, "pr", [128, NT, NE])
    others = sb(ctx, "others", [128, NT, NE])
    eq = sb(ctx, "eq", [128, NT, NE])
    top = sb(ctx, "top", [128, 2, NT, NE])
    comb = sb(ctx, "comb", [128, NT, NE])
    sel = sb(ctx, "sel", [128, NT, NE])
    tot = sb(ctx, "tot", [128, NE, NT])
    run_ = sb(ctx, "run_", [128, NE, NT])
    cmp_ = sb(ctx, "cmp_", [128, NE, TOK // 128])
    te = sb(ctx, "te", [128, NE])
    ti = sb(ctx, "ti", [128, NE])
    place = sb(ctx, "place", [128, 2, NT, NE])
    pk = sb(ctx, "pk", [128, 2, 2, NT, NE])
    slot = sb(ctx, "slot", [128, 2, 2, NT])
    spare = wts[:, SLOTS - 1, :]
    A, B = NT * 2 * 128, NT * 2 * (128 + STP)
    in_tile = spare[:, 0:A].rearrange("p (t k n) -> p t k n", t=NT, k=2)
    of_tile = spare[:, A:B].rearrange("p (t k n) -> p t k n", t=NT, k=2)
    sf = sb(ctx, "sf", [128, 2, ST])
    fold = sb(ctx, "fold", [128, ST])
    et = sb(ctx, "et", [128, ST, NE - 1])
    ef = sb(ctx, "ef", [128, 2, ST])
    s = sems("ls_ok ex_ok comb_ok sel_ok cnt_ok rchain place_ok slot_ok comb_out")
    WP = ps[0:R, 0, 0:NT * NE].rearrange("p (t e) -> p t e", e=NE)
    TPS = ps[:, 1, 0:NT * NE].rearrange("p (t e) -> p e t", e=NE)
    SLOT = ps[:, 2, 0:ST]
    SLOTP = ps[:, 2, 0:STP]
    PARTS = 2
    TH = NT // PARTS

    def r(t):
        return t[0:R]

    with nc.Block() as block:
        @block.sync
        def _(sp):
            for e in range(EARLY):
                load_expert(sp, wts, wload, parts, e)
                if e == 0:
                    sp.wait_ge(s["comb_ok"], 1)
                    sp.dma_start(rec[0:(NT - 1) * R, CW:RECW].rearrange("(t p) w -> p t w", p=R),
                                 comb[0:R, 0:NT - 1, :]).then_inc(s["comb_out"], 16)
                    sp.dma_start(rec[(NT - 1) * R:TOK, CW:RECW], comb[0:LAST, NT - 1, :]).then_inc(s["comb_out"], 16)
            sp.wait_ge(s["comb_out"], 32)

        @block.scalar
        def _(act):
            act.wait_ge(s["ls_ok"], 1)
            nc.scalar.activation(r(pr), r(pr), ACT.Exp).then_inc(s["ex_ok"], 1)

        @block.tensor
        def _(pe):
            pe.wait_ge(s["sel_ok"], 1)
            flat = sel[0:R].rearrange("p t e -> p (t e)")
            nc.tensor.matmul(ps[0:R, 0, 0:NT * NE], c("before")[:, 0:R], flat, start=True, stop=True)
            nc.tensor.matmul(ps[:, 1, 0:NT * NE], c("ones"), flat, start=True, stop=True).then_inc(s["cnt_ok"], 1)
            for h in range(PARTS):
                pe.wait_ge(s["place_ok"], h + 1)
                for t in range(h * TH, (h + 1) * TH):
                    for k in range(2):
                        last = nc.tensor.matmul(SLOTP, in_tile[0:R, t, k, :], of_tile[0:R, t, k, :],
                                                start=(t == 0 and k == 0), stop=(t == NT - 1 and k == 1))
            last.then_inc(s["slot_ok"], 1)

        @block.vector
        def _(dve):
            v = nc.vector
            n = [0]

            def link(ins):
                n[0] += 1
                ins.then_inc(s["rchain"], 1)
                dve.wait_ge(s["rchain"], n[0])

            link(v.reduce_max(r(mx), r(logits), AX.X))
            v.tensor_tensor(r(pr), r(logits), mx[0:R, :, None].to_broadcast([R, NT, NE]), ALU.subtract).then_inc(s["ls_ok"], 1)
            dve.wait_ge(s["ex_ok"], 1)
            link(v.reduce_sum(r(mx), r(pr), AX.X))
            link(v.reciprocal(r(mx), r(mx)))
            link(v.tensor_tensor(r(pr), r(pr), mx[0:R, :, None].to_broadcast([R, NT, NE]), ALU.mult))
            early = c("early")[:, None, :].to_broadcast([R, NT, NE])
            for k, probs in ((0, pr), (1, others)):
                if k == 1:
                    link(v.scalar_tensor_tensor(out=r(others), in0=r(top)[:, 0], scalar=-2.0, in1=r(pr), op0=ALU.mult, op1=ALU.add))
                link(v.reduce_max(r(mx), r(probs), AX.X))
                link(v.tensor_tensor(r(eq), r(probs), mx[0:R, :, None].to_broadcast([R, NT, NE]), ALU.is_equal))
                link(v.tensor_tensor(r(eq), r(eq), early, ALU.mult))
                link(v.reduce_max(r(mx), r(eq), AX.X))
                link(v.tensor_tensor(r(top)[:, k], early, mx[0:R, :, None].to_broadcast([R, NT, NE]), ALU.is_equal))
            link(v.tensor_tensor(r(comb), r(top)[:, 0], r(top)[:, 1], ALU.add))
            v.tensor_tensor(r(sel), r(comb), c("valid")[:, :, None].to_broadcast([R, NT, NE]), ALU.mult).then_inc(s["sel_ok"], 1)
            dve.wait_ge(s["sel_ok"], 1)
            link(v.tensor_tensor(r(comb), r(comb), r(pr), ALU.mult))
            link(v.reduce_sum(r(mx), r(comb), AX.X))
            link(v.reciprocal(r(mx), r(mx)))
            v.tensor_tensor(r(comb), r(comb), mx[0:R, :, None].to_broadcast([R, NT, NE]), ALU.mult).then_inc(s["comb_ok"], 1)
            dve.wait_ge(s["cnt_ok"], 1)
            link(v.tensor_copy(tot[:], TPS))
            link(v.tensor_tensor_scan(run_[:].rearrange("p e t -> p (e t)"), c("carry", 128), tot[:].rearrange("p e t -> p (e t)"),
                                      0.0, ALU.mult, ALU.add))
            link(v.tensor_tensor(cmp_[:], run_[:, :, NT - 1:NT].to_broadcast([128, NE, TOK // 128]),
                                 c("by128", 128)[:, None, :].to_broadcast([128, NE, TOK // 128]), ALU.is_gt))
            link(v.reduce_sum(te[:], cmp_[:], AX.X))
            link(v.tensor_tensor_scan(ti[:], c("ones", 128)[:, 0:NE], te[:], 0.0, ALU.mult, ALU.add))
            v.tensor_copy(upto_e[:], ti[:])
            link(v.tensor_tensor(run_[:], run_[:], tot[:], ALU.subtract))
            link(v.tensor_tensor(te[:], ti[:], te[:], ALU.subtract))
            own, whole = place[:, 0], place[:, 1]
            link(v.tensor_tensor(r(own), WP, run_[0:R].rearrange("p e t -> p t e"), ALU.add))
            link(v.tensor_scalar(r(whole), r(own), -63.5, 1.0 / 128, ALU.add, ALU.mult))
            link(v.tensor_scalar(r(whole), r(whole), MAGIC, MAGIC, ALU.add, ALU.subtract))
            link(v.scalar_tensor_tensor(out=r(own), in0=r(whole), scalar=-128.0, in1=r(own), op0=ALU.mult, op1=ALU.add))
            link(v.tensor_tensor(r(whole), r(whole), te[0:R, None, :].to_broadcast([R, NT, NE]), ALU.add))
            def flat(ap):
                return ap.rearrange("p w t e -> p w (t e)")

            for k in range(2):
                last = v.tensor_tensor(flat(pk[0:R, k]), flat(top[0:R, k:k + 1]).to_broadcast([R, 2, NT * NE]), flat(r(place)), ALU.mult)
            link(last)
            link(v.reduce_sum(slot[0:R].rearrange("p k w t -> p (k w t)"), pk[0:R].rearrange("p k w t e -> p (k w t) e"), AX.X))
            lo, hi = slot[0:R, :, 0].rearrange("p k t -> p t k"), slot[0:R, :, 1].rearrange("p k t -> p t k")
            link(v.tensor_tensor(hi, hi, c("far")[:, :, None].to_broadcast([R, NT, 2]), ALU.add))
            for h in range(PARTS):
                t = slice(h * TH, (h + 1) * TH)
                link(v.tensor_tensor(of_tile[0:R, t], hi[:, t, :, None].to_broadcast([R, TH, 2, STP]),
                                     c("tiles")[:, None, None, :].to_broadcast([R, TH, 2, STP]), ALU.is_equal))
                v.tensor_tensor(of_tile[0:R, t].rearrange("p t k s -> p t (k s)"),
                                of_tile[0:R, t].bitcast(f32).rearrange("p t k s -> p t (k s)"),
                                c("rowid1")[:, t, None].to_broadcast([R, TH, 2 * STP]), ALU.mult)
                v.tensor_tensor(in_tile[0:R, t], lo[:, t, :, None].to_broadcast([R, TH, 2, 128]),
                                c("lanes")[:, None, None, :].to_broadcast([R, TH, 2, 128]), ALU.is_equal).then_inc(s["place_ok"], 1)
            link(v.tensor_tensor(et[:], c("tiles", 128)[:, 0:ST, None].to_broadcast([128, ST, NE - 1]),
                                 ti[:, None, 0:NE - 1].to_broadcast([128, ST, NE - 1]), ALU.is_ge))
            link(v.reduce_sum(ef[:, 0, :], et[:], AX.X))
            link(v.tensor_copy(ef[:, 1, :], ef[:, 0, :]))
            for first in range(SLOTS, NE, SLOTS):
                link(v.tensor_scalar(fold[:], ef[:, 0, :], float(first), -float(SLOTS), ALU.is_ge, ALU.mult))
                link(v.tensor_tensor(ef[:, 1, :], ef[:, 1, :], fold[:], ALU.add))
            v.tensor_copy(tab[:], ef[:])
            v.tensor_tensor(onehot[:], ef[:, 0, :, None].to_broadcast([128, ST, NE]),
                            c("experts", 128)[:, None, :].to_broadcast([128, ST, NE]), ALU.is_equal)
            dve.wait_ge(s["slot_ok"], 1)
            link(v.tensor_scalar(sf[:, 0, :], SLOT, 0.0, None, ALU.is_equal))
            link(v.scalar_tensor_tensor(out=sf[:, 1, :], in0=sf[:, 0, :], scalar=c("spare1", 128), in1=SLOT, op0=ALU.mult, op1=ALU.add))
            v.tensor_scalar(slot_row[:], sf[:, 1, :], -1.0, None, ALU.add)


def experts(nc, ctx, sb, sems, ps, c, slot_row, tab, upto_e, onehot, rec, acc, wts, wload, parts, out):
    xr = sb(ctx, "xr", [128, 2, RECW])
    xt = sb(ctx, "xt4", [128, 2, 2, KC, 128], f32r)
    sg = sb(ctx, "sg", [128, 2, HFF])
    hh = sb(ctx, "hh", [128, 2, HFF])
    ht = sb(ctx, "ht", [128, 2, 2, 4, 128], f32r)
    ys = sb(ctx, "ys", [128, 2, E])
    wj = sb(ctx, "wj", [128, NE])
    ws = sb(ctx, "ws", [128, 2])
    take = sb(ctx, "take", [128, 2], i32)
    give = sb(ctx, "give", [128, 2], i32)
    s = sems("passed_c take_ok rec0 rec1 xt4_ps xhigh_ok xt4_ok gu_ok sg_ok hh_ok ht_ps hhigh_ok ht_ok dn_ok wj_ok ws_ok ys_ok add0 add1 copied")
    recd, added = [s["rec0"], s["rec1"]], [s["add0"], s["add1"]]
    GUP = [[ps[:, 2 * q, :], ps[:, 2 * q + 1, :]] for q in range(2)]
    HT = [ps[:, 4 + q, :].rearrange("p (a r) -> p a r", a=4) for q in range(2)]
    YP = ps[:, 6, 0:E]
    XP = ps[:, 7, 0:KC * 128].rearrange("p (a r) -> p a r", a=KC)

    def each_tile(eng, step):
        step(0, 0, False, True)
        step(1, 1, True, True)
        pairs(eng, lambda i, b: step(i, b, True, True), 2, ST - 3)
        step(ST - 3, 0, True, True)
        step(ST - 2, 1, True, True)
        step(ST - 1, 0, True, False)

    def add_done(eng, t, b):
        if not isinstance(t, int) or t >= 2:
            eng.wait_ge(added[b], 8 * (t - b))

    with nc.Block() as block:
        @block.sync
        def _(sp):
            for e in range(EARLY, NE):
                if e >= SLOTS:
                    tiles = sp.value_load(upto_e[0:1, e - SLOTS:e - SLOTS + 1], min_val=0, max_val=ST)
                    sp.wait_ge(s["dn_ok"], 2 * tiles + 1)
                load_expert(sp, wts, wload, parts, e)
            for q in range(2):
                sp.wait_ge(added[q], 16 * ((ST + 1 - q) // 2))
            sp.dma_start(out.rearrange("b l e -> (b l) e"), acc[0:TOK, :]).then_inc(s["copied"], 16)
            sp.wait_ge(s["copied"], 16)

        @block.gpsimd
        def _(pool):
            def record(t, b):
                pool.wait_ge(s["take_ok"], t + 1)
                settle(pool, s["passed_c"])
                nc.gpsimd.indirect_dma_start(
                    out=xr[:, b, :], out_offset=None, in_=rec,
                    in_offset=bass.IndirectOffsetOnAxis(ap=take[:, b:b + 1], axis=0)).then_inc(recd[b], 16)

            def step(i, b, before, more):
                if not isinstance(i, int) or i < ST - 2:
                    pool.wait_ge(s["ws_ok"], i + 1)
                    pool.wait_ge(s["xt4_ps"], i + 1)
                    record(i + 2, b)
                if before:
                    scatter(i - 1, 1 - b)

            def scatter(t, b):
                pool.wait_ge(s["ys_ok"], t + 1)
                if not isinstance(t, int) or t >= 1:
                    pool.wait_ge(added[1 - b], 8 * t if b == 0 else 8 * (t + 1))
                settle(pool, s["passed_c"])
                nc.gpsimd.indirect_dma_start(
                    out=acc, out_offset=bass.IndirectOffsetOnAxis(ap=give[:, b:b + 1], axis=0),
                    in_=ys[:, b, :], in_offset=None, compute_op=ALU.add).then_inc(added[b], 16)

            record(0, 0)
            record(1, 1)
            each_tile(pool, step)
            scatter(ST - 1, 0)

        @block.tensor
        def _(pe):
            ident = c("ident", 128)

            def features(t, b):
                pe.wait_ge(recd[b], 8 * (t + 2 - b))
                lag(pe, s["xt4_ok"], t, 1)
                for k in range(KC):
                    last = nc.tensor.transpose(XP[:, k, :], xr[:, b, k * 128:(k + 1) * 128], ident)
                last.then_inc(s["xt4_ps"], 1)

            def gate_up(i, b, q, place):
                if q == 0:
                    pe.wait_ge(s["xt4_ok"], i + 1)
                for k in range(KC):
                    for x, w in PRODUCTS:
                        for u in range(2):
                            at = w * WEXP + OFF_GU + k * 2 * FF + u * FF + q * HFF
                            last = nc.tensor.matmul(GUP[q][u], xt[:, b, x, k, :], row(wts, place, 128)[:, at:at + HFF],
                                                    start=(k == 0 and (x, w) == PRODUCTS[0]),
                                                    stop=(k == KC - 1 and (x, w) == PRODUCTS[-1]))
                last.then_inc(s["gu_ok"], 1)

            def turn(i, q):
                pe.wait_ge(s["hh_ok"], 2 * i + q + 1)
                for a in range(4):
                    last = nc.tensor.transpose(HT[q][:, a, :], hh[:, q, a * 128:(a + 1) * 128], ident)
                last.then_inc(s["ht_ps"], 1)

            def down(i, q, place):
                pe.wait_ge(s["ht_ok"], 2 * i + q + 1)
                if q == 0:
                    lag(pe, s["ys_ok"], i, 1)
                for a in range(4):
                    for x, w in PRODUCTS:
                        at = w * WEXP + OFF_DN + (4 * q + a) * E
                        last = nc.tensor.matmul(YP, ht[:, q, x, a, :], row(wts, place, 128)[:, at:at + E],
                                                start=(q == 0 and a == 0 and (x, w) == PRODUCTS[0]),
                                                stop=(q == 1 and a == 3 and (x, w) == PRODUCTS[-1]))
                last.then_inc(s["dn_ok"], 1)

            def place_of(t):
                return pe.value_load(tab[0:1, 1, bass.ds(t, 1)], min_val=0, max_val=SLOTS - 1)

            def look_up(t):
                place = place_of(t)
                expert = pe.value_load(tab[0:1, 0, bass.ds(t, 1)], min_val=0, max_val=NE - 1)
                pe.wait_ge(wload["w_ready"], expert + 1)
                return place

            def step(i, b, before, more):
                held[b] = place = look_up(i) if b == 0 else held[1]
                gate_up(i, b, 0, place)
                if before:
                    last_place = place_of(i - 1) if b == 0 else held[0]
                    turn(i - 1, 1)
                    down(i - 1, 0, last_place)
                gate_up(i, b, 1, place)
                if more:
                    features(i + 1, 1 - b)
                    if b == 0:
                        held[1] = look_up(i + 1)
                turn(i, 0)
                if before:
                    down(i - 1, 1, last_place)

            held = {}
            pe.sem_inc(s["dn_ok"], 1)
            features(0, 0)
            each_tile(pe, step)
            turn(ST - 1, 1)
            last_place = place_of(ST - 1)
            down(ST - 1, 0, last_place)
            down(ST - 1, 1, last_place)

        @block.scalar
        def _(act):
            a = nc.scalar

            def gate(i, q):
                act.wait_ge(s["gu_ok"], 2 * i + q + 1)
                if not isinstance(i, int) or i >= 1:
                    act.wait_ge(s["hh_ok"], 2 * i + q - 1)
                a.activation(sg[:, q, :], GUP[q][0], ACT.Silu).then_inc(s["sg_ok"], 1)

            def turned(i, q):
                act.wait_ge(s["ht_ps"], 2 * i + q + 1)
                if not isinstance(i, int) or i >= 1:
                    act.wait_ge(s["dn_ok"], 2 * i + q)
                a.activation(ht[:, q, 0], HT[q], ACT.Copy).then_inc(s["hhigh_ok"], 1)

            def features(t, b):
                act.wait_ge(s["xt4_ps"], t + 1)
                if not isinstance(t, int) or t >= 2:
                    act.wait_ge(s["gu_ok"], 2 * t - 2)
                a.activation(xt[:, b, 0], XP, ACT.Copy).then_inc(s["xhigh_ok"], 1)

            def step(i, b, before, more):
                gate(i, 0)
                if before:
                    turned(i - 1, 1)
                gate(i, 1)
                if more:
                    features(i + 1, 1 - b)
                turned(i, 0)

            features(0, 0)
            each_tile(act, step)
            turned(ST - 1, 1)

        @block.vector
        def _(dve):
            v = nc.vector

            def features(t, b):
                dve.wait_ge(s["xhigh_ok"], t + 1)
                v.tensor_tensor(xt[:, b, 1], XP, xt[:, b, 0].bitcast(f32), ALU.subtract).then_inc(s["xt4_ok"], 1)

            def turned(i, q):
                dve.wait_ge(s["hhigh_ok"], 2 * i + q + 1)
                v.tensor_tensor(ht[:, q, 1], HT[q], ht[:, q, 0].bitcast(f32), ALU.subtract).then_inc(s["ht_ok"], 1)

            def gated(i, q):
                dve.wait_ge(s["sg_ok"], 2 * i + q + 1)
                if not isinstance(i, int) or i >= 1:
                    dve.wait_ge(s["ht_ps"], 2 * i + q - 1)
                v.tensor_tensor(hh[:, q, :], sg[:, q, :], GUP[q][1], ALU.mult).then_inc(s["hh_ok"], 1)

            def weights(t, b):
                dve.wait_ge(recd[b], 8 * (t + 2 - b))
                add_done(dve, t, b)
                v.tensor_tensor(wj[:], xr[:, b, CW:CW + NE], row(onehot, t, 128), ALU.mult).then_inc(s["wj_ok"], 1)
                dve.wait_ge(s["wj_ok"], t + 1)
                v.reduce_sum(ws[:, b:b + 1], wj[:], AX.X)
                v.tensor_copy(give[:, b:b + 1], slot_row[:, bass.ds(t, 1)]).then_inc(s["ws_ok"], 1)

            def result(t, b):
                dve.wait_ge(s["dn_ok"], 2 * t + 3)
                dve.wait_ge(s["ws_ok"], t + 1)
                v.tensor_scalar(ys[:, b, :], YP, ws[:, b:b + 1], None, ALU.mult).then_inc(s["ys_ok"], 1)

            def taking(t, b):
                if not isinstance(t, int) or t >= 2:
                    dve.wait_ge(recd[b], 8 * (t - b))
                v.tensor_copy(take[:, b:b + 1], slot_row[:, bass.ds(t, 1)]).then_inc(s["take_ok"], 1)

            def step(i, b, before, more):
                gated(i, 0)
                if before:
                    turned(i - 1, 1)
                weights(i, b)
                if not isinstance(i, int) or i < ST - 2:
                    taking(i + 2, b)
                gated(i, 1)
                if more:
                    features(i + 1, 1 - b)
                turned(i, 0)
                if before:
                    result(i - 1, 1 - b)

            taking(0, 0)
            taking(1, 1)
            features(0, 0)
            each_tile(dve, step)
            turned(ST - 1, 1)
            result(ST - 1, 0)


def kernel(x, cls_tok, L0_tok_W, L0_tok_b, L0_tok_cls_token, L0_tok_pos_embedding, L0_tok_gamma, L0_tok_beta,
           L0_attn_norm_scale, L0_attn_norm_bias, L0_attn_in_proj_w, L0_attn_A_log, L0_attn_dt_bias,
           L0_attn_bcB_scale, L0_attn_bcC_scale, L0_attn_B_bias, L0_attn_C_bias, L0_attn_theta_w, L0_attn_D,
           L0_attn_out_proj_w, L0_ffn_gate_w, L0_ffn_gate_up_proj, L0_ffn_down_proj):
    import concourse.bacc as bacc
    from concourse.bass_utils import run_bass_kernel_spmd

    def f(a):
        return np.asarray(a)

    p = f(x).reshape(BATCH, CH, HP, PATCH, HP, PATCH).transpose(1, 3, 5, 0, 2, 4).reshape(D, BATCH, NP)
    full = np.zeros((D, NT * G3, L), p.dtype)
    full[:, :BATCH, 2:] = p
    patches = full.reshape(DC, 128, NT, R).transpose(2, 1, 0, 3).reshape(NT, 128, DC * R)
    pos = f(L0_tok_pos_embedding)[0]
    base_a = np.tile(np.concatenate([np.zeros_like(pos[:1]), pos], 0), (G3, 1))
    base_b = np.tile(np.concatenate([f(cls_tok)[0], f(L0_tok_cls_token)[0], np.broadcast_to(f(L0_tok_b), (NP, E))], 0), (G3, 1))
    gam = np.tile(np.concatenate([np.ones_like(pos[:1]), np.broadcast_to(f(L0_tok_gamma), (L - 1, E))], 0), (G3, 1))
    bet = np.tile(np.concatenate([np.zeros_like(pos[:1]), np.broadcast_to(f(L0_tok_beta), (L - 1, E))], 0), (G3, 1))

    def chunks(w):
        return w.reshape(-1, 128, w.shape[-1]).transpose(1, 0, 2)

    def spread(rows_):
        return np.broadcast_to(np.stack(rows_)[None], (R, len(rows_), rows_[0].shape[-1]))

    gu = f(L0_ffn_gate_up_proj).transpose(0, 2, 1).reshape(NE, KC, 128, 2 * FF).transpose(0, 2, 1, 3).reshape(NE, 128, -1)
    dn = f(L0_ffn_down_proj).transpose(0, 2, 1).reshape(NE, FC, 128, E).transpose(0, 2, 1, 3).reshape(NE, 128, -1)
    w_experts = np.zeros((128, PIECES * PIECE), gu.dtype)
    w_experts[:, :NE * WEXP] = np.concatenate([gu, dn], 2).transpose(1, 0, 2).reshape(128, -1)
    arrays = dict(
        patches=patches, base_a=base_a, base_b=base_b, gammas=gam, betas=bet,
        w_tok=chunks(f(L0_tok_W)), w_in=chunks(f(L0_attn_in_proj_w)), w_theta=chunks(f(L0_attn_theta_w)),
        norm_cols=np.stack([f(L0_attn_norm_scale).reshape(KC, 128).T, f(L0_attn_norm_bias).reshape(KC, 128).T], 1),
        head_rows=spread([f(L0_attn_A_log), f(L0_attn_dt_bias), f(L0_attn_D)]),
        bc_rows=spread([f(L0_attn_bcB_scale), f(L0_attn_bcC_scale), f(L0_attn_B_bias), f(L0_attn_C_bias)]),
        w_out=chunks(f(L0_attn_out_proj_w)), w_gate=chunks(f(L0_ffn_gate_w).T),
        w_experts=w_experts, consts=CONSTS)
    nc = bacc.Bacc("TRN2", target_bir_lowering=False, num_devices=1)
    fed, args = {}, {}
    for name, a in arrays.items():
        fed["in_" + name] = np.ascontiguousarray(a)
        args[name] = nc.dram_tensor("in_" + name, a.shape, mybir.dt.from_np(a.dtype), kind="ExternalInput").ap()
    out = nc.dram_tensor("result", (BATCH, L, E), f32, kind="ExternalOutput").ap()
    program(nc, out=out, **args)
    return run_bass_kernel_spmd(nc, [fed], core_ids=[0]).results[0]["result"]
```
